# Optimizing a Trainium2 kernel written in Bass

```python
import numpy as np
import jax
import jax.numpy as jnp

def _softmax(x, axis=-1):
    return jax.nn.softmax(x, axis=axis)

def _gelu(x):
    return jax.nn.gelu(x, approximate=True)

def _silu(x):
    return jax.nn.silu(x)

def _sigmoid(x):
    return jax.nn.sigmoid(x)

def _layernorm(x, axis=-1, eps=1e-05):
    m = jnp.mean(x, axis=axis, keepdims=True)
    v = jnp.var(x, axis=axis, keepdims=True)
    return (x - m) / jnp.sqrt(v + eps)

def _scatter_add(tgt, idx, src, axis=0):
    return tgt.at[idx].add(src)

def _segment_sum(src, seg, n):
    return jax.ops.segment_sum(src, seg, n)
kernel_name = 'mk_gnn_resnorm_d2_gnn_r8_882415'

def setup_inputs(seed: int=0):
    np.random.seed(seed)
    _w = jnp.asarray

    def _rec_inputs():
        import jax
        import jax.numpy as jnp
        _gk = jax.random.key(seed)
        x = -0.0003713 + 1 * jax.random.normal(jax.random.fold_in(_gk, 1), (6250, 128), jnp.float32)
        src = jax.random.randint(jax.random.fold_in(_gk, 2), (100000,), 0, 6250, jnp.int32)
        dst = jax.random.randint(jax.random.fold_in(_gk, 3), (100000,), 0, 6250, jnp.int32)
        _o = jnp.argsort(dst, stable=True)
        src = src[_o]
        dst = dst[_o]
        edge_attr_128 = -2.25437e-05 + 0.999858 * jax.random.normal(jax.random.fold_in(_gk, 11), (100000, 128), jnp.float32)
        edge_attr_16 = 0.000196303 + 1.00016 * jax.random.normal(jax.random.fold_in(_gk, 12), (100000, 16), jnp.float32)
        return (x, src, dst, edge_attr_128, edge_attr_16)
    x, src, dst, edge_attr_128, edge_attr_16 = _rec_inputs()

    def _L0_gnn_setup():
        import jax, jax.numpy as jnp
        import numpy as np
        N, E = (12500, 200000)
        IN_DIM, EDGE_DIM, H, D = (128, 16, 8, 16)
        SLOPE = 0.2

        def _leaky_relu(x, slope=SLOPE):
            return jnp.where(x >= 0, x, slope * x)
        key = jax.random.key(seed)
        k1, k2, k3, k4, k5, k6, k7 = jax.random.split(key, 7)
        node_embeddings = jax.random.normal(k1, (N, IN_DIM), dtype=jnp.float32)
        edge_index = jax.random.randint(k2, (2, E), 0, N, dtype=jnp.int64)
        edge_features = jax.random.normal(k3, (E, EDGE_DIM), dtype=jnp.float32)
        g = 1.0 / np.sqrt(2.0)
        b_node = g * np.sqrt(6.0 / (IN_DIM + H * D))
        W_node = jax.random.uniform(k4, (H * D, IN_DIM), jnp.float32, -b_node, b_node)
        b_edge = g * np.sqrt(6.0 / (EDGE_DIM + H * D))
        W_edge = jax.random.uniform(k5, (H * D, EDGE_DIM), jnp.float32, -b_edge, b_edge)
        b_a = np.sqrt(6.0 / (H + 3 * D))
        attn_vec = jax.random.uniform(k6, (H, 3 * D), jnp.float32, -b_a, b_a)
        return {'node_embeddings': node_embeddings, 'edge_features': edge_features, 'W_node': W_node, 'W_edge': W_edge, 'attn_vec': attn_vec, 'edge_index': edge_index}
    _L0_gnn_all = _L0_gnn_setup()
    _L0_gnn_in = {k: v for k, v in _L0_gnn_all.items() if k in ('W_node', 'W_edge', 'attn_vec')}
    del _L0_gnn_all

    def _L1_gnn_setup():
        import jax, jax.numpy as jnp
        import numpy as np
        N_NODES = 6250
        N_EDGES = 62500
        D_FEAT = 128
        key = jax.random.key(seed)
        k1, k2, k3 = jax.random.split(key, 3)
        r = jax.random.normal(k1, (N_NODES, D_FEAT), dtype=jnp.float32)
        e = jax.random.normal(k2, (N_EDGES, D_FEAT), dtype=jnp.float32)
        a = jax.random.randint(k3, (N_EDGES, 2), 0, N_NODES, dtype=jnp.int64)
        return {'r': r, 'e': e, 'a': a}
    _L1_gnn_all = _L1_gnn_setup()
    _L1_gnn_in = {k: v for k, v in _L1_gnn_all.items() if k in ()}
    del _L1_gnn_all
    return {'x': x, 'src': src, 'dst': dst, 'edge_attr_128': edge_attr_128, 'edge_attr_16': edge_attr_16, 'L0_gnn_W_node': _L0_gnn_in['W_node'], 'L0_gnn_W_edge': _L0_gnn_in['W_edge'], 'L0_gnn_attn_vec': _L0_gnn_in['attn_vec']}

def reference(x, src, dst, edge_attr_128, edge_attr_16, L0_gnn_W_node, L0_gnn_W_edge, L0_gnn_attn_vec):
    import jax
    import jax.numpy as jnp

    def _L0_gnn_ref(node_embeddings, edge_features, W_node, W_edge, attn_vec, edge_index):
        import jax, jax.numpy as jnp
        import numpy as np
        N, E = (12500, 200000)
        IN_DIM, EDGE_DIM, H, D = (128, 16, 8, 16)
        SLOPE = 0.2

        def _leaky_relu(x, slope=SLOPE):
            return jnp.where(x >= 0, x, slope * x)
        n = node_embeddings.shape[0]
        src, dst = (edge_index[0], edge_index[1])
        h = (node_embeddings @ W_node.T).reshape(n, H, D)
        ef = (edge_features @ W_edge.T).reshape(-1, H, D)
        a_src, a_dst, a_edge = (attn_vec[:, :D], attn_vec[:, D:2 * D], attn_vec[:, 2 * D:])
        s_node_src = jnp.einsum('nhd,hd->nh', h, a_src)
        s_node_dst = jnp.einsum('nhd,hd->nh', h, a_dst)
        score = s_node_src[src] + s_node_dst[dst] + jnp.einsum('ehd,hd->eh', ef, a_edge)
        score = _leaky_relu(score)
        seg_max = jnp.maximum(jax.ops.segment_max(score, dst, num_segments=n), 0.0)
        exp_s = jnp.exp(score - seg_max[dst])
        denom = jax.ops.segment_sum(exp_s, dst, num_segments=n)
        w = exp_s / (denom[dst] + 1e-09)
        msg = h[src] * w[:, :, None]
        out = jax.ops.segment_sum(msg, dst, num_segments=n)
        return jax.nn.elu(out).reshape(n, H * D)

    def _L1_gnn_ref(r, e, a):
        import jax, jax.numpy as jnp
        import numpy as np
        N_NODES = 6250
        N_EDGES = 62500
        D_FEAT = 128
        rij = r[a[:, 0]] * e
        rji = r[a[:, 1]] * e
        out = jax.ops.segment_sum(rij, a[:, 1], num_segments=r.shape[0])
        out = out + jax.ops.segment_sum(rji, a[:, 0], num_segments=r.shape[0])
        return out
    edge_index = jnp.stack([src, dst])
    edge_index_t = jnp.stack([src, dst], axis=1)
    x = _layernorm(x + _L0_gnn_ref(x, edge_attr_16, L0_gnn_W_node, L0_gnn_W_edge, L0_gnn_attn_vec, edge_index), axis=-1)
    x = _layernorm(x + _L1_gnn_ref(x, edge_attr_128, edge_index_t), axis=-1)
    return x

_drawn_inputs = setup_inputs


def setup_inputs(seed=0):
    import zlib

    import numpy as np

    out = dict(_drawn_inputs(seed))
    spreads = {}
    factors = {}
    for name, (base, spread) in spreads.items():
        noise = np.random.default_rng([zlib.crc32(name.encode()), seed]).standard_normal(out[name].shape)
        drawn = base * np.exp(spread * noise) if base else spread * noise
        out[name] = jnp.asarray(drawn.astype(out[name].dtype))
    for name, factor in factors.items():
        out[name] = (out[name] * factor).astype(out[name].dtype)
    return out
```

```python
from contextlib import ExitStack

import numpy as np

import concourse.bass as bass
from concourse import mybir

F32 = mybir.dt.float32
I32 = mybir.dt.int32
U32 = mybir.dt.uint32
ALU = mybir.AluOpType
ACT = mybir.ActivationFunctionType
AX = mybir.AxisListType

P = 128
N_REAL, E_REAL = 6250, 100000
BLOCKS = -(-N_REAL // P)
NODES = BLOCKS * P
HEADS, HDIM, FEAT, EDIM = 8, 16, 128, 16
CHUNKS = P // HEADS
TILES_IN_CHUNK = -(-E_REAL // (CHUNKS * P))
GROUPS = TILES_IN_CHUNK
CHUNK = TILES_IN_CHUNK * P
EDGES = CHUNKS * CHUNK
TILES = EDGES // P
RES = BLOCKS - 1
RGROUPS = RES // CHUNKS
STEPS = TILES + RES
ALLG = GROUPS + RGROUPS
G = CHUNKS
SLOPE, EPS_DEN, EPS_LN = 0.2, 1e-9, 1e-5
NEG = -1.0e30
FAR = 1.0e5
HW = FEAT + HEADS
MW = 2 * HEADS + 2
NODE_STEP = 7
NODE_ITERS = BLOCKS // NODE_STEP
TABLES = 4
TROWS = NODES + P
QUADS, QUAD = 4, 4

C_ID, C_IOTA, C_HEAD, C_BD = 0, P, 2 * P, 2 * P + HEADS
C_W3, C_THR = C_BD + 2 * CHUNKS, C_BD + 2 * CHUNKS + 1
C_DUMMY, C_BLK, C_ONE = C_THR + 1, C_THR + 2, C_THR + 3
C_WIDTH = C_ONE + P


def shape_constants():
    p = np.arange(P, dtype=np.float32)
    c = np.zeros((P, C_WIDTH), np.float32)
    c[:, C_ID:C_ID + P] = np.eye(P, dtype=np.float32)
    c[:, C_IOTA:C_IOTA + P] = p
    for lane in range(P):
        c[lane, C_HEAD + lane // HDIM] = 1.0
        for half in range(2):
            c[lane, C_BD + half * CHUNKS + lane // EDIM + 8 * half] = 1.0
    c[:, C_W3] = np.float32(3.0) ** (64 - p)
    c[:, C_THR] = np.float32(1.75) * c[:, C_W3]
    c[:, C_DUMMY] = NODES + p
    c[:, C_BLK] = P * (p + 1)
    c[:, C_ONE:] = 1.0
    return c


class Chain:

    def __init__(self, engine, sem):
        self.engine, self.sem, self.n = engine, sem, 0

    def __call__(self, instruction):
        self.n += 1
        instruction.then_inc(self.sem, 1)
        self.engine.wait_ge(self.sem, self.n)


class Memory:
    pass


def late(g):
    return not (isinstance(g, int) and g < 2)


def beside(engine, m):
    engine.wait_ge(m.begun, 1)


def take_waits(nc, m, sem):
    nc.gpsimd.tensor_tensor(m.spare[:, 0:1], m.spare[:, 1:2], m.spare[:, 2:3], ALU.add).then_inc(sem, 1)


def pairs(engine, groups, emit, first=0):
    for k in range(2):
        emit(0, k)
    with engine.Fori(1, groups // 2) as i:
        for k in range(2):
            emit(i, k)
    for g in range(groups // 2 * 2, groups):
        emit(g // 2, g % 2)


def phase_nodes(nc, m):
    with ExitStack() as ctx:
        sb = lambda name, shape, dt=F32: ctx.enter_context(nc.sbuf_tensor(name, shape, dt))
        sem = lambda name: ctx.enter_context(nc.semaphore(name))
        wn, we, av = sb("wn", [P, P]), sb("we", [P, EDIM]), sb("av", [P, 3])
        amask = sb("amask", [P, 3, HEADS])
        waug = sb("waug", [P, FEAT + 2 * HEADS])
        wrep = sb("wrep", [P, HEADS, EDIM])
        wedge = sb("wedge", [P, HEADS])
        xs, xt = sb("xs", [P, NODE_STEP, P]), sb("xt", [P, NODE_STEP, P])
        hrow = sb("hrow", [P, NODE_STEP, HW])
        R = 2 * TILES_IN_CHUNK
        ii, ff = sb("ii", [R, 2, CHUNKS // 2, P], I32), sb("ff", [R, 2, CHUNKS // 2, P])
        first_i, first_f = sb("first_i", [1, TILES], I32), sb("first_f", [1, TILES])
        block_i = sb("block_i", [1, TILES], I32)
        base = sb("base", [1, STEPS])
        cnt, crow = sb("cnt", [RES, 3]), sb("crow", [1, 4, RES])
        c_in, w_in, i_in, f_in, x_in = (sem(n) for n in ("c_in", "w_in", "i_in", "f_in", "x_in"))
        chain, pe_w, pe_i, pe_f, pe_c, pe_b = (sem(n) for n in ("n_chain", "pe_w", "pe_i", "pe_f", "pe_c", "pe_b"))
        base_ready, waug_ready, xt_psum, xt_ready, h_psum, h_ready, h_out, z_out = (
            sem(n) for n in ("base_ready", "waug_ready", "xt_psum", "xt_ready", "h_psum", "h_ready", "h_out", "z_out"))
        amask_ready, ff_ready, first_ready, cnt_ready, zero_ready, idx_done = (
            sem(n) for n in ("amask_ready", "ff_ready", "first_ready", "cnt_ready", "zero_ready", "idx_done"))
        C = m.const
        bank = m.bank
        ident = C[:, C_ID:C_ID + P]

        with nc.Block() as block:
            @block.sync
            def _(sp):
                sp.dma_start(C[:, :], m.in_const).then_inc(c_in, 16)
                sp.dma_start(wn[:, :], m.W_node).then_inc(w_in, 16)
                sp.dma_start(we[:, :], m.W_edge).then_inc(w_in, 16)
                sp.dma_start(av[:, :], m.attn).then_inc(w_in, 16)
                sp.dma_start(ii[:, 0, :, :], m.dst.rearrange("(q r e) -> r q e", r=R, e=P)).then_inc(i_in, 16)
                sp.dma_start(ii[:, 1, :, :], m.src.rearrange("(q r e) -> r q e", r=R, e=P)).then_inc(i_in, 16)
                with nc.allow_non_contiguous_dma(reason="first edge of each tile"):
                    first = m.dst.rearrange("(c j e) -> e j c", c=CHUNKS, e=P)
                    for j in range(TILES_IN_CHUNK):
                        sp.dma_start(first_i[0:1, j * CHUNKS:(j + 1) * CHUNKS], first[0:1, j, :]).then_inc(f_in, 16)
                sp.wait_ge(zero_ready, 1)
                for t in range(TABLES):
                    sp.dma_start(m.table[t].rearrange("(p r) f -> p (r f)", p=P),
                                 m.acc_flat[:, 0:TROWS // P * FEAT]).then_inc(z_out, 16)
                xv = m.x.rearrange("(b p) f -> p b f", p=P)
                hv = m.H.rearrange("(b p) f -> p b f", p=P)
                sp.dma_start(xs[:, :, :], xv[:, 0:NODE_STEP, :]).then_inc(x_in, 16)
                with sp.Fori(0, NODE_ITERS - 1) as i:
                    sp.wait_ge(xt_psum, i + 1)
                    sp.dma_start(xs[:, :, :], xv[:, bass.ds(NODE_STEP * i + NODE_STEP, NODE_STEP), :]).then_inc(x_in, 16)
                    sp.wait_ge(h_ready, i + 1)
                    sp.dma_start(hv[:, bass.ds(NODE_STEP * i, NODE_STEP), :], hrow[:, :, :]).then_inc(h_out, 16)
                sp.wait_ge(h_ready, NODE_ITERS)
                sp.dma_start(hv[:, BLOCKS - NODE_STEP:BLOCKS, :], hrow[:, :, :]).then_inc(h_out, 16)
                sp.wait_ge(h_out, 16 * NODE_ITERS)
                sp.wait_ge(z_out, 16 * TABLES)

            @block.vector
            def _(dve):
                link = Chain(dve, chain)
                nc.vector.memset(m.acc_flat[:, :], 0.0).then_inc(zero_ready, 1)
                nc.vector.memset(m.spare[:, :], 0.0).then_inc(m.begun, 1)
                dve.wait_ge(c_in, 16)
                dve.wait_ge(w_in, 48)
                for w in range(3):
                    last = nc.vector.tensor_scalar(amask[:, w, :], C[:, C_HEAD:C_HEAD + HEADS], av[:, w:w + 1], None, ALU.mult)
                last.then_inc(amask_ready, 1)
                link(nc.vector.tensor_copy(wrep[:, :, :], we[:, :].unsqueeze(1).to_broadcast([P, HEADS, EDIM])))
                dve.wait_ge(f_in, 16 * TILES_IN_CHUNK)
                link(nc.vector.tensor_scalar(block_i[:, :], first_i[:, :], 7, None, ALU.arith_shift_right))
                nc.vector.tensor_copy(m.btab[0:1, 0:TILES], block_i[:, :])
                nc.vector.tensor_scalar(base[0:1, 0:TILES], block_i[:, :], float(P), None, ALU.mult)
                nc.vector.tensor_copy(first_f[:, :], first_i[:, :]).then_inc(first_ready, 1)
                dve.wait_ge(i_in, 32)
                nc.vector.tensor_copy(ff[:, :, :, :], ii[:, :, :, :]).then_inc(ff_ready, 1)
                dve.wait_ge(pe_w, 1)
                nc.vector.tensor_copy(waug[:, 0:FEAT], bank[6][:, 0:FEAT])
                nc.vector.tensor_copy(waug[:, FEAT:], bank[6][:, FEAT:FEAT + 2 * HEADS]).then_inc(waug_ready, 1)
                link(nc.vector.tensor_copy(wedge[:, :], bank[6][:, 256:256 + HEADS]))
                for half in range(2):
                    nc.vector.tensor_tensor(m.wblock[:, half, :, :], wedge[:, :].unsqueeze(1).to_broadcast([P, CHUNKS, HEADS]),
                                            C[:, C_BD + half * CHUNKS:C_BD + (half + 1) * CHUNKS].unsqueeze(2).to_broadcast([P, CHUNKS, HEADS]),
                                            ALU.mult)
                dve.wait_ge(pe_i, 1)
                for w, cols in enumerate((m.dstT, m.srcT)):
                    cv = cols[:, :].rearrange("p (j c) -> p c j", c=CHUNKS)
                    for q in range(CHUNKS // 2):
                        n = w * (CHUNKS // 2) + q
                        last = nc.vector.tensor_copy(cv[:, 2 * q:2 * q + 2, :], bank[n // 4][:, n % 4 * R:(n % 4 + 1) * R].rearrange("p (c j) -> p c j", c=2))
                last.then_inc(idx_done, 1)
                dve.wait_ge(pe_f, 1)
                half = TILES // 2
                for w in range(2):
                    last = nc.vector.tensor_scalar(m.scratch[0:RES, 0:half], bank[4 + w][0:RES, 0:half], C[0:RES, C_BLK:C_BLK + 1], 0.0,
                                                   ALU.is_lt, ALU.add, accum_out=cnt[:, w:w + 1])
                    link(last)
                nc.vector.tensor_tensor(cnt[:, 2:3], cnt[:, 0:1], cnt[:, 1:2], ALU.add).then_inc(cnt_ready, 1)
                dve.wait_ge(pe_c, 1)
                link(nc.vector.tensor_copy(crow[0:1, 0, :], bank[7][0:1, 0:RES]))
                link(nc.vector.tensor_scalar(crow[0:1, 1, :], crow[0:1, 0, :], -1.0, 0.0, ALU.add, ALU.max))
                nc.vector.tensor_copy(m.ttab[0:1, :], crow[0:1, 1, :])
                link(nc.vector.tensor_scalar(crow[0:1, 2, :], crow[0:1, 0, :], 0.5, FAR, ALU.is_lt, ALU.mult))
                link(nc.vector.tensor_scalar(crow[0:1, 3, :], C[0:1, C_IOTA:C_IOTA + RES], 1.0, None, ALU.add))
                nc.vector.tensor_copy(m.btab[0:1, TILES:STEPS], crow[0:1, 3, :])
                nc.vector.scalar_tensor_tensor(base[0:1, TILES:STEPS], crow[0:1, 3, :], float(P), crow[0:1, 2, :],
                                               ALU.mult, ALU.add).then_inc(base_ready, 1)
                dve.wait_ge(pe_b, 1)
                for w in range(2):
                    last = nc.vector.tensor_copy(m.baseB[:, w * STEPS // 2:(w + 1) * STEPS // 2], bank[6 + w][:, 0:STEPS // 2])
                link(last)
                with dve.Fori(0, NODE_ITERS) as i:
                    dve.wait_ge(h_psum, i + 1)
                    dve.wait_ge(h_out, 16 * i)
                    for n in range(4):
                        w = min(2, NODE_STEP - 2 * n)
                        hp = bank[2 + n][:, 0:512].rearrange("p (s f) -> p s f", s=2)
                        nc.vector.tensor_copy(hrow[:, 2 * n:2 * n + w, :], hp[:, 0:w, 0:HW])
                        last = nc.vector.tensor_copy(m.sdst[:, bass.ds(NODE_STEP * i + 2 * n, w), :], hp[:, 0:w, HW:HW + HEADS])
                    last.then_inc(h_ready, 1)

            @block.scalar
            def _(act):
                with act.Fori(0, NODE_ITERS) as i:
                    act.wait_ge(xt_psum, i + 1)
                    act.wait_ge(h_psum, i)
                    nc.scalar.copy(xt[:, 0:4, :], bank[0][:, :].rearrange("p (s f) -> p s f", s=4))
                    nc.scalar.copy(xt[:, 4:7, :], bank[1][:, 0:3 * P].rearrange("p (s f) -> p s f", s=3)).then_inc(xt_ready, 1)

            @block.tensor
            def _(pe):
                pe.wait_ge(amask_ready, 1)
                pe.wait_ge(chain, 1)
                nc.tensor.transpose(bank[6][:, 0:P], wn[:, :], ident)
                nc.tensor.matmul(bank[6][:, FEAT:FEAT + 2 * HEADS], wn[:, :], amask[:, 0:2, :].rearrange("p a h -> p (a h)"), start=True, stop=True)
                nc.tensor.matmul(bank[6][:, 256:256 + HEADS], wrep[:, :, :].rearrange("p a i -> p (a i)"), amask[:, 2, :], start=True, stop=True).then_inc(pe_w, 1)
                pe.wait_ge(ff_ready, 1)
                for w in range(2):
                    for q in range(CHUNKS // 2):
                        n = w * (CHUNKS // 2) + q
                        last = nc.tensor.transpose(bank[n // 4][:, n % 4 * R:(n % 4 + 1) * R], ff[:, w, q, :], C[0:R, C_ID:C_ID + R])
                last.then_inc(pe_i, 1)
                pe.wait_ge(first_ready, 1)
                for w in range(2):
                    last = nc.tensor.matmul(bank[4 + w][0:RES, 0:TILES // 2], C[0:1, C_ONE:C_ONE + RES],
                                            first_f[0:1, w * TILES // 2:(w + 1) * TILES // 2], start=True, stop=True)
                last.then_inc(pe_f, 1)
                pe.wait_ge(cnt_ready, 1)
                nc.tensor.matmul(bank[7][0:1, 0:RES], cnt[:, 2:3], C[0:RES, C_ID:C_ID + RES], start=True, stop=True).then_inc(pe_c, 1)
                pe.wait_ge(base_ready, 1)
                pe.wait_ge(waug_ready, 1)
                for w in range(2):
                    last = nc.tensor.matmul(bank[6 + w][:, 0:STEPS // 2], C[0:1, C_ONE:C_ONE + P],
                                            base[0:1, w * STEPS // 2:(w + 1) * STEPS // 2], start=True, stop=True)
                last.then_inc(pe_b, 1)
                pe.wait_ge(idx_done, 1)
                with pe.Fori(0, NODE_ITERS) as i:
                    pe.wait_ge(x_in, 16 * i + 16)
                    pe.wait_ge(xt_ready, i)
                    for u in range(NODE_STEP):
                        last = nc.tensor.transpose(bank[u // 4][:, u % 4 * P:(u % 4 + 1) * P], xs[:, u, :], ident)
                    last.then_inc(xt_psum, 1)
                    pe.wait_ge(xt_ready, i + 1)
                    pe.wait_ge(h_ready, i)
                    for u in range(NODE_STEP):
                        last = nc.tensor.matmul(bank[2 + u // 2][:, u % 2 * 256:u % 2 * 256 + HW + HEADS], xt[:, u, :], waug[:, :], start=True, stop=True)
                    last.then_inc(h_psum, 1)


def phase_scores(nc, m, aT):
    with ExitStack() as ctx:
        sb = lambda name, shape, dt=F32: ctx.enter_context(nc.sbuf_tensor(name, shape, dt))
        sem = lambda name: ctx.enter_context(nc.semaphore(name))
        rows = sb("rows", [P, 2, G, HW])
        ef, efT = sb("ef", [P, 2, G, EDIM]), sb("efT", [P, 2, 2, P])
        s_src = sb("s_src", [P, 2, G * HEADS])
        idx = [sb(f"idx{k}", [P, G], U32) for k in range(2)]
        ef_in = [sem(f"ef_in{k}") for k in range(2)]
        rows_out = [sem(f"rows_out{k}") for k in range(2)]
        got = [sem(f"got{s}") for s in range(G)]
        idx_ready, efT_psum, efT_ready, a_psum, a_ready, packed, taken = (
            sem(n) for n in ("idx_ready", "efT_psum", "efT_ready", "a_psum", "a_ready", "packed", "taken"))
        bank = m.bank
        ident = m.const[:, C_ID:C_ID + P]
        ev = m.ea16.rearrange("(c j p) f -> j p c f", c=CHUNKS, p=P)
        hv = m.Hs.rearrange("(c j p) f -> j p c f", c=CHUNKS, p=P)

        def gathered(engine, g):
            for s in range(G):
                engine.wait_ge(got[s], 16 * (g + 1))

        with nc.Block() as block:
            @block.sync
            def _(sp):
                def load(i, k):
                    g = 2 * i + k
                    if late(g):
                        sp.wait_ge(efT_psum, g - 1)
                    sp.dma_start(ef[:, k, :, :], ev[g] if isinstance(g, int) else ev[bass.ds(g, 1)].rearrange("a p c f -> (a p) c f")).then_inc(ef_in[k], 16)

                pairs(sp, GROUPS, load)

            @block.gpsimd
            def _(pool):
                def gather(i, k):
                    g = 2 * i + k
                    pool.wait_ge(idx_ready, g + 1)
                    if late(g):
                        pool.wait_ge(rows_out[k], 16 * i)
                        pool.wait_ge(packed, g - 1)
                    if late(g) or g:
                        pool.wait_ge(got[0], 16 * g)
                        pool.wait_ge(taken, g)
                    take_waits(nc, m, taken)
                    for s in range(G):
                        if late(g) or g:
                            beside(pool, m)
                            pool.wait_ge(got[s], 16 * g)
                        nc.gpsimd.indirect_dma_start(rows[:, k, s, :], None, m.H, bass.IndirectOffsetOnAxis(ap=idx[k][:, s:s + 1], axis=0)).then_inc(got[s], 16)

                pairs(pool, GROUPS, gather)

            @block.scalar
            def _(act):
                def work(i, k):
                    g = 2 * i + k
                    gathered(act, g)
                    nc.scalar.copy(s_src[:, k, :].rearrange("p (c h) -> p c h", h=HEADS), rows[:, k, :, FEAT:HW]).then_inc(packed, 1)
                    if late(g):
                        act.wait_ge(rows_out[k], 16 * i)
                    act.dma_start(hv[g] if isinstance(g, int) else hv[bass.ds(g, 1)].rearrange("a p c f -> (a p) c f"), rows[:, k, :, 0:FEAT]).then_inc(rows_out[k], 16)
                    act.wait_ge(a_psum, g + 1)
                    nc.scalar.copy(aT[:, bass.ds(P * g, P)], bank[2 + k][:, 0:P]).then_inc(a_ready, 1)

                pairs(act, GROUPS, work)
                act.wait_ge(rows_out[0], 16 * (GROUPS - GROUPS // 2))
                act.wait_ge(rows_out[1], 16 * (GROUPS // 2))

            @block.vector
            def _(dve):
                def work(i, k):
                    g = 2 * i + k
                    if late(g):
                        gathered(dve, g - 2)
                    nc.vector.tensor_copy(idx[k][:, :], m.srcT[:, bass.ds(G * g, G)]).then_inc(idx_ready, 1)
                    dve.wait_ge(efT_psum, g + 1)
                    if late(g):
                        dve.wait_ge(a_psum, g - 1)
                    nc.vector.tensor_copy(efT[:, k, :, :], bank[k][:, 0:2 * P].rearrange("p (a e) -> p a e", a=2)).then_inc(efT_ready, 1)

                pairs(dve, GROUPS, work)

            @block.tensor
            def _(pe):
                def work(i, k):
                    g = 2 * i + k
                    pe.wait_ge(ef_in[k], 16 * i + 16)
                    if late(g):
                        pe.wait_ge(efT_ready, g - 1)
                    e2 = ef[:, k, :, :].rearrange("p (a c) f -> p a (c f)", a=2)
                    for half in range(2):
                        last = nc.tensor.transpose(bank[k][:, half * P:(half + 1) * P], e2[:, half, :], ident)
                    last.then_inc(efT_psum, 1)
                    pe.wait_ge(efT_ready, g + 1)
                    if late(g):
                        pe.wait_ge(a_ready, g - 1)
                    for half in range(2):
                        nc.tensor.matmul(bank[2 + k][:, 0:P], m.wblock[:, half, :, :].rearrange("p c h -> p (c h)"), efT[:, k, half, :], start=(half == 0), stop=False)
                    pe.wait_ge(packed, g + 1)
                    nc.tensor.matmul(bank[2 + k][:, 0:P], s_src[:, k, :], ident, start=False, stop=True).then_inc(a_psum, 1)

                pairs(pe, GROUPS, work)


def phase_scan(nc, m, aT, amax):
    with ExitStack() as ctx:
        sb = lambda name, shape, dt=F32: ctx.enter_context(nc.sbuf_tensor(name, shape, dt))
        sem = lambda name: ctx.enter_context(nc.semaphore(name))
        di = sb("di", [P, CHUNK], I32)
        pen = sb("pen", [P, CHUNK + 1])
        fwd = sb("fwd", [P, CHUNK])
        ends_i = sb("ends_i", [HEADS, 2, CHUNKS], I32)
        ends = sb("ends", [HEADS, 2, CHUNKS])
        whole, joint, both = sb("whole", [HEADS, CHUNKS]), sb("joint", [HEADS, CHUNKS]), sb("both", [HEADS, 2, CHUNKS])
        tip, run = sb("tip", [HEADS, 2, CHUNKS]), sb("run", [HEADS, 2, CHUNKS])
        carry, carryT = sb("carry", [HEADS, 2, CHUNKS]), sb("carryT", [P, 2])
        tips = sb("tips", [P, 2])
        d_in, e_in, t_out, t_in, c_out, c_in2 = (sem(n) for n in ("d_in", "e_in", "t_out", "t_in", "c_out", "c_in2"))
        chain, tips_ready, carry_ready = sem("s_chain"), sem("tips_ready"), sem("carry_ready")
        dv = m.dst.rearrange("(c e) -> c e", c=CHUNKS)

        with nc.Block() as block:
            @block.sync
            def _(sp):
                for c in range(CHUNKS):
                    sp.dma_start(di[c * HEADS:(c + 1) * HEADS, :], dv[c:c + 1, :].to_broadcast([HEADS, CHUNK])).then_inc(d_in, 16)
                with nc.allow_non_contiguous_dma(reason="ends of the chunks"):
                    for w, e in enumerate((0, CHUNK - 1)):
                        sp.dma_start(ends_i[:, w, :], dv[:, e:e + 1].rearrange("c e -> e c").to_broadcast([HEADS, CHUNKS])).then_inc(e_in, 16)
                    sp.wait_ge(tips_ready, 1)
                    sp.dma_start(m.tips, tips[:, :]).then_inc(t_out, 16)
                    sp.wait_ge(t_out, 16)
                    for w in range(2):
                        sp.dma_start(tip[:, w, :], m.tips.rearrange("(c h) w -> h w c", h=HEADS)[:, w, :]).then_inc(t_in, 16)
                    sp.wait_ge(carry_ready, 1)
                    for w in range(2):
                        sp.dma_start(m.carries.rearrange("(c h) w -> h w c", h=HEADS)[:, w, :], carry[:, w, :]).then_inc(c_out, 16)
                    sp.wait_ge(c_out, 32)
                    sp.dma_start(carryT[:, :], m.carries).then_inc(c_in2, 16)

            @block.vector
            def _(dve):
                link = Chain(dve, chain)
                v = nc.vector
                v.memset(pen[:, 0:1], 0.0)
                link(v.memset(pen[:, CHUNK:CHUNK + 1], 0.0))
                dve.wait_ge(d_in, 16 * CHUNKS)
                link(v.tensor_tensor(pen[:, 1:CHUNK], di[:, 1:CHUNK], di[:, 0:CHUNK - 1], ALU.not_equal))
                link(v.tensor_scalar(pen[:, 1:CHUNK], pen[:, 1:CHUNK], NEG, None, ALU.mult))
                link(v.tensor_tensor_scan(fwd[:, :], pen[:, 0:CHUNK], aT[:, :], NEG, ALU.add, ALU.max))
                link(v.tensor_copy(tips[:, 0:1], fwd[:, CHUNK - 1:CHUNK]))
                link(v.tensor_tensor_scan(amax[:, ::-1], pen[:, CHUNK:0:-1], aT[:, ::-1], NEG, ALU.add, ALU.max))
                v.tensor_copy(tips[:, 1:2], amax[:, 0:1]).then_inc(tips_ready, 1)
                dve.wait_ge(e_in, 32)
                link(v.tensor_copy(ends[:, :, :], ends_i[:, :, :]))
                link(v.tensor_tensor(whole[:, :], ends[:, 0, :], ends[:, 1, :], ALU.not_equal))
                link(v.tensor_scalar(whole[:, :], whole[:, :], NEG, None, ALU.mult))
                link(v.memset(joint[:, :], NEG))
                L = CHUNKS - 1
                link(v.tensor_tensor(joint[:, 0:L], ends[:, 1, 0:L], ends[:, 0, 1:CHUNKS], ALU.not_equal))
                link(v.tensor_scalar(joint[:, 0:L], joint[:, 0:L], NEG, None, ALU.mult))
                link(v.memset(both[:, :, :], NEG))
                link(v.tensor_tensor(both[:, 0, 1:CHUNKS], whole[:, 1:CHUNKS], joint[:, 0:L], ALU.add))
                link(v.tensor_tensor(both[:, 1, 0:L], whole[:, 0:L], joint[:, 0:L], ALU.add))
                dve.wait_ge(t_in, 32)
                link(v.tensor_tensor_scan(run[:, 0, :], both[:, 0, :], tip[:, 0, :], NEG, ALU.add, ALU.max))
                link(v.tensor_tensor_scan(run[:, 1, ::-1], both[:, 1, ::-1], tip[:, 1, ::-1], NEG, ALU.add, ALU.max))
                link(v.memset(carry[:, :, :], NEG))
                link(v.tensor_tensor(carry[:, 0, 1:CHUNKS], run[:, 0, 0:L], joint[:, 0:L], ALU.add))
                v.tensor_tensor(carry[:, 1, 0:L], run[:, 1, 1:CHUNKS], joint[:, 0:L], ALU.add).then_inc(carry_ready, 1)
                dve.wait_ge(c_in2, 16)
                link(v.tensor_tensor_scan(fwd[:, :], pen[:, 0:CHUNK], aT[:, :], carryT[:, 0:1], ALU.add, ALU.max))
                link(v.tensor_tensor_scan(amax[:, ::-1], pen[:, CHUNK:0:-1], aT[:, ::-1], carryT[:, 1:2], ALU.add, ALU.max))
                link(v.tensor_tensor(amax[:, :], amax[:, :], fwd[:, :], ALU.max))


def phase_meta(nc, m, aT, amax):
    with ExitStack() as ctx:
        sb = lambda name, shape, dt=F32: ctx.enter_context(nc.sbuf_tensor(name, shape, dt))
        sem = lambda name: ctx.enter_context(nc.semaphore(name))
        stage, meta = sb("stage", [P, 2, 2, P]), sb("meta_s", [P, 2, G, MW])
        staged, turned, filled, cols = (sem(n) for n in ("staged", "turned", "filled", "cols"))
        out = [sem(f"meta_out{k}") for k in range(2)]
        bank = m.bank
        ident = m.const[:, C_ID:C_ID + P]
        mv = m.meta.rearrange("(c j p) f -> j p c f", c=CHUNKS, p=P)

        with nc.Block() as block:
            @block.sync
            def _(sp):
                def work(i, k):
                    g = 2 * i + k
                    sp.wait_ge(filled, g + 1)
                    sp.wait_ge(cols, g + 1)
                    sp.dma_start(mv[g] if isinstance(g, int) else mv[bass.ds(g, 1)].rearrange("a p c f -> (a p) c f"), meta[:, k, :, :]).then_inc(out[k], 16)

                pairs(sp, GROUPS, work)
                sp.wait_ge(out[0], 16 * (GROUPS - GROUPS // 2))
                sp.wait_ge(out[1], 16 * (GROUPS // 2))

            @block.scalar
            def _(act):
                def work(i, k):
                    g = 2 * i + k
                    if late(g):
                        act.wait_ge(turned, g - 1)
                    nc.scalar.copy(stage[:, k, 0, :], aT[:, bass.ds(P * g, P)])
                    nc.scalar.copy(stage[:, k, 1, :], amax[:, bass.ds(P * g, P)]).then_inc(staged, 1)

                pairs(act, GROUPS, work)

            @block.tensor
            def _(pe):
                def work(i, k):
                    g = 2 * i + k
                    pe.wait_ge(staged, g + 1)
                    if late(g):
                        pe.wait_ge(filled, g - 1)
                    for w in range(2):
                        last = nc.tensor.transpose(bank[k][:, w * P:(w + 1) * P], stage[:, k, w, :], ident)
                    last.then_inc(turned, 1)

                pairs(pe, GROUPS, work)

            @block.vector
            def _(dve):
                def work(i, k):
                    g = 2 * i + k
                    if late(g):
                        dve.wait_ge(out[k], 16 * i)
                    nc.vector.tensor_copy(meta[:, k, :, 2 * HEADS], m.dstT[:, bass.ds(G * g, G)])
                    nc.vector.tensor_copy(meta[:, k, :, 2 * HEADS + 1], m.srcT[:, bass.ds(G * g, G)]).then_inc(cols, 1)
                    dve.wait_ge(turned, g + 1)
                    nc.vector.tensor_copy(meta[:, k, :, 0:2 * HEADS].rearrange("p c (w h) -> p w c h", w=2),
                                          bank[k][:, 0:2 * P].rearrange("p (w c h) -> p w c h", w=2, c=CHUNKS)).then_inc(filled, 1)

                pairs(dve, GROUPS, work)


def load_steps(nc, sp, m, i, k, parts, sem, residual):
    g = 2 * i + k
    for rows, slot in parts:
        if not residual:
            v = rows.rearrange("(c j p) f -> j p c f", c=CHUNKS, p=P)
            v = v[g] if isinstance(g, int) else v[bass.ds(g, 1)].rearrange("a p c f -> (a p) c f")
            for half in range(2):
                cs = slice(half * G // 2, (half + 1) * G // 2)
                sp.dma_start(slot[:, cs, :], v[:, cs, :]).then_inc(sem, 16)
    if residual:
        for s in range(G):
            r = (g - GROUPS) * G + s
            tile = sp.value_load(m.ttab[0:1, r:r + 1], min_val=0, max_val=TILES - 1)
            for rows, slot in parts:
                v = rows.rearrange("(t p) f -> t p f", p=P)
                sp.dma_start(slot[:, s, :], v[bass.ds(tile, 1)].rearrange("a p f -> (a p) f")).then_inc(sem, 16)


def arrived(engine, main, rest, i, k, parts):
    g = 2 * i + k
    if isinstance(g, int) and g >= GROUPS:
        engine.wait_ge(rest[g - GROUPS], 16 * G * parts)
    else:
        engine.wait_ge(main[k], 2 * 16 * parts * (i + 1))




def phase_attend(nc, m):
    with ExitStack() as ctx:
        sb = lambda name, shape, dt=F32: ctx.enter_context(nc.sbuf_tensor(name, shape, dt))
        sem = lambda name: ctx.enter_context(nc.semaphore(name))
        h, meta = sb("h_b", [P, 2, G, FEAT]), sb("meta_b", [P, 2, G, MW])
        rel = sb("rel_b", [P, 2, G])
        O, OT = sb("O_b", [P, 2, G, P]), sb("OT_b", [P, 2, QUAD, P])
        msg = sb("msg_b", [P, 2, G, HW])
        z, zm, lz, gap = (sb(n, [P, G, HEADS]) for n in ("z_b", "zm_b", "lz_b", "gap_b"))
        main = [sem(f"b_in{k}") for k in range(2)]
        rest = [sem(f"b_rest{r}") for r in range(RGROUPS)]
        O_ready, OT_psum, OT_ready, spread_done, ex_ready, msg_ready, agg_psum, added, chain = (
            sem(n) for n in ("bO_ready", "bOT_psum", "bOT_ready", "spread_done", "ex_ready", "msg_ready", "bagg_psum", "badded", "b_chain"))
        bank = m.bank
        ident = m.const[:, C_ID:C_ID + P]
        iota = m.const[:, C_IOTA:C_IOTA + P]
        slot = lambda s: bank[4 + s % 4][:, 0:HW]

        def run(engine, emit, lead):
            emit(0, 0, 0)
            emit(0, 0, 1)
            emit(1, 0, 0)
            with engine.Fori(1, GROUPS // 2) as i:
                emit(0, i, 0)
                emit(1, i - 1, 1)
                emit(0, i, 1)
                emit(1, i, 0)
            for g in range(GROUPS // 2 * 2, ALLG):
                emit(0, g // 2, g % 2)
                emit(1, (g - 1) // 2, (g - 1) % 2)
            emit(1, (ALLG - 1) // 2, (ALLG - 1) % 2)

        with nc.Block() as block:
            @block.sync
            def _(sp):
                def load(i, k):
                    g = 2 * i + k
                    residual = isinstance(g, int) and g >= GROUPS
                    if late(g):
                        beside(sp, m)
                        sp.wait_ge(msg_ready, g - 1)
                    load_steps(nc, sp, m, i, k, [(m.Hs, h[:, k, :, :]), (m.meta, meta[:, k, :, :])],
                               rest[g - GROUPS] if residual else main[k], residual)

                pairs(sp, GROUPS, load)
                for g in range(GROUPS, ALLG):
                    load(g // 2, g % 2)

            @block.vector
            def _(dve):
                v = nc.vector

                def stage(part, i, k):
                    g = 2 * i + k
                    if part == 0:
                        arrived(dve, main, rest, i, k, 2)
                        if late(g):
                            dve.wait_ge(agg_psum, G * (g - 1))
                        v.tensor_tensor(rel[:, k, :], meta[:, k, :, 2 * HEADS], m.baseB[:, bass.ds(G * g, G)], ALU.subtract).then_inc(chain, 1)
                        dve.wait_ge(chain, 4 * g + 1)
                        v.tensor_tensor(O[:, k, :, :], iota.unsqueeze(1).to_broadcast([P, G, P]), rel[:, k, :].unsqueeze(2).to_broadcast([P, G, P]), ALU.is_equal).then_inc(O_ready, 1)
                        dve.wait_ge(spread_done, QUADS * g + QUADS)
                        if not (isinstance(g, int) and g < 1):
                            dve.wait_ge(ex_ready, g)
                        sd = bank[2 + k][:, 0:G * HEADS].rearrange("p (s h) -> p s h", s=G)
                        v.tensor_tensor(zm[:, :, :], meta[:, k, :, HEADS:2 * HEADS], sd, ALU.add)
                        v.tensor_tensor(z[:, :, :], meta[:, k, :, 0:HEADS], sd, ALU.add).then_inc(chain, 1)
                        dve.wait_ge(chain, 4 * g + 2)
                        v.scalar_tensor_tensor(lz[:, :, :], z[:, :, :], SLOPE, z[:, :, :], ALU.mult, ALU.max).then_inc(chain, 1)
                        dve.wait_ge(chain, 4 * g + 3)
                        v.scalar_tensor_tensor(gap[:, :, :], zm[:, :, :], 0.0, lz[:, :, :], ALU.max, ALU.subtract).then_inc(chain, 1)
                        dve.wait_ge(chain, 4 * g + 4)
                        return
                    dve.wait_ge(ex_ready, g + 1)
                    v.tensor_tensor(msg[:, k, :, 0:FEAT].rearrange("p s (h d) -> p s h d", h=HEADS),
                                    h[:, k, :, :].rearrange("p s (h d) -> p s h d", h=HEADS),
                                    msg[:, k, :, FEAT:HW].unsqueeze(3).to_broadcast([P, G, HEADS, HDIM]), ALU.mult).then_inc(msg_ready, 1)
                    for s in range(G):
                        b = dve.value_load(m.btab[0:1, bass.ds(G * g + s, 1)], min_val=0, max_val=BLOCKS - 1)
                        if s or not (isinstance(g, int) and g < 1):
                            dve.wait_ge(added, G * g + s)
                        dve.wait_ge(agg_psum, G * g + s + 1)
                        a = m.acc[:, bass.ds(b, 1), :].rearrange("p b f -> p (b f)")
                        v.tensor_tensor(a, a, slot(s), ALU.add).then_inc(added, 1)

                run(dve, stage, 1)

            @block.scalar
            def _(act):
                def stage(part, i, k):
                    g = 2 * i + k
                    if part == 0:
                        for q in range(QUADS):
                            act.wait_ge(OT_psum, QUADS * g + q + 1)
                            if late(g) or g or q > 1:
                                act.wait_ge(spread_done, QUADS * g + q - 1)
                            nc.scalar.copy(OT[:, q % 2, :, :], bank[q % 2][:, :].rearrange("p (s e) -> p s e", s=QUAD)).then_inc(OT_ready, 1)
                        act.wait_ge(chain, 4 * g + 4)
                        if late(g):
                            act.wait_ge(agg_psum, G * (g - 1))
                        nc.scalar.activation(msg[:, k, :, FEAT:HW], gap[:, :, :], ACT.Exp, scale=-1.0).then_inc(ex_ready, 1)

                for k in range(2):
                    stage(0, 0, k)
                with act.Fori(1, GROUPS // 2) as i:
                    for k in range(2):
                        stage(0, i, k)
                for g in range(GROUPS // 2 * 2, ALLG):
                    stage(0, g // 2, g % 2)

            @block.tensor
            def _(pe):
                def stage(part, i, k):
                    g = 2 * i + k
                    if part == 0:
                        pe.wait_ge(O_ready, g + 1)

                        def turn(q):
                            if late(g) or g or q > 1:
                                pe.wait_ge(OT_ready, QUADS * g + q - 1)
                            for u in range(QUAD):
                                last = nc.tensor.transpose(bank[q % 2][:, u * P:(u + 1) * P], O[:, k, QUAD * q + u, :], ident)
                            last.then_inc(OT_psum, 1)

                        def spread(q):
                            pe.wait_ge(OT_ready, QUADS * g + q + 1)
                            for u in range(QUAD):
                                s = QUAD * q + u
                                b = pe.value_load(m.btab[0:1, bass.ds(G * g + s, 1)], min_val=0, max_val=BLOCKS - 1)
                                last = nc.tensor.matmul(bank[2 + k][:, s * HEADS:(s + 1) * HEADS], OT[:, q % 2, u, :],
                                                        m.sdst[:, bass.ds(b, 1), :].rearrange("p b h -> p (b h)"), start=True, stop=True)
                            last.then_inc(spread_done, 1)

                        turn(0)
                        turn(1)
                        for q in range(QUADS):
                            spread(q)
                            if q + 2 < QUADS:
                                turn(q + 2)
                        return
                    pe.wait_ge(msg_ready, g + 1)
                    for s in range(G):
                        if late(g) or g or s >= 4:
                            pe.wait_ge(added, G * g + s - 3)
                        nc.tensor.matmul(slot(s), O[:, k, s, :], msg[:, k, s, :], start=True, stop=True).then_inc(agg_psum, 1)

                run(pe, stage, 1)


def phase_norm(nc, m, last_layer):
    L = "2" if last_layer else "1"
    with ExitStack() as ctx:
        sb = lambda name, shape, dt=F32: ctx.enter_context(nc.sbuf_tensor(name + L, shape, dt))
        sem = lambda name: ctx.enter_context(nc.semaphore(name + L))
        S = NODE_STEP
        y, e, sq = sb("y", [P, S, FEAT]), sb("e", [P, S, FEAT]), sb("sq", [P, S, FEAT])
        rec = sb("rec", [P, S, HEADS])
        add = sb("add", [P, TABLES, S, FEAT])
        mean, var, dev = sb("mean", [P, S]), sb("var", [P, S]), sb("dev", [P, S])
        eps = sb("eps", [P, 1])
        chain, x_in, exp_ready, exp_less, summed, dev_ready, normed, out, ready = (
            sem(n) for n in ("f_chain", "f_in", "exp_ready", "exp_less", "summed", "dev_ready", "normed", "f_out", "f_ready"))
        PER = 5 + 6
        xv = m.x.rearrange("(b p) f -> p b f", p=P)
        REST = N_REAL - (BLOCKS - 1) * P

        with nc.Block() as block:
            @block.sync
            def _(sp):
                with sp.Fori(0, NODE_ITERS) as i:
                    sp.wait_ge(normed, i)
                    if last_layer:
                        for t in range(TABLES):
                            tv = m.table[t][0:NODES, :].rearrange("(b p) f -> p b f", p=P)
                            sp.dma_start(add[:, t, :, :], tv[:, bass.ds(S * i, S), :]).then_inc(x_in, 16)
                    else:
                        sp.dma_start(add[:, 0, :, :], xv[:, bass.ds(S * i, S), :]).then_inc(x_in, 16)
                        sp.wait_ge(normed, i + 1)
                        sp.dma_start(m.X1.rearrange("(b p) f -> p b f", p=P)[:, bass.ds(S * i, S), :], m.x1[:, bass.ds(S * i, S), :]).then_inc(out, 16)
                if last_layer:
                    sp.wait_ge(normed, NODE_ITERS)
                    sp.dma_start(m.out[0:(BLOCKS - 1) * P, :].rearrange("(b p) f -> p b f", p=P), m.x1[:, 0:BLOCKS - 1, :]).then_inc(out, 16)
                    sp.dma_start(m.out[(BLOCKS - 1) * P:N_REAL, :], m.x1[0:REST, BLOCKS - 1, :]).then_inc(out, 16)
                    sp.wait_ge(out, 32)
                else:
                    sp.wait_ge(out, 16 * NODE_ITERS)

            @block.scalar
            def _(act):
                act.wait_ge(ready, 1)
                with act.Fori(0, NODE_ITERS) as i:
                    if not last_layer:
                        act.wait_ge(chain, PER * i + 4)
                        nc.scalar.activation(e[:, :, :], e[:, :, :], ACT.Exp).then_inc(exp_ready, 1)
                    act.wait_ge(chain, PER * i + 10)
                    nc.scalar.activation(dev[:, :], var[:, :], ACT.Sqrt, bias=eps[:, 0:1], scale=1.0 / FEAT).then_inc(dev_ready, 1)

            @block.vector
            def _(dve):
                v = nc.vector
                v.memset(eps[:, :], EPS_LN).then_inc(ready, 1)
                with dve.Fori(0, NODE_ITERS) as i:
                    here = bass.ds(S * i, S)
                    done = [0]

                    def link(instruction):
                        done[0] += 1
                        instruction.then_inc(chain, 1)
                        dve.wait_ge(chain, PER * i + done[0])

                    if last_layer:
                        dve.wait_ge(x_in, 16 * TABLES * (i + 1))
                        link(v.tensor_tensor(y[:, :, :], m.x1[:, here, :], m.acc1[:, here, :], ALU.add))
                        for t in range(TABLES):
                            link(v.tensor_tensor(y[:, :, :], y[:, :, :], add[:, t, :, :], ALU.add))
                    else:
                        link(v.tensor_scalar(rec[:, :, :], m.acc[:, here, FEAT:HW], EPS_DEN, None, ALU.add))
                        link(v.reciprocal(rec[:, :, :], rec[:, :, :]))
                        y4 = y[:, :, :].rearrange("p s (h d) -> p s h d", h=HEADS)
                        for s in range(S):
                            a = m.acc[:, bass.ds(S * i + s, 1), 0:FEAT].rearrange("p b (h d) -> p (b h) d", h=HEADS)
                            last = v.tensor_tensor(y4[:, s, :, :], a, rec[:, s, :].unsqueeze(2).to_broadcast([P, HEADS, HDIM]), ALU.mult)
                        link(last)
                        link(v.tensor_scalar(e[:, :, :], y[:, :, :], 0.0, None, ALU.min))
                        dve.wait_ge(exp_ready, i + 1)
                        v.tensor_scalar(e[:, :, :], e[:, :, :], -1.0, None, ALU.add).then_inc(exp_less, 1)
                        dve.wait_ge(exp_less, i + 1)
                        link(v.scalar_tensor_tensor(y[:, :, :], y[:, :, :], 0.0, e[:, :, :], ALU.max, ALU.add))
                        dve.wait_ge(x_in, 16 * (i + 1))
                        v.tensor_tensor(y[:, :, :], y[:, :, :], add[:, 0, :, :], ALU.add).then_inc(summed, 1)
                        dve.wait_ge(summed, i + 1)
                    link(v.tensor_reduce(mean[:, :], y[:, :, :], AX.X, ALU.add))
                    link(v.tensor_scalar(mean[:, :], mean[:, :], 1.0 / FEAT, None, ALU.mult))
                    link(v.tensor_tensor(y[:, :, :], y[:, :, :], mean[:, :].unsqueeze(2).to_broadcast([P, S, FEAT]), ALU.subtract))
                    link(v.tensor_tensor(sq[:, :, :], y[:, :, :], y[:, :, :], ALU.mult))
                    link(v.tensor_reduce(var[:, :], sq[:, :, :], AX.X, ALU.add))
                    dve.wait_ge(dev_ready, i + 1)
                    link(v.reciprocal(dev[:, :], dev[:, :]))
                    assert done[0] == PER
                    v.tensor_tensor(m.x1[:, here, :], y[:, :, :], dev[:, :].unsqueeze(2).to_broadcast([P, S, FEAT]), ALU.mult).then_inc(normed, 1)


def phase_messages(nc, m):
    with ExitStack() as ctx:
        sb = lambda name, shape, dt=F32: ctx.enter_context(nc.sbuf_tensor(name, shape, dt))
        sem = lambda name: ctx.enter_context(nc.semaphore(name))
        ea, got_rows = sb("ea", [P, 2, G, FEAT]), sb("got_rows", [P, 2, G, FEAT])
        ends = sb("ends_l", [P, 2, G, 2])
        rel = sb("rel_l", [P, 2, G])
        O, OT = sb("O_l", [P, 2, G, P]), sb("OT_l", [P, 2, QUAD, P])
        same = sb("same", [P, G, P])
        back = sb("back", [P, G, FEAT])
        merged = sb("merged", [P, 2, G, FEAT])
        dup, far = sb("dup", [P, G]), sb("far", [P, G])
        idx = [sb(f"gidx{k}", [P, G], U32) for k in range(2)]
        sidx = [sb(f"sidx{k}", [P, G], U32) for k in range(2)]
        main = [sem(f"l_in{k}") for k in range(2)]
        rest = [sem(f"l_rest{r}") for r in range(RGROUPS)]
        got = [sem(f"lgot{s}") for s in range(G)]
        put = [sem(f"put{s}") for s in range(G)]
        merged_ready = [sem(f"l_merged{q}") for q in range(QUADS)]
        (idx_ready, O_ready, OT_psum, OT_ready, srcT_psum, same_ready, rank_psum, sidx_ready, spread_done, back_ready,
         merged_psum, fwd_ready, agg_psum, added, chain, taken) = (
            sem(n) for n in ("l_idx", "l_O", "l_OTp", "l_OT", "l_srcT", "l_same", "l_rank", "l_sidx", "l_spread", "l_back",
                             "l_mergedp", "l_fwd", "l_agg", "l_added", "l_chain", "l_taken"))
        bank = m.bank
        C = m.const
        ident = C[:, C_ID:C_ID + P]
        iota = C[:, C_IOTA:C_IOTA + P]
        quad_of = lambda t, q: t[:, QUAD * q:QUAD * (q + 1), :]
        as_quad = lambda b: b[:, :].rearrange("p (s e) -> p s e", s=QUAD)

        def gathered(engine, g):
            for s in range(G):
                engine.wait_ge(got[s], 16 * (g + 1))

        def scattered(engine, g):
            for s in range(G):
                engine.wait_ge(put[s], 16 * (g + 1))

        def all_groups(engine, emit):
            pairs(engine, GROUPS, emit)
            for g in range(GROUPS, ALLG):
                emit(g // 2, g % 2)

        with nc.Block() as block:
            @block.sync
            def _(sp):
                def load(i, k):
                    g = 2 * i + k
                    residual = isinstance(g, int) and g >= GROUPS
                    if late(g):
                        beside(sp, m)
                        sp.wait_ge(fwd_ready, g - 1)
                    load_steps(nc, sp, m, i, k, [(m.ea, ea[:, k, :, :]), (m.meta[:, 2 * HEADS:MW], ends[:, k, :, :])],
                               rest[g - GROUPS] if residual else main[k], residual)

                all_groups(sp, load)

            @block.gpsimd
            def _(pool):
                def gather(g, k, s):
                    if late(g) or g:
                        beside(pool, m)
                        pool.wait_ge(got[s], 16 * g)
                    nc.gpsimd.indirect_dma_start(got_rows[:, k, s, :], None, m.X1, bass.IndirectOffsetOnAxis(ap=idx[k][:, s:s + 1], axis=0)).then_inc(got[s], 16)

                def scatter(after, k, s):
                    if s % QUAD == 0:
                        beside(pool, m)
                        pool.wait_ge(merged_ready[s // QUAD], after)
                    if s >= TABLES:
                        beside(pool, m)
                        pool.wait_ge(put[s - TABLES], 16 * after)
                    elif late(after):
                        beside(pool, m)
                        pool.wait_ge(put[s - TABLES + G], 16 * after - 16)
                    nc.gpsimd.indirect_dma_start(m.table[s % TABLES], bass.IndirectOffsetOnAxis(ap=sidx[k][:, s:s + 1], axis=0), merged[:, k, s, :], None,
                                                 compute_op=ALU.add).then_inc(put[s], 16)

                def work(i, k):
                    g = 2 * i + k
                    pool.wait_ge(idx_ready, g + 1)
                    pool.wait_ge(sidx_ready, g)
                    pool.wait_ge(got[0], 16 * g)
                    if late(g):
                        pool.wait_ge(agg_psum, QUADS * (g - 1))
                        pool.wait_ge(put[G - TABLES], 16 * g - 16)
                        pool.wait_ge(taken, g - 1)
                    take_waits(nc, m, taken)
                    for s in range(G):
                        gather(g, k, s)
                        scatter(g, 1 - k, s)

                pool.wait_ge(idx_ready, 1)
                for s in range(G):
                    gather(0, 0, s)
                work(0, 1)
                with pool.Fori(1, GROUPS // 2) as i:
                    for k in range(2):
                        work(i, k)
                for g in range(GROUPS // 2 * 2, ALLG):
                    work(g // 2, g % 2)
                pool.wait_ge(sidx_ready, ALLG)
                for s in range(G):
                    scatter(ALLG, (ALLG - 1) % 2, s)
                scattered(pool, ALLG - 1)

            @block.scalar
            def _(act):
                def index(i, k):
                    g = 2 * i + k
                    arrived(act, main, rest, i, k, 2)
                    if late(g):
                        gathered(act, g - 2)
                    nc.scalar.copy(idx[k][:, :], ends[:, k, :, 1]).then_inc(idx_ready, 1)

                def work(i, k):
                    g = 2 * i + k
                    for q in range(QUADS):
                        act.wait_ge(OT_psum, QUADS * g + q + 1)
                        if late(g) or g or q > 1:
                            act.wait_ge(spread_done, QUADS * g + q - 1)
                        nc.scalar.copy(OT[:, q % 2, :, :], as_quad(bank[q % 2])).then_inc(OT_ready, 1)
                    for q in range(QUADS):
                        if q == 0 and late(g):
                            scattered(act, g - 2)
                        act.wait_ge(merged_psum, QUADS * g + q + 1)
                        nc.scalar.copy(merged[:, k, QUAD * q:QUAD * (q + 1), :], as_quad(bank[7])).then_inc(merged_ready[q], 1)

                index(0, 0)
                index(0, 1)
                work(0, 0)
                with act.Fori(1, GROUPS // 2) as i:
                    index(i, 0)
                    work(i - 1, 1)
                    index(i, 1)
                    work(i, 0)
                for g in range(GROUPS // 2 * 2, ALLG):
                    index(g // 2, g % 2)
                    work((g - 1) // 2, (g - 1) % 2)
                work((ALLG - 1) // 2, (ALLG - 1) % 2)

            @block.vector
            def _(dve):
                v = nc.vector
                v.memset(m.acc1[:, :, :], 0.0).then_inc(chain, 1)
                LINKS = 3

                def work(i, k):
                    g = 2 * i + k
                    arrived(dve, main, rest, i, k, 2)
                    if late(g):
                        dve.wait_ge(agg_psum, QUADS * (g - 1))
                    v.tensor_tensor(rel[:, k, :], ends[:, k, :, 0], m.baseB[:, bass.ds(G * g, G)], ALU.subtract).then_inc(chain, 1)
                    dve.wait_ge(chain, LINKS * g + 2)
                    v.tensor_tensor(O[:, k, :, :], iota.unsqueeze(1).to_broadcast([P, G, P]), rel[:, k, :].unsqueeze(2).to_broadcast([P, G, P]), ALU.is_equal).then_inc(O_ready, 1)
                    for q in range(QUADS):
                        dve.wait_ge(srcT_psum, QUADS * g + q + 1)
                        if late(g) or g:
                            dve.wait_ge(merged_psum, QUADS * (g - 1) + q + 1)
                        v.tensor_tensor(quad_of(same, q), as_quad(bank[2]), ends[:, k, QUAD * q:QUAD * (q + 1), 1:2].to_broadcast([P, QUAD, P]), ALU.is_equal).then_inc(same_ready, 1)
                    dve.wait_ge(rank_psum, g + 1)
                    v.tensor_scalar(far[:, :], ends[:, k, :, 1], -1.0, C[:, C_DUMMY:C_DUMMY + 1], ALU.mult, ALU.add)
                    v.tensor_scalar(dup[:, :], bank[6][:, 0:G], C[:, C_THR:C_THR + 1], None, ALU.is_gt).then_inc(chain, 1)
                    dve.wait_ge(chain, LINKS * g + 3)
                    v.tensor_tensor(far[:, :], far[:, :], dup[:, :], ALU.mult).then_inc(chain, 1)
                    dve.wait_ge(chain, LINKS * g + 4)
                    if late(g):
                        scattered(dve, g - 2)
                    v.tensor_tensor(sidx[k][:, :], far[:, :], ends[:, k, :, 1], ALU.add).then_inc(sidx_ready, 1)
                    dve.wait_ge(sidx_ready, g + 1)
                    for q in range(QUADS):
                        dve.wait_ge(spread_done, QUADS * g + q + 1)
                        v.tensor_tensor(quad_of(back, q), ea[:, k, QUAD * q:QUAD * (q + 1), :], as_quad(bank[3 + q % 2]), ALU.mult).then_inc(back_ready, 1)
                    gathered(dve, g)
                    v.tensor_tensor(got_rows[:, k, :, :], got_rows[:, k, :, :], ea[:, k, :, :], ALU.mult).then_inc(fwd_ready, 1)
                    for s in range(G):
                        b = dve.value_load(m.btab[0:1, bass.ds(G * g + s, 1)], min_val=0, max_val=BLOCKS - 1)
                        if s or late(g) or g:
                            dve.wait_ge(added, G * g + s)
                        if s % QUAD == 0:
                            dve.wait_ge(agg_psum, QUADS * g + s // QUAD + 1)
                        a = m.acc1[:, bass.ds(b, 1), :].rearrange("p b f -> p (b f)")
                        v.tensor_tensor(a, a, bank[5][:, s % QUAD * P:(s % QUAD + 1) * P], ALU.add).then_inc(added, 1)

                all_groups(dve, work)

            @block.tensor
            def _(pe):
                def work(i, k):
                    g = 2 * i + k
                    arrived(pe, main, rest, i, k, 2)
                    for q in range(QUADS):
                        if late(g) or g or q:
                            pe.wait_ge(same_ready, QUADS * g + q)
                        for u in range(QUAD):
                            s = QUAD * q + u
                            last = nc.tensor.transpose(bank[2][:, u * P:(u + 1) * P], ends[:, k, s, 1:2].to_broadcast([P, P]), ident)
                        last.then_inc(srcT_psum, 1)
                    pe.wait_ge(same_ready, QUADS * (g + 1))
                    if late(g) or g:
                        pe.wait_ge(sidx_ready, g)
                    for s in range(G):
                        last = nc.tensor.matmul(bank[6][:, s:s + 1], same[:, s, :], C[:, C_W3:C_W3 + 1], start=True, stop=True)
                    last.then_inc(rank_psum, 1)

                    def turn(q):
                        if late(g) or g or q > 1:
                            pe.wait_ge(OT_ready, QUADS * g + q - 1)
                        for u in range(QUAD):
                            last = nc.tensor.transpose(bank[q % 2][:, u * P:(u + 1) * P], O[:, k, QUAD * q + u, :], ident)
                        last.then_inc(OT_psum, 1)

                    def spread(q):
                        pe.wait_ge(OT_ready, QUADS * g + q + 1)
                        if late(g) or g or q > 1:
                            pe.wait_ge(back_ready, QUADS * g + q - 1)
                        for u in range(QUAD):
                            s = QUAD * q + u
                            b = pe.value_load(m.btab[0:1, bass.ds(G * g + s, 1)], min_val=0, max_val=BLOCKS - 1)
                            last = nc.tensor.matmul(bank[3 + q % 2][:, u * P:(u + 1) * P], OT[:, q % 2, u, :],
                                                    m.x1[:, bass.ds(b, 1), :].rearrange("p b f -> p (b f)"), start=True, stop=True)
                        last.then_inc(spread_done, 1)

                    pe.wait_ge(O_ready, g + 1)
                    turn(0)
                    turn(1)
                    for q in range(QUADS):
                        spread(q)
                        if q + 2 < QUADS:
                            turn(q + 2)
                    for q in range(QUADS):
                        pe.wait_ge(back_ready, QUADS * g + q + 1)
                        if q:
                            pe.wait_ge(merged_ready[q - 1], g + 1)
                        elif late(g) or g:
                            pe.wait_ge(merged_ready[QUADS - 1], g)
                        for u in range(QUAD):
                            s = QUAD * q + u
                            last = nc.tensor.matmul(bank[7][:, u * P:(u + 1) * P], same[:, s, :], back[:, s, :], start=True, stop=True)
                        last.then_inc(merged_psum, 1)
                    pe.wait_ge(fwd_ready, g + 1)
                    for q in range(QUADS):
                        if late(g) or g or q:
                            pe.wait_ge(added, G * g + QUAD * q)
                        for u in range(QUAD):
                            s = QUAD * q + u
                            last = nc.tensor.matmul(bank[5][:, u * P:(u + 1) * P], O[:, k, s, :], got_rows[:, k, s, :], start=True, stop=True)
                        last.then_inc(agg_psum, 1)

                all_groups(pe, work)


def gnn(nc, x, src, dst, ea, ea16, W_node, W_edge, attn, const, out, upto=99):
    m = Memory()
    m.x, m.src, m.dst, m.ea, m.ea16 = x, src, dst, ea, ea16
    m.W_node, m.W_edge, m.attn, m.in_const, m.out = W_node, W_edge, attn, const, out
    dram = lambda name, shape: nc.dram_tensor(name, shape, F32, kind="Internal").ap()
    m.H, m.X1 = dram("h_rows", (NODES, HW)), dram("x1_rows", (NODES, FEAT))
    m.Hs, m.meta = dram("h_of_src", (EDGES, FEAT)), dram("edge_rows", (EDGES, MW))
    m.table = [dram(f"table{t}", (TROWS, FEAT)) for t in range(TABLES)]
    m.tips, m.carries = dram("tips_d", (P, 2)), dram("carries_d", (P, 2))
    with ExitStack() as ctx:
        sb = lambda name, shape, dt=F32: ctx.enter_context(nc.sbuf_tensor(name, shape, dt))
        m.bank = [ctx.enter_context(nc.psum_tensor(f"bank{n}", [P, 512], F32)) for n in range(8)]
        m.begun = ctx.enter_context(nc.semaphore("begun"))
        m.const = sb("const", [P, C_WIDTH])
        m.spare = sb("spare", [P, 4])
        m.btab, m.ttab = sb("btab", [1, STEPS], I32), sb("ttab", [1, RES], I32)
        m.baseB = sb("baseB", [P, STEPS])
        m.wblock = sb("wblock", [P, 2, CHUNKS, HEADS])
        m.dstT, m.srcT = sb("dstT", [P, TILES]), sb("srcT", [P, TILES])
        m.sdst = sb("sdst", [P, BLOCKS, HEADS])
        m.acc = sb("acc", [P, BLOCKS, HW])
        m.acc_flat = m.acc[:, :, :].rearrange("p b f -> p (b f)")
        with ExitStack() as early:
            m.scratch = early.enter_context(nc.sbuf_tensor("scratch", [P, TILES // 2], F32))
            phase_nodes(nc, m)
        with ExitStack() as early:
            aT = early.enter_context(nc.sbuf_tensor("aT", [P, CHUNK], F32))
            phase_scores(nc, m, aT)
            amax = early.enter_context(nc.sbuf_tensor("amax", [P, CHUNK], F32))
            phase_scan(nc, m, aT, amax)
            phase_meta(nc, m, aT, amax)
        phase_attend(nc, m)
        m.x1 = sb("x1", [P, BLOCKS, FEAT])
        phase_norm(nc, m, last_layer=False)
        m.acc1 = m.acc_flat[:, 0:BLOCKS * FEAT].rearrange("p (b f) -> p b f", b=BLOCKS)
        phase_messages(nc, m)
        phase_norm(nc, m, last_layer=True)


def kernel(x, src, dst, edge_attr_128, edge_attr_16, L0_gnn_W_node, L0_gnn_W_edge, L0_gnn_attn_vec):
    import concourse.bacc as bacc
    from concourse.bass_utils import run_bass_kernel_spmd

    def rows(a, n):
        a = np.asarray(a)
        return np.concatenate([a, np.zeros((n - a.shape[0],) + a.shape[1:], a.dtype)])

    def indices(a):
        a = np.asarray(a)
        return np.concatenate([a, np.full(EDGES - E_REAL, NODES - 1, a.dtype)])

    attn = np.asarray(L0_gnn_attn_vec).reshape(HEADS, 3, HDIM).transpose(0, 2, 1).reshape(P, 3)
    arrays = {
        "x": rows(x, NODES), "src": indices(src), "dst": indices(dst),
        "ea": rows(edge_attr_128, EDGES), "ea16": rows(edge_attr_16, EDGES),
        "W_node": np.ascontiguousarray(L0_gnn_W_node), "W_edge": np.ascontiguousarray(L0_gnn_W_edge),
        "attn": np.ascontiguousarray(attn), "const": shape_constants(),
    }
    nc = bacc.Bacc("TRN2", target_bir_lowering=False, num_devices=1)
    args = {n: nc.dram_tensor("in_" + n, a.shape, mybir.dt.from_np(a.dtype), kind="ExternalInput").ap() for n, a in arrays.items()}
    out = nc.dram_tensor("out_rows", (N_REAL, FEAT), F32, kind="ExternalOutput").ap()
    gnn(nc, out=out, **args)
    r = run_bass_kernel_spmd(nc, [{"in_" + n: a for n, a in arrays.items()}], core_ids=[0])
    return r.results[0]["out_rows"]
```

```python
from contextlib import ExitStack

import numpy as np

import concourse.bass as bass
from concourse import mybir

F32 = mybir.dt.float32
I32 = mybir.dt.int32
U32 = mybir.dt.uint32
ALU = mybir.AluOpType
ACT = mybir.ActivationFunctionType
AX = mybir.AxisListType

P = 128
N_REAL, E_REAL = 6250, 100000
BLOCKS = -(-N_REAL // P)
NODES = BLOCKS * P
HEADS, HDIM, FEAT, EDIM = 8, 16, 128, 16
CHUNKS = P // HEADS
TILES_IN_CHUNK = -(-E_REAL // (CHUNKS * P))
GROUPS = TILES_IN_CHUNK
CHUNK = TILES_IN_CHUNK * P
EDGES = CHUNKS * CHUNK
TILES = EDGES // P
RES = BLOCKS - 1
RGROUPS = RES // CHUNKS
STEPS = TILES + RES
ALLG = GROUPS + RGROUPS
G = CHUNKS
SLOPE, EPS_DEN, EPS_LN = 0.2, 1e-9, 1e-5
NEG = -1.0e30
FAR = 1.0e5
HW = FEAT + HEADS
MW = 2 * HEADS + 2
NODE_STEP = 7
NODE_ITERS = BLOCKS // NODE_STEP
TABLES = 4
TROWS = NODES + P
WORD_BITS = 6
WORD = 1 << WORD_BITS
QUADS, QUAD = 4, 4

C_ID, C_IOTA, C_HEAD, C_BD = 0, P, 2 * P, 2 * P + HEADS
C_W3, C_THR = C_BD + 2 * CHUNKS, C_BD + 2 * CHUNKS + 1
C_DUMMY, C_BLK, C_ONE = C_THR + 1, C_THR + 2, C_THR + 3
C_WIDTH = C_ONE + P


def shape_constants():
    p = np.arange(P, dtype=np.float32)
    c = np.zeros((P, C_WIDTH), np.float32)
    c[:, C_ID:C_ID + P] = np.eye(P, dtype=np.float32)
    c[:, C_IOTA:C_IOTA + P] = p
    for lane in range(P):
        c[lane, C_HEAD + lane // HDIM] = 1.0
        for half in range(2):
            c[lane, C_BD + half * CHUNKS + lane // EDIM + 8 * half] = 1.0
    c[:, C_W3] = np.float32(3.0) ** (64 - p)
    c[:, C_THR] = np.float32(1.75) * c[:, C_W3]
    c[:, C_DUMMY] = NODES + p
    c[:, C_BLK] = P * (p + 1)
    c[:, C_ONE:] = 1.0
    return c


class Chain:

    def __init__(self, engine, sem):
        self.engine, self.sem, self.n = engine, sem, 0

    def __call__(self, instruction):
        self.n += 1
        instruction.then_inc(self.sem, 1)
        self.engine.wait_ge(self.sem, self.n)


class Memory:
    pass


def late(g):
    return not (isinstance(g, int) and g < 2)


def beside(engine, m):
    engine.wait_ge(m.begun, 1)


def take_waits(nc, m, sem):
    nc.gpsimd.tensor_tensor(m.spare[:, 0:1], m.spare[:, 1:2], m.spare[:, 2:3], ALU.add).then_inc(sem, 1)


def windows(nc, engine, m, g, q):
    word = engine.value_load(m.wtab[0:1, bass.ds(QUADS * g + q, 1)], min_val=0, max_val=WORD ** QUAD - 1)
    return [nc.s_assert_within(engine.snap((word >> u * WORD_BITS) & (WORD - 1)), 0, BLOCKS - 1, skip_runtime_bounds_check_because="each field is a block of nodes") for u in range(QUAD)]


def pairs(engine, groups, emit, first=0):
    for k in range(2):
        emit(0, k)
    with engine.Fori(1, groups // 2) as i:
        for k in range(2):
            emit(i, k)
    for g in range(groups // 2 * 2, groups):
        emit(g // 2, g % 2)


def phase_nodes(nc, m):
    with ExitStack() as ctx:
        sb = lambda name, shape, dt=F32: ctx.enter_context(nc.sbuf_tensor(name, shape, dt))
        sem = lambda name: ctx.enter_context(nc.semaphore(name))
        wn, we, av = sb("wn", [P, P]), sb("we", [P, EDIM]), sb("av", [P, 3])
        amask = sb("amask", [P, 3, HEADS])
        waug = sb("waug", [P, FEAT + 2 * HEADS])
        wrep = sb("wrep", [P, HEADS, EDIM])
        wedge = sb("wedge", [P, HEADS])
        xs, xt = sb("xs", [P, NODE_STEP, P]), sb("xt", [P, NODE_STEP, P])
        hrow = sb("hrow", [P, NODE_STEP, HW])
        R = 2 * TILES_IN_CHUNK
        ii, ff = sb("ii", [R, 2, CHUNKS // 2, P], I32), sb("ff", [R, 2, CHUNKS // 2, P])
        first_i, first_f = sb("first_i", [1, TILES], I32), sb("first_f", [1, TILES])
        block_i = sb("block_i", [1, TILES], I32)
        base = sb("base", [1, STEPS])
        block_f, word_f = sb("block_f", [1, STEPS]), sb("word_f", [1, STEPS // QUAD])
        cnt, crow = sb("cnt", [RES, 3]), sb("crow", [1, 4, RES])
        c_in, w_in, i_in, f_in, x_in = (sem(n) for n in ("c_in", "w_in", "i_in", "f_in", "x_in"))
        chain, pe_w, pe_i, pe_f, pe_c, pe_b = (sem(n) for n in ("n_chain", "pe_w", "pe_i", "pe_f", "pe_c", "pe_b"))
        base_ready, waug_ready, xt_psum, xt_ready, h_psum, h_ready, h_out, z_out = (
            sem(n) for n in ("base_ready", "waug_ready", "xt_psum", "xt_ready", "h_psum", "h_ready", "h_out", "z_out"))
        amask_ready, ff_ready, first_ready, cnt_ready, zero_ready, idx_done = (
            sem(n) for n in ("amask_ready", "ff_ready", "first_ready", "cnt_ready", "zero_ready", "idx_done"))
        C = m.const
        bank = m.bank
        ident = C[:, C_ID:C_ID + P]

        with nc.Block() as block:
            @block.sync
            def _(sp):
                sp.dma_start(C[:, :], m.in_const).then_inc(c_in, 16)
                sp.dma_start(wn[:, :], m.W_node).then_inc(w_in, 16)
                sp.dma_start(we[:, :], m.W_edge).then_inc(w_in, 16)
                sp.dma_start(av[:, :], m.attn).then_inc(w_in, 16)
                sp.dma_start(ii[:, 0, :, :], m.dst.rearrange("(q r e) -> r q e", r=R, e=P)).then_inc(i_in, 16)
                sp.dma_start(ii[:, 1, :, :], m.src.rearrange("(q r e) -> r q e", r=R, e=P)).then_inc(i_in, 16)
                with nc.allow_non_contiguous_dma(reason="first edge of each tile"):
                    first = m.dst.rearrange("(c j e) -> e j c", c=CHUNKS, e=P)
                    for j in range(TILES_IN_CHUNK):
                        sp.dma_start(first_i[0:1, j * CHUNKS:(j + 1) * CHUNKS], first[0:1, j, :]).then_inc(f_in, 16)
                sp.wait_ge(zero_ready, 1)
                for t in range(TABLES):
                    sp.dma_start(m.table[t].rearrange("(p r) f -> p (r f)", p=P),
                                 m.acc_flat[:, 0:TROWS // P * FEAT]).then_inc(z_out, 16)
                xv = m.x.rearrange("(b p) f -> p b f", p=P)
                hv = m.H.rearrange("(b p) f -> p b f", p=P)
                sp.dma_start(xs[:, :, :], xv[:, 0:NODE_STEP, :]).then_inc(x_in, 16)
                with sp.Fori(0, NODE_ITERS - 1) as i:
                    sp.wait_ge(xt_psum, i + 1)
                    sp.dma_start(xs[:, :, :], xv[:, bass.ds(NODE_STEP * i + NODE_STEP, NODE_STEP), :]).then_inc(x_in, 16)
                    sp.wait_ge(h_ready, i + 1)
                    sp.dma_start(hv[:, bass.ds(NODE_STEP * i, NODE_STEP), :], hrow[:, :, :]).then_inc(h_out, 16)
                sp.wait_ge(h_ready, NODE_ITERS)
                sp.dma_start(hv[:, BLOCKS - NODE_STEP:BLOCKS, :], hrow[:, :, :]).then_inc(h_out, 16)
                sp.wait_ge(h_out, 16 * NODE_ITERS)
                sp.wait_ge(z_out, 16 * TABLES)

            @block.vector
            def _(dve):
                link = Chain(dve, chain)
                nc.vector.memset(m.acc_flat[:, :], 0.0).then_inc(zero_ready, 1)
                nc.vector.memset(m.spare[:, :], 0.0).then_inc(m.begun, 1)
                dve.wait_ge(c_in, 16)
                dve.wait_ge(w_in, 48)
                for w in range(3):
                    last = nc.vector.tensor_scalar(amask[:, w, :], C[:, C_HEAD:C_HEAD + HEADS], av[:, w:w + 1], None, ALU.mult)
                last.then_inc(amask_ready, 1)
                link(nc.vector.tensor_copy(wrep[:, :, :], we[:, :].unsqueeze(1).to_broadcast([P, HEADS, EDIM])))
                dve.wait_ge(f_in, 16 * TILES_IN_CHUNK)
                link(nc.vector.tensor_scalar(block_i[:, :], first_i[:, :], 7, None, ALU.arith_shift_right))
                nc.vector.tensor_copy(block_f[0:1, 0:TILES], block_i[:, :])
                nc.vector.tensor_scalar(base[0:1, 0:TILES], block_i[:, :], float(P), None, ALU.mult)
                nc.vector.tensor_copy(first_f[:, :], first_i[:, :]).then_inc(first_ready, 1)
                dve.wait_ge(i_in, 32)
                nc.vector.tensor_copy(ff[:, :, :, :], ii[:, :, :, :]).then_inc(ff_ready, 1)
                dve.wait_ge(pe_w, 1)
                nc.vector.tensor_copy(waug[:, 0:FEAT], bank[6][:, 0:FEAT])
                nc.vector.tensor_copy(waug[:, FEAT:], bank[6][:, FEAT:FEAT + 2 * HEADS]).then_inc(waug_ready, 1)
                link(nc.vector.tensor_copy(wedge[:, :], bank[6][:, 256:256 + HEADS]))
                for half in range(2):
                    nc.vector.tensor_tensor(m.wblock[:, half, :, :], wedge[:, :].unsqueeze(1).to_broadcast([P, CHUNKS, HEADS]),
                                            C[:, C_BD + half * CHUNKS:C_BD + (half + 1) * CHUNKS].unsqueeze(2).to_broadcast([P, CHUNKS, HEADS]),
                                            ALU.mult)
                dve.wait_ge(pe_i, 1)
                for w, cols in enumerate((m.dstT, m.srcT)):
                    cv = cols[:, :].rearrange("p (j c) -> p c j", c=CHUNKS)
                    for q in range(CHUNKS // 2):
                        n = w * (CHUNKS // 2) + q
                        last = nc.vector.tensor_copy(cv[:, 2 * q:2 * q + 2, :], bank[n // 4][:, n % 4 * R:(n % 4 + 1) * R].rearrange("p (c j) -> p c j", c=2))
                last.then_inc(idx_done, 1)
                dve.wait_ge(pe_f, 1)
                half = TILES // 2
                for w in range(2):
                    last = nc.vector.tensor_scalar(m.scratch[0:RES, 0:half], bank[4 + w][0:RES, 0:half], C[0:RES, C_BLK:C_BLK + 1], 0.0,
                                                   ALU.is_lt, ALU.add, accum_out=cnt[:, w:w + 1])
                    link(last)
                nc.vector.tensor_tensor(cnt[:, 2:3], cnt[:, 0:1], cnt[:, 1:2], ALU.add).then_inc(cnt_ready, 1)
                dve.wait_ge(pe_c, 1)
                link(nc.vector.tensor_copy(crow[0:1, 0, :], bank[7][0:1, 0:RES]))
                link(nc.vector.tensor_scalar(crow[0:1, 1, :], crow[0:1, 0, :], -1.0, 0.0, ALU.add, ALU.max))
                nc.vector.tensor_copy(m.ttab[0:1, :], crow[0:1, 1, :])
                link(nc.vector.tensor_scalar(crow[0:1, 2, :], crow[0:1, 0, :], 0.5, FAR, ALU.is_lt, ALU.mult))
                link(nc.vector.tensor_scalar(crow[0:1, 3, :], C[0:1, C_IOTA:C_IOTA + RES], 1.0, None, ALU.add))
                link(nc.vector.tensor_copy(block_f[0:1, TILES:STEPS], crow[0:1, 3, :]))
                bv = block_f[0:1, :].rearrange("p (w u) -> p u w", u=QUAD)
                link(nc.vector.tensor_copy(word_f[:, :], bv[:, QUAD - 1, :]))
                for u in range(QUAD - 2, -1, -1):
                    link(nc.vector.scalar_tensor_tensor(word_f[:, :], word_f[:, :], float(WORD), bv[:, u, :], ALU.mult, ALU.add))
                nc.vector.tensor_copy(m.wtab[:, :], word_f[:, :])
                nc.vector.scalar_tensor_tensor(base[0:1, TILES:STEPS], crow[0:1, 3, :], float(P), crow[0:1, 2, :],
                                               ALU.mult, ALU.add).then_inc(base_ready, 1)
                dve.wait_ge(pe_b, 1)
                for w in range(2):
                    last = nc.vector.tensor_copy(m.baseB[:, w * STEPS // 2:(w + 1) * STEPS // 2], bank[6 + w][:, 0:STEPS // 2])
                link(last)
                nc.vector.tensor_scalar(m.nodeB[:, :], m.baseB[:, :], C[:, C_DUMMY:C_DUMMY + 1], float(NODES), ALU.add, ALU.subtract)
                with dve.Fori(0, NODE_ITERS) as i:
                    dve.wait_ge(h_psum, i + 1)
                    dve.wait_ge(h_out, 16 * i)
                    for n in range(4):
                        w = min(2, NODE_STEP - 2 * n)
                        hp = bank[2 + n][:, 0:512].rearrange("p (s f) -> p s f", s=2)
                        nc.vector.tensor_copy(hrow[:, 2 * n:2 * n + w, :], hp[:, 0:w, 0:HW])
                        last = nc.vector.tensor_copy(m.sdst[:, bass.ds(NODE_STEP * i + 2 * n, w), :], hp[:, 0:w, HW:HW + HEADS])
                    last.then_inc(h_ready, 1)

            @block.scalar
            def _(act):
                with act.Fori(0, NODE_ITERS) as i:
                    act.wait_ge(xt_psum, i + 1)
                    act.wait_ge(h_psum, i)
                    nc.scalar.copy(xt[:, 0:4, :], bank[0][:, :].rearrange("p (s f) -> p s f", s=4))
                    nc.scalar.copy(xt[:, 4:7, :], bank[1][:, 0:3 * P].rearrange("p (s f) -> p s f", s=3)).then_inc(xt_ready, 1)

            @block.tensor
            def _(pe):
                pe.wait_ge(amask_ready, 1)
                pe.wait_ge(chain, 1)
                nc.tensor.transpose(bank[6][:, 0:P], wn[:, :], ident)
                nc.tensor.matmul(bank[6][:, FEAT:FEAT + 2 * HEADS], wn[:, :], amask[:, 0:2, :].rearrange("p a h -> p (a h)"), start=True, stop=True)
                nc.tensor.matmul(bank[6][:, 256:256 + HEADS], wrep[:, :, :].rearrange("p a i -> p (a i)"), amask[:, 2, :], start=True, stop=True).then_inc(pe_w, 1)
                pe.wait_ge(ff_ready, 1)
                for w in range(2):
                    for q in range(CHUNKS // 2):
                        n = w * (CHUNKS // 2) + q
                        last = nc.tensor.transpose(bank[n // 4][:, n % 4 * R:(n % 4 + 1) * R], ff[:, w, q, :], C[0:R, C_ID:C_ID + R])
                last.then_inc(pe_i, 1)
                pe.wait_ge(first_ready, 1)
                for w in range(2):
                    last = nc.tensor.matmul(bank[4 + w][0:RES, 0:TILES // 2], C[0:1, C_ONE:C_ONE + RES],
                                            first_f[0:1, w * TILES // 2:(w + 1) * TILES // 2], start=True, stop=True)
                last.then_inc(pe_f, 1)
                pe.wait_ge(cnt_ready, 1)
                nc.tensor.matmul(bank[7][0:1, 0:RES], cnt[:, 2:3], C[0:RES, C_ID:C_ID + RES], start=True, stop=True).then_inc(pe_c, 1)
                pe.wait_ge(base_ready, 1)
                pe.wait_ge(waug_ready, 1)
                for w in range(2):
                    last = nc.tensor.matmul(bank[6 + w][:, 0:STEPS // 2], C[0:1, C_ONE:C_ONE + P],
                                            base[0:1, w * STEPS // 2:(w + 1) * STEPS // 2], start=True, stop=True)
                last.then_inc(pe_b, 1)
                pe.wait_ge(idx_done, 1)
                with pe.Fori(0, NODE_ITERS) as i:
                    pe.wait_ge(x_in, 16 * i + 16)
                    pe.wait_ge(xt_ready, i)
                    for u in range(NODE_STEP):
                        last = nc.tensor.transpose(bank[u // 4][:, u % 4 * P:(u % 4 + 1) * P], xs[:, u, :], ident)
                    last.then_inc(xt_psum, 1)
                    pe.wait_ge(xt_ready, i + 1)
                    pe.wait_ge(h_ready, i)
                    for u in range(NODE_STEP):
                        last = nc.tensor.matmul(bank[2 + u // 2][:, u % 2 * 256:u % 2 * 256 + HW + HEADS], xt[:, u, :], waug[:, :], start=True, stop=True)
                    last.then_inc(h_psum, 1)


def phase_scores(nc, m, aT):
    with ExitStack() as ctx:
        sb = lambda name, shape, dt=F32: ctx.enter_context(nc.sbuf_tensor(name, shape, dt))
        sem = lambda name: ctx.enter_context(nc.semaphore(name))
        rows = sb("rows", [P, 2, G, HW])
        ef, efT = sb("ef", [P, 2, G, EDIM]), sb("efT", [P, 2, 2, P])
        s_src = sb("s_src", [P, 2, G * HEADS])
        idx = [sb(f"idx{k}", [P, G], U32) for k in range(2)]
        ef_in = [sem(f"ef_in{k}") for k in range(2)]
        rows_out = [sem(f"rows_out{k}") for k in range(2)]
        got = m.got
        idx_ready, efT_psum, efT_ready, a_psum, a_ready, packed, taken = (
            sem(n) for n in ("idx_ready", "efT_psum", "efT_ready", "a_psum", "a_ready", "packed", "taken"))
        bank = m.bank
        ident = m.const[:, C_ID:C_ID + P]
        ev = m.ea16.rearrange("(c j p) f -> j p c f", c=CHUNKS, p=P)
        hv = m.Hs.rearrange("(c j p) f -> j p c f", c=CHUNKS, p=P)

        def gathered(engine, g):
            for s in range(G):
                engine.wait_ge(got[s], 16 * (g + 1))

        with nc.Block() as block:
            @block.sync
            def _(sp):
                def load(i, k):
                    g = 2 * i + k
                    if late(g):
                        sp.wait_ge(efT_psum, g - 1)
                    sp.dma_start(ef[:, k, :, :], ev[g] if isinstance(g, int) else ev[bass.ds(g, 1)].rearrange("a p c f -> (a p) c f")).then_inc(ef_in[k], 16)

                pairs(sp, GROUPS, load)

            @block.gpsimd
            def _(pool):
                def gather(i, k):
                    g = 2 * i + k
                    pool.wait_ge(idx_ready, g + 1)
                    if late(g):
                        pool.wait_ge(rows_out[k], 16 * i)
                        pool.wait_ge(packed, g - 1)
                    if late(g) or g:
                        pool.wait_ge(got[0], 16 * g)
                        pool.wait_ge(taken, g)
                    take_waits(nc, m, taken)
                    for s in range(G):
                        if late(g) or g:
                            beside(pool, m)
                            pool.wait_ge(got[s], 16 * g)
                        nc.gpsimd.indirect_dma_start(rows[:, k, s, :], None, m.H, bass.IndirectOffsetOnAxis(ap=idx[k][:, s:s + 1], axis=0)).then_inc(got[s], 16)

                pairs(pool, GROUPS, gather)

            @block.scalar
            def _(act):
                def work(i, k):
                    g = 2 * i + k
                    gathered(act, g)
                    nc.scalar.copy(s_src[:, k, :].rearrange("p (c h) -> p c h", h=HEADS), rows[:, k, :, FEAT:HW]).then_inc(packed, 1)
                    if late(g):
                        act.wait_ge(rows_out[k], 16 * i)
                    act.dma_start(hv[g] if isinstance(g, int) else hv[bass.ds(g, 1)].rearrange("a p c f -> (a p) c f"), rows[:, k, :, 0:FEAT]).then_inc(rows_out[k], 16)
                    act.wait_ge(a_psum, g + 1)
                    nc.scalar.copy(aT[:, bass.ds(P * g, P)], bank[2 + k][:, 0:P]).then_inc(a_ready, 1)

                pairs(act, GROUPS, work)
                act.wait_ge(rows_out[0], 16 * (GROUPS - GROUPS // 2))
                act.wait_ge(rows_out[1], 16 * (GROUPS // 2))

            @block.vector
            def _(dve):
                def work(i, k):
                    g = 2 * i + k
                    if late(g):
                        gathered(dve, g - 2)
                    nc.vector.tensor_copy(idx[k][:, :], m.srcT[:, bass.ds(G * g, G)]).then_inc(idx_ready, 1)
                    dve.wait_ge(efT_psum, g + 1)
                    if late(g):
                        dve.wait_ge(a_psum, g - 1)
                    nc.vector.tensor_copy(efT[:, k, :, :], bank[k][:, 0:2 * P].rearrange("p (a e) -> p a e", a=2)).then_inc(efT_ready, 1)

                pairs(dve, GROUPS, work)

            @block.tensor
            def _(pe):
                def work(i, k):
                    g = 2 * i + k
                    pe.wait_ge(ef_in[k], 16 * i + 16)
                    if late(g):
                        pe.wait_ge(efT_ready, g - 1)
                    e2 = ef[:, k, :, :].rearrange("p (a c) f -> p a (c f)", a=2)
                    for half in range(2):
                        last = nc.tensor.transpose(bank[k][:, half * P:(half + 1) * P], e2[:, half, :], ident)
                    last.then_inc(efT_psum, 1)
                    pe.wait_ge(efT_ready, g + 1)
                    if late(g):
                        pe.wait_ge(a_ready, g - 1)
                    for half in range(2):
                        nc.tensor.matmul(bank[2 + k][:, 0:P], m.wblock[:, half, :, :].rearrange("p c h -> p (c h)"), efT[:, k, half, :], start=(half == 0), stop=False)
                    pe.wait_ge(packed, g + 1)
                    nc.tensor.matmul(bank[2 + k][:, 0:P], s_src[:, k, :], ident, start=False, stop=True).then_inc(a_psum, 1)

                pairs(pe, GROUPS, work)


def phase_scan(nc, m, aT, amax):
    with ExitStack() as ctx:
        sb = lambda name, shape, dt=F32: ctx.enter_context(nc.sbuf_tensor(name, shape, dt))
        sem = lambda name: ctx.enter_context(nc.semaphore(name))
        di = sb("di", [P, CHUNK], I32)
        pen = sb("pen", [P, CHUNK + 1])
        fwd = sb("fwd", [P, CHUNK])
        ends_i = sb("ends_i", [HEADS, 2, CHUNKS], I32)
        ends = sb("ends", [HEADS, 2, CHUNKS])
        whole, joint, both = sb("whole", [HEADS, CHUNKS]), sb("joint", [HEADS, CHUNKS]), sb("both", [HEADS, 2, CHUNKS])
        tip, run = sb("tip", [HEADS, 2, CHUNKS]), sb("run", [HEADS, 2, CHUNKS])
        carry, carryT = sb("carry", [HEADS, 2, CHUNKS]), sb("carryT", [P, 2])
        tips = sb("tips", [P, 2])
        d_in, e_in, t_out, t_in, c_out, c_in2 = (sem(n) for n in ("d_in", "e_in", "t_out", "t_in", "c_out", "c_in2"))
        chain, tips_ready, carry_ready = sem("s_chain"), sem("tips_ready"), sem("carry_ready")
        dv = m.dst.rearrange("(c e) -> c e", c=CHUNKS)

        with nc.Block() as block:
            @block.sync
            def _(sp):
                for c in range(CHUNKS):
                    sp.dma_start(di[c * HEADS:(c + 1) * HEADS, :], dv[c:c + 1, :].to_broadcast([HEADS, CHUNK])).then_inc(d_in, 16)
                with nc.allow_non_contiguous_dma(reason="ends of the chunks"):
                    for w, e in enumerate((0, CHUNK - 1)):
                        sp.dma_start(ends_i[:, w, :], dv[:, e:e + 1].rearrange("c e -> e c").to_broadcast([HEADS, CHUNKS])).then_inc(e_in, 16)
                    sp.wait_ge(tips_ready, 1)
                    sp.dma_start(m.tips, tips[:, :]).then_inc(t_out, 16)
                    sp.wait_ge(t_out, 16)
                    for w in range(2):
                        sp.dma_start(tip[:, w, :], m.tips.rearrange("(c h) w -> h w c", h=HEADS)[:, w, :]).then_inc(t_in, 16)
                    sp.wait_ge(carry_ready, 1)
                    for w in range(2):
                        sp.dma_start(m.carries.rearrange("(c h) w -> h w c", h=HEADS)[:, w, :], carry[:, w, :]).then_inc(c_out, 16)
                    sp.wait_ge(c_out, 32)
                    sp.dma_start(carryT[:, :], m.carries).then_inc(c_in2, 16)

            @block.vector
            def _(dve):
                link = Chain(dve, chain)
                v = nc.vector
                v.memset(pen[:, 0:1], 0.0)
                link(v.memset(pen[:, CHUNK:CHUNK + 1], 0.0))
                dve.wait_ge(d_in, 16 * CHUNKS)
                link(v.tensor_tensor(pen[:, 1:CHUNK], di[:, 1:CHUNK], di[:, 0:CHUNK - 1], ALU.not_equal))
                link(v.tensor_scalar(pen[:, 1:CHUNK], pen[:, 1:CHUNK], NEG, None, ALU.mult))
                link(v.tensor_tensor_scan(fwd[:, :], pen[:, 0:CHUNK], aT[:, :], NEG, ALU.add, ALU.max))
                link(v.tensor_copy(tips[:, 0:1], fwd[:, CHUNK - 1:CHUNK]))
                link(v.tensor_tensor_scan(amax[:, ::-1], pen[:, CHUNK:0:-1], aT[:, ::-1], NEG, ALU.add, ALU.max))
                v.tensor_copy(tips[:, 1:2], amax[:, 0:1]).then_inc(tips_ready, 1)
                dve.wait_ge(e_in, 32)
                link(v.tensor_copy(ends[:, :, :], ends_i[:, :, :]))
                link(v.tensor_tensor(whole[:, :], ends[:, 0, :], ends[:, 1, :], ALU.not_equal))
                link(v.tensor_scalar(whole[:, :], whole[:, :], NEG, None, ALU.mult))
                link(v.memset(joint[:, :], NEG))
                L = CHUNKS - 1
                link(v.tensor_tensor(joint[:, 0:L], ends[:, 1, 0:L], ends[:, 0, 1:CHUNKS], ALU.not_equal))
                link(v.tensor_scalar(joint[:, 0:L], joint[:, 0:L], NEG, None, ALU.mult))
                link(v.memset(both[:, :, :], NEG))
                link(v.tensor_tensor(both[:, 0, 1:CHUNKS], whole[:, 1:CHUNKS], joint[:, 0:L], ALU.add))
                link(v.tensor_tensor(both[:, 1, 0:L], whole[:, 0:L], joint[:, 0:L], ALU.add))
                dve.wait_ge(t_in, 32)
                link(v.tensor_tensor_scan(run[:, 0, :], both[:, 0, :], tip[:, 0, :], NEG, ALU.add, ALU.max))
                link(v.tensor_tensor_scan(run[:, 1, ::-1], both[:, 1, ::-1], tip[:, 1, ::-1], NEG, ALU.add, ALU.max))
                link(v.memset(carry[:, :, :], NEG))
                link(v.tensor_tensor(carry[:, 0, 1:CHUNKS], run[:, 0, 0:L], joint[:, 0:L], ALU.add))
                v.tensor_tensor(carry[:, 1, 0:L], run[:, 1, 1:CHUNKS], joint[:, 0:L], ALU.add).then_inc(carry_ready, 1)
                dve.wait_ge(c_in2, 16)
                link(v.tensor_tensor_scan(fwd[:, :], pen[:, 0:CHUNK], aT[:, :], carryT[:, 0:1], ALU.add, ALU.max))
                link(v.tensor_tensor_scan(amax[:, ::-1], pen[:, CHUNK:0:-1], aT[:, ::-1], carryT[:, 1:2], ALU.add, ALU.max))
                link(v.tensor_tensor(amax[:, :], amax[:, :], fwd[:, :], ALU.max))


def phase_meta(nc, m, aT, amax):
    with ExitStack() as ctx:
        sb = lambda name, shape, dt=F32: ctx.enter_context(nc.sbuf_tensor(name, shape, dt))
        sem = lambda name: ctx.enter_context(nc.semaphore(name))
        stage, meta = sb("stage", [P, 2, 2, P]), sb("meta_s", [P, 2, G, MW])
        staged, turned, filled, cols = (sem(n) for n in ("staged", "turned", "filled", "cols"))
        out = [sem(f"meta_out{k}") for k in range(2)]
        bank = m.bank
        ident = m.const[:, C_ID:C_ID + P]
        mv = m.meta.rearrange("(c j p) f -> j p c f", c=CHUNKS, p=P)

        with nc.Block() as block:
            @block.sync
            def _(sp):
                def work(i, k):
                    g = 2 * i + k
                    sp.wait_ge(filled, g + 1)
                    sp.wait_ge(cols, g + 1)
                    sp.dma_start(mv[g] if isinstance(g, int) else mv[bass.ds(g, 1)].rearrange("a p c f -> (a p) c f"), meta[:, k, :, :]).then_inc(out[k], 16)

                pairs(sp, GROUPS, work)
                sp.wait_ge(out[0], 16 * (GROUPS - GROUPS // 2))
                sp.wait_ge(out[1], 16 * (GROUPS // 2))

            @block.scalar
            def _(act):
                def work(i, k):
                    g = 2 * i + k
                    if late(g):
                        act.wait_ge(turned, g - 1)
                    nc.scalar.copy(stage[:, k, 0, :], aT[:, bass.ds(P * g, P)])
                    nc.scalar.copy(stage[:, k, 1, :], amax[:, bass.ds(P * g, P)]).then_inc(staged, 1)

                pairs(act, GROUPS, work)

            @block.tensor
            def _(pe):
                def work(i, k):
                    g = 2 * i + k
                    pe.wait_ge(staged, g + 1)
                    if late(g):
                        pe.wait_ge(filled, g - 1)
                    for w in range(2):
                        last = nc.tensor.transpose(bank[k][:, w * P:(w + 1) * P], stage[:, k, w, :], ident)
                    last.then_inc(turned, 1)

                pairs(pe, GROUPS, work)

            @block.vector
            def _(dve):
                def work(i, k):
                    g = 2 * i + k
                    if late(g):
                        dve.wait_ge(out[k], 16 * i)
                    nc.vector.tensor_copy(meta[:, k, :, 2 * HEADS], m.dstT[:, bass.ds(G * g, G)])
                    nc.vector.tensor_copy(meta[:, k, :, 2 * HEADS + 1], m.srcT[:, bass.ds(G * g, G)]).then_inc(cols, 1)
                    dve.wait_ge(turned, g + 1)
                    nc.vector.tensor_copy(meta[:, k, :, 0:2 * HEADS].rearrange("p c (w h) -> p w c h", w=2),
                                          bank[k][:, 0:2 * P].rearrange("p (w c h) -> p w c h", w=2, c=CHUNKS)).then_inc(filled, 1)

                pairs(dve, GROUPS, work)


def load_steps(nc, sp, m, i, k, parts, sem, residual):
    g = 2 * i + k

    def at(v, n, form):
        return v[n] if isinstance(n, int) else v[bass.ds(n, 1)].rearrange(form)

    for rows, slot in parts:
        spread = len(rows.shape) == 1
        if residual:
            continue
        for half in range(2):
            cs = slice(half * G // 2, (half + 1) * G // 2)
            if spread:
                v = at(rows.rearrange("(c j p) -> j c p", c=CHUNKS, p=P), g, "a c p -> (a c) p")
                sp.dma_start(slot[:, cs, :], v[cs, :].unsqueeze(0).to_broadcast([P, G // 2, P])).then_inc(sem, 16)
            else:
                v = at(rows.rearrange("(c j p) f -> j p c f", c=CHUNKS, p=P), g, "a p c f -> (a p) c f")
                sp.dma_start(slot[:, cs, :], v[:, cs, :]).then_inc(sem, 16)
    for s in range(G) if residual else ():
        r = (g - GROUPS) * G + s
        tile = sp.value_load(m.ttab[0:1, r:r + 1], min_val=0, max_val=TILES - 1)
        for rows, slot in parts:
            if len(rows.shape) == 1:
                v = rows.rearrange("(t p) -> t p", p=P)[bass.ds(tile, 1)]
                sp.dma_start(slot[:, s, :], v.to_broadcast([P, P])).then_inc(sem, 16)
            else:
                v = rows.rearrange("(t p) f -> t p f", p=P)
                sp.dma_start(slot[:, s, :], v[bass.ds(tile, 1)].rearrange("a p f -> (a p) f")).then_inc(sem, 16)


def arrived(engine, main, rest, i, k, parts):
    g = 2 * i + k
    if isinstance(g, int) and g >= GROUPS:
        engine.wait_ge(rest[g - GROUPS], 16 * G * parts)
    else:
        engine.wait_ge(main[k], 2 * 16 * parts * (i + 1))




def phase_attend(nc, m):
    with ExitStack() as ctx:
        sb = lambda name, shape, dt=F32: ctx.enter_context(nc.sbuf_tensor(name, shape, dt))
        sem = lambda name: ctx.enter_context(nc.semaphore(name))
        h, meta = sb("h_b", [P, 2, G, FEAT]), sb("meta_b", [P, 2, G, MW])
        rel = sb("rel_b", [P, 2, G])
        O, OT = sb("O_b", [P, 2, G, P]), sb("OT_b", [P, 2, QUAD, P])
        msg = sb("msg_b", [P, 2, G, HW])
        z, zm, lz, gap = (sb(n, [P, G, HEADS]) for n in ("z_b", "zm_b", "lz_b", "gap_b"))
        main = [sem(f"b_in{k}") for k in range(2)]
        rest = [sem(f"b_rest{r}") for r in range(RGROUPS)]
        odd_zero, rel_ready, O_ready, OT_psum, OT_ready, spread_done, ex_ready, msg_ready, chain = (
            sem(n) for n in ("odd_zero", "rel_ready", "bO_ready", "bOT_psum", "bOT_ready", "spread_done", "ex_ready", "msg_ready", "b_chain"))
        agg_psum, added = [sem(f"bagg{u}") for u in range(QUAD)], [sem(f"badded{u}") for u in range(QUAD)]
        bank = m.bank
        ident = m.const[:, C_ID:C_ID + P]
        iota = m.const[:, C_IOTA:C_IOTA + P]
        slot = lambda s: bank[4 + s % 4][:, 0:HW]

        def run(engine, emit):
            emit(0, 0)
            emit(0, 1)
            with engine.Fori(1, GROUPS // 2) as i:
                emit(i, 0)
                emit(i, 1)
            for g in range(GROUPS // 2 * 2, ALLG + 1):
                emit(g // 2, g % 2)

        with nc.Block() as block:
            @block.sync
            def _(sp):
                def load(i, k):
                    g = 2 * i + k
                    residual = isinstance(g, int) and g >= GROUPS
                    if late(g):
                        beside(sp, m)
                        sp.wait_ge(msg_ready, g - 1)
                    load_steps(nc, sp, m, i, k, [(m.Hs, h[:, k, :, :]), (m.meta, meta[:, k, :, :])],
                               rest[g - GROUPS] if residual else main[k], residual)

                pairs(sp, GROUPS, load)
                for g in range(GROUPS, ALLG):
                    load(g // 2, g % 2)

            @block.vector
            def _(dve):
                v = nc.vector
                v.memset(m.acc_odd[:, :, :], 0.0).then_inc(odd_zero, 1)
                dve.wait_ge(odd_zero, 1)

                def hot(i, k):
                    g = 2 * i + k
                    arrived(dve, main, rest, i, k, 2)
                    if late(g):
                        dve.wait_ge(agg_psum[QUAD - 1], QUADS * (g - 1))
                    v.tensor_tensor(rel[:, k, :], meta[:, k, :, 2 * HEADS], m.baseB[:, bass.ds(G * g, G)], ALU.subtract).then_inc(rel_ready, 1)
                    dve.wait_ge(rel_ready, g + 1)
                    v.tensor_tensor(O[:, k, :, :], iota.unsqueeze(1).to_broadcast([P, G, P]), rel[:, k, :].unsqueeze(2).to_broadcast([P, G, P]), ALU.is_equal).then_inc(O_ready, 1)

                def scores(i, k):
                    g = 2 * i + k
                    arrived(dve, main, rest, i, k, 2)
                    dve.wait_ge(spread_done, QUADS * g + QUADS)
                    if late(g) or g:
                        dve.wait_ge(ex_ready, g)
                    sd = bank[2 + k][:, 0:G * HEADS].rearrange("p (s h) -> p s h", s=G)
                    v.tensor_tensor(zm[:, :, :], meta[:, k, :, HEADS:2 * HEADS], sd, ALU.add)
                    v.tensor_tensor(z[:, :, :], meta[:, k, :, 0:HEADS], sd, ALU.add).then_inc(chain, 1)
                    dve.wait_ge(chain, 3 * g + 1)
                    v.scalar_tensor_tensor(lz[:, :, :], z[:, :, :], SLOPE, z[:, :, :], ALU.mult, ALU.max).then_inc(chain, 1)
                    dve.wait_ge(chain, 3 * g + 2)
                    v.scalar_tensor_tensor(gap[:, :, :], zm[:, :, :], 0.0, lz[:, :, :], ALU.max, ALU.subtract).then_inc(chain, 1)

                def sums(g, k):
                    for q in range(QUADS):
                        blocks = windows(nc, dve, m, g, q)
                        for u in range(QUAD):
                            if u >= 2:
                                dve.wait_ge(added[u - 2], QUADS * g + q + 1)
                            elif q or not (isinstance(g, int) and g < 1):
                                dve.wait_ge(added[u + 2], QUADS * g + q)
                            dve.wait_ge(agg_psum[u], QUADS * g + q + 1)
                            a = (m.acc, m.acc_odd)[u % 2][:, bass.ds(blocks[u], 1), :].rearrange("p b f -> p (b f)")
                            v.tensor_tensor(a, a, slot(u), ALU.add).then_inc(added[u], 1)

                def work(i, k):
                    g = 2 * i + k
                    if not (isinstance(g, int) and g >= ALLG):
                        hot(i, k)
                    if late(g) or g:
                        sums(g - 1, 1 - k)
                    if not (isinstance(g, int) and g >= ALLG):
                        scores(i, k)

                run(dve, work)

            @block.gpsimd
            def _(pool):
                def weigh(i, k):
                    g = 2 * i + k
                    pool.wait_ge(ex_ready, g + 1)
                    nc.gpsimd.tensor_tensor(msg[:, k, :, 0:FEAT].rearrange("p s (h d) -> p s h d", h=HEADS),
                                            h[:, k, :, :].rearrange("p s (h d) -> p s h d", h=HEADS),
                                            msg[:, k, :, FEAT:HW].unsqueeze(3).to_broadcast([P, G, HEADS, HDIM]), ALU.mult).then_inc(msg_ready, 1)

                pairs(pool, GROUPS, weigh)
                for g in range(GROUPS, ALLG):
                    weigh(g // 2, g % 2)

            @block.scalar
            def _(act):
                def work(i, k):
                    g = 2 * i + k
                    for q in range(QUADS):
                        act.wait_ge(OT_psum, QUADS * g + q + 1)
                        if late(g) or g or q > 1:
                            act.wait_ge(spread_done, QUADS * g + q - 1)
                        nc.scalar.copy(OT[:, q % 2, :, :], bank[q % 2][:, :].rearrange("p (s e) -> p s e", s=QUAD)).then_inc(OT_ready, 1)
                    act.wait_ge(chain, 3 * g + 3)
                    if late(g):
                        act.wait_ge(agg_psum[QUAD - 1], QUADS * (g - 1))
                    nc.scalar.activation(msg[:, k, :, FEAT:HW], gap[:, :, :], ACT.Exp, scale=-1.0).then_inc(ex_ready, 1)

                pairs(act, GROUPS, work)
                for g in range(GROUPS, ALLG):
                    work(g // 2, g % 2)

            @block.tensor
            def _(pe):
                def turn(g, k, q):
                    if late(g) or g or q > 1:
                        pe.wait_ge(OT_ready, QUADS * g + q - 1)
                    for u in range(QUAD):
                        last = nc.tensor.transpose(bank[q % 2][:, u * P:(u + 1) * P], O[:, k, QUAD * q + u, :], ident)
                    last.then_inc(OT_psum, 1)

                def spread(g, k, q):
                    blocks = windows(nc, pe, m, g, q)
                    pe.wait_ge(OT_ready, QUADS * g + q + 1)
                    for u in range(QUAD):
                        s = QUAD * q + u
                        last = nc.tensor.matmul(bank[2 + k][:, s * HEADS:(s + 1) * HEADS], OT[:, q % 2, u, :],
                                                m.sdst[:, bass.ds(blocks[u], 1), :].rearrange("p b h -> p (b h)"), start=True, stop=True)
                    last.then_inc(spread_done, 1)

                def total(g, k, q):
                    for u in range(QUAD):
                        s = QUAD * q + u
                        if q or not (isinstance(g, int) and g < 1):
                            pe.wait_ge(added[u], QUADS * g + q)
                        nc.tensor.matmul(slot(u), O[:, k, s, :], msg[:, k, s, :], start=True, stop=True).then_inc(agg_psum[u], 1)

                def work(i, k):
                    g = 2 * i + k
                    begins, ends = not (isinstance(g, int) and g >= ALLG), late(g) or g
                    if begins:
                        pe.wait_ge(O_ready, g + 1)
                        turn(g, k, 0)
                    if ends:
                        pe.wait_ge(msg_ready, g)
                    for q in range(QUADS):
                        if ends:
                            total(g - 1, 1 - k, q)
                        if begins and q + 1 < QUADS:
                            turn(g, k, q + 1)
                        if begins:
                            spread(g, k, q)

                run(pe, work)


def phase_norm(nc, m, last_layer):
    L = "2" if last_layer else "1"
    with ExitStack() as ctx:
        sb = lambda name, shape, dt=F32: ctx.enter_context(nc.sbuf_tensor(name + L, shape, dt))
        sem = lambda name: ctx.enter_context(nc.semaphore(name + L))
        S = NODE_STEP
        y, e, sq = sb("y", [P, S, FEAT]), sb("e", [P, S, FEAT]), sb("sq", [P, S, FEAT])
        rec = sb("rec", [P, S, HEADS])
        add = sb("add", [P, TABLES, S, FEAT])
        mean, var, dev = sb("mean", [P, S]), sb("var", [P, S]), sb("dev", [P, S])
        eps = sb("eps", [P, 1])
        chain, dev_ready, normed, ready = (m.norm[n] for n in ("norm_chain", "dev_ready", "normed", "eps_ready"))
        x_in, out = sem("f_in"), sem("f_out")
        if not last_layer:
            exp_ready, exp_less, summed, halves = sem("exp_ready"), sem("exp_less"), sem("summed"), sem("halves")
        BEFORE = NODE_ITERS if last_layer else 0
        PER = 5 + 6
        xv = m.x.rearrange("(b p) f -> p b f", p=P)
        REST = N_REAL - (BLOCKS - 1) * P

        with nc.Block() as block:
            @block.sync
            def _(sp):
                with sp.Fori(0, NODE_ITERS) as i:
                    sp.wait_ge(normed, i + BEFORE)
                    if last_layer:
                        for t in range(TABLES):
                            tv = m.table[t][0:NODES, :].rearrange("(b p) f -> p b f", p=P)
                            sp.dma_start(add[:, t, :, :], tv[:, bass.ds(S * i, S), :]).then_inc(x_in, 16)
                    else:
                        sp.dma_start(add[:, 0, :, :], xv[:, bass.ds(S * i, S), :]).then_inc(x_in, 16)
                        sp.wait_ge(normed, i + 1 + BEFORE)
                        sp.dma_start(m.X1.rearrange("(b p) f -> p b f", p=P)[:, bass.ds(S * i, S), :], m.x1[:, bass.ds(S * i, S), :]).then_inc(out, 16)
                if last_layer:
                    sp.wait_ge(normed, NODE_ITERS + BEFORE)
                    sp.dma_start(m.out[0:(BLOCKS - 1) * P, :].rearrange("(b p) f -> p b f", p=P), m.x1[:, 0:BLOCKS - 1, :]).then_inc(out, 16)
                    sp.dma_start(m.out[(BLOCKS - 1) * P:N_REAL, :], m.x1[0:REST, BLOCKS - 1, :]).then_inc(out, 16)
                    sp.wait_ge(out, 32)
                else:
                    sp.wait_ge(out, 16 * NODE_ITERS)

            @block.scalar
            def _(act):
                act.wait_ge(ready, 2 if last_layer else 1)
                with act.Fori(0, NODE_ITERS) as i:
                    if not last_layer:
                        act.wait_ge(chain, PER * (i + BEFORE) + 4)
                        nc.scalar.activation(e[:, :, :], e[:, :, :], ACT.Exp).then_inc(exp_ready, 1)
                    act.wait_ge(chain, PER * (i + BEFORE) + 10)
                    nc.scalar.activation(dev[:, :], var[:, :], ACT.Sqrt, bias=eps[:, 0:1], scale=1.0 / FEAT).then_inc(dev_ready, 1)

            @block.vector
            def _(dve):
                v = nc.vector
                v.memset(eps[:, :], EPS_LN).then_inc(ready, 1)
                with dve.Fori(0, NODE_ITERS) as i:
                    here = bass.ds(S * i, S)
                    done = [0]

                    def link(instruction):
                        done[0] += 1
                        instruction.then_inc(chain, 1)
                        dve.wait_ge(chain, PER * (i + BEFORE) + done[0])

                    if last_layer:
                        dve.wait_ge(x_in, 16 * TABLES * (i + 1))
                        link(v.tensor_tensor(y[:, :, :], m.x1[:, here, :], m.acc1[:, here, :], ALU.add))
                        for t in range(TABLES):
                            link(v.tensor_tensor(y[:, :, :], y[:, :, :], add[:, t, :, :], ALU.add))
                    else:
                        v.tensor_tensor(m.acc[:, here, :], m.acc[:, here, :], m.acc_odd[:, here, :], ALU.add).then_inc(halves, 1)
                        dve.wait_ge(halves, i + 1)
                        link(v.tensor_scalar(rec[:, :, :], m.acc[:, here, FEAT:HW], EPS_DEN, None, ALU.add))
                        link(v.reciprocal(rec[:, :, :], rec[:, :, :]))
                        y4 = y[:, :, :].rearrange("p s (h d) -> p s h d", h=HEADS)
                        for s in range(S):
                            a = m.acc[:, bass.ds(S * i + s, 1), 0:FEAT].rearrange("p b (h d) -> p (b h) d", h=HEADS)
                            last = v.tensor_tensor(y4[:, s, :, :], a, rec[:, s, :].unsqueeze(2).to_broadcast([P, HEADS, HDIM]), ALU.mult)
                        link(last)
                        link(v.tensor_scalar(e[:, :, :], y[:, :, :], 0.0, None, ALU.min))
                        dve.wait_ge(exp_ready, i + 1)
                        v.tensor_scalar(e[:, :, :], e[:, :, :], -1.0, None, ALU.add).then_inc(exp_less, 1)
                        dve.wait_ge(exp_less, i + 1)
                        link(v.scalar_tensor_tensor(y[:, :, :], y[:, :, :], 0.0, e[:, :, :], ALU.max, ALU.add))
                        dve.wait_ge(x_in, 16 * (i + 1))
                        v.tensor_tensor(y[:, :, :], y[:, :, :], add[:, 0, :, :], ALU.add).then_inc(summed, 1)
                        dve.wait_ge(summed, i + 1)
                    link(v.tensor_reduce(mean[:, :], y[:, :, :], AX.X, ALU.add))
                    link(v.tensor_scalar(mean[:, :], mean[:, :], 1.0 / FEAT, None, ALU.mult))
                    link(v.tensor_tensor(y[:, :, :], y[:, :, :], mean[:, :].unsqueeze(2).to_broadcast([P, S, FEAT]), ALU.subtract))
                    link(v.tensor_tensor(sq[:, :, :], y[:, :, :], y[:, :, :], ALU.mult))
                    link(v.tensor_reduce(var[:, :], sq[:, :, :], AX.X, ALU.add))
                    dve.wait_ge(dev_ready, i + 1 + BEFORE)
                    link(v.reciprocal(dev[:, :], dev[:, :]))
                    assert done[0] == PER
                    v.tensor_tensor(m.x1[:, here, :], y[:, :, :], dev[:, :].unsqueeze(2).to_broadcast([P, S, FEAT]), ALU.mult).then_inc(normed, 1)


def phase_messages(nc, m):
    with ExitStack() as ctx:
        sb = lambda name, shape, dt=F32: ctx.enter_context(nc.sbuf_tensor(name, shape, dt))
        sem = lambda name: ctx.enter_context(nc.semaphore(name))
        ea, got_rows = sb("ea", [P, 2, G, FEAT]), sb("got_rows", [P, 2, G, FEAT])
        ends = sb("ends_l", [P, 2, G, 2])
        rel = sb("rel_l", [P, 2, G])
        dstR, srcR = sb("dstR", [P, 2, G, P], I32), sb("srcR", [P, 2, G, P], I32)
        O, OT = sb("O_l", [P, 2, G, P]), sb("OT_l", [P, G, P])
        same = sb("same", [P, G, P])
        back = sb("back", [P, G, FEAT])
        merged = sb("merged", [P, 2, G, FEAT])
        dup, far = sb("dup", [P, G]), sb("far", [P, G])
        idx = [sb(f"gidx{k}", [P, G], U32) for k in range(2)]
        sidx = [sb(f"sidx{k}", [P, G], U32) for k in range(2)]
        main = [sem(f"l_in{k}") for k in range(2)]
        rest = [sem(f"l_rest{r}") for r in range(RGROUPS)]
        got = m.got
        put = [sem(f"put{s}") for s in range(G)]
        merged_ready = [sem(f"l_merged{q}") for q in range(QUADS)]
        (idx_ready, O_ready, OT_ready, same_ready, rank_psum, sidx_ready, spread_done, back_ready,
         merged_psum, fwd_ready, agg_psum, added, chain, taken) = (
            sem(n) for n in ("l_idx", "l_O", "l_OT", "l_same", "l_rank", "l_sidx", "l_spread", "l_back",
                             "l_mergedp", "l_fwd", "l_agg", "l_added", "l_chain", "l_taken"))
        bank = m.bank
        C = m.const
        ident = C[:, C_ID:C_ID + P]
        iota = C[:, C_IOTA:C_IOTA + P]
        quad_of = lambda t, q: t[:, QUAD * q:QUAD * (q + 1), :]
        as_quad = lambda b: b[:, :].rearrange("p (s e) -> p s e", s=QUAD)

        def gathered(engine, g):
            for s in range(G):
                engine.wait_ge(got[s], 16 * (g + GROUPS + 1))

        def scattered(engine, g):
            for s in range(G):
                engine.wait_ge(put[s], 16 * (g + 1))

        def all_groups(engine, emit):
            pairs(engine, GROUPS, emit)
            for g in range(GROUPS, ALLG):
                emit(g // 2, g % 2)

        with nc.Block() as block:
            @block.sync
            def _(sp):
                def load(i, k):
                    g = 2 * i + k
                    residual = isinstance(g, int) and g >= GROUPS
                    if late(g):
                        beside(sp, m)
                        sp.wait_ge(fwd_ready, g - 1)
                    load_steps(nc, sp, m, i, k, [(m.meta[:, 2 * HEADS:MW], ends[:, k, :, :]), (m.dst, dstR[:, k, :, :]),
                                                 (m.src, srcR[:, k, :, :]), (m.ea, ea[:, k, :, :])],
                               rest[g - GROUPS] if residual else main[k], residual)

                all_groups(sp, load)

            @block.gpsimd
            def _(pool):
                def gather(g, k, s):
                    if late(g) or g:
                        beside(pool, m)
                        pool.wait_ge(got[s], 16 * (g + GROUPS))
                    nc.gpsimd.indirect_dma_start(got_rows[:, k, s, :], None, m.X1, bass.IndirectOffsetOnAxis(ap=idx[k][:, s:s + 1], axis=0)).then_inc(got[s], 16)

                def scatter(after, k, s):
                    if s % QUAD == 0:
                        beside(pool, m)
                        pool.wait_ge(merged_ready[s // QUAD], after)
                    if s >= TABLES:
                        beside(pool, m)
                        pool.wait_ge(put[s - TABLES], 16 * after)
                    elif late(after):
                        beside(pool, m)
                        pool.wait_ge(put[s - TABLES + G], 16 * after - 16)
                    nc.gpsimd.indirect_dma_start(m.table[s % TABLES], bass.IndirectOffsetOnAxis(ap=sidx[k][:, s:s + 1], axis=0), merged[:, k, s, :], None,
                                                 compute_op=ALU.add).then_inc(put[s], 16)

                def work(i, k):
                    g = 2 * i + k
                    pool.wait_ge(idx_ready, g + 1)
                    pool.wait_ge(sidx_ready, g)
                    pool.wait_ge(got[0], 16 * g)
                    pool.wait_ge(got[0], 16 * (g + GROUPS))
                    if late(g):
                        pool.wait_ge(agg_psum, QUADS * (g - 1))
                        pool.wait_ge(put[G - TABLES], 16 * g - 16)
                        pool.wait_ge(taken, g - 1)
                    take_waits(nc, m, taken)
                    for s in range(G):
                        gather(g, k, s)
                        scatter(g, 1 - k, s)

                pool.wait_ge(idx_ready, 1)
                for s in range(G):
                    gather(0, 0, s)
                work(0, 1)
                with pool.Fori(1, GROUPS // 2) as i:
                    for k in range(2):
                        work(i, k)
                for g in range(GROUPS // 2 * 2, ALLG):
                    work(g // 2, g % 2)
                pool.wait_ge(sidx_ready, ALLG)
                for s in range(G):
                    scatter(ALLG, (ALLG - 1) % 2, s)
                scattered(pool, ALLG - 1)

            @block.scalar
            def _(act):
                def index(i, k):
                    g = 2 * i + k
                    arrived(act, main, rest, i, k, 4)
                    if late(g):
                        gathered(act, g - 2)
                    nc.scalar.copy(idx[k][:, :], ends[:, k, :, 1]).then_inc(idx_ready, 1)

                def work(i, k):
                    g = 2 * i + k
                    for q in range(QUADS):
                        if q == 0 and late(g):
                            scattered(act, g - 2)
                        act.wait_ge(merged_psum, QUADS * g + q + 1)
                        nc.scalar.copy(merged[:, k, QUAD * q:QUAD * (q + 1), :], as_quad(bank[6 + q % 2])).then_inc(merged_ready[q], 1)

                index(0, 0)
                index(0, 1)
                work(0, 0)
                with act.Fori(1, GROUPS // 2) as i:
                    index(i, 0)
                    work(i - 1, 1)
                    index(i, 1)
                    work(i, 0)
                for g in range(GROUPS // 2 * 2, ALLG):
                    index(g // 2, g % 2)
                    work((g - 1) // 2, (g - 1) % 2)
                work((ALLG - 1) // 2, (ALLG - 1) % 2)

            @block.vector
            def _(dve):
                v = nc.vector
                v.memset(m.acc1[:, :, :], 0.0).then_inc(chain, 1)
                LINKS = 3

                def work(i, k):
                    g = 2 * i + k
                    arrived(dve, main, rest, i, k, 4)
                    if late(g):
                        dve.wait_ge(agg_psum, QUADS * (g - 1))
                    v.tensor_tensor(rel[:, k, :], ends[:, k, :, 0], m.baseB[:, bass.ds(G * g, G)], ALU.subtract).then_inc(chain, 1)
                    dve.wait_ge(chain, LINKS * g + 2)
                    v.tensor_tensor(O[:, k, :, :], iota.unsqueeze(1).to_broadcast([P, G, P]), rel[:, k, :].unsqueeze(2).to_broadcast([P, G, P]), ALU.is_equal).then_inc(O_ready, 1)
                    if late(g) or g:
                        dve.wait_ge(spread_done, QUADS * g)
                        dve.wait_ge(merged_psum, QUADS * g)
                    v.tensor_tensor(OT[:, :, :], dstR[:, k, :, :], m.nodeB[:, bass.ds(G * g, G)].unsqueeze(2).to_broadcast([P, G, P]), ALU.is_equal).then_inc(OT_ready, 1)
                    v.tensor_tensor(same[:, :, :], srcR[:, k, :, :], ends[:, k, :, 1:2].to_broadcast([P, G, P]), ALU.is_equal).then_inc(same_ready, 1)
                    dve.wait_ge(rank_psum, g + 1)
                    v.tensor_scalar(far[:, :], ends[:, k, :, 1], -1.0, C[:, C_DUMMY:C_DUMMY + 1], ALU.mult, ALU.add)
                    v.tensor_scalar(dup[:, :], bank[5][:, 0:G], C[:, C_THR:C_THR + 1], None, ALU.is_gt).then_inc(chain, 1)
                    dve.wait_ge(chain, LINKS * g + 3)
                    v.tensor_tensor(far[:, :], far[:, :], dup[:, :], ALU.mult).then_inc(chain, 1)
                    dve.wait_ge(chain, LINKS * g + 4)
                    if late(g):
                        scattered(dve, g - 2)
                    v.tensor_tensor(sidx[k][:, :], far[:, :], ends[:, k, :, 1], ALU.add).then_inc(sidx_ready, 1)
                    dve.wait_ge(sidx_ready, g + 1)
                    for q in range(QUADS):
                        dve.wait_ge(spread_done, QUADS * g + q + 1)
                        v.tensor_tensor(quad_of(back, q), ea[:, k, QUAD * q:QUAD * (q + 1), :], as_quad(bank[q % 2]), ALU.mult).then_inc(back_ready, 1)
                    gathered(dve, g)
                    v.tensor_tensor(got_rows[:, k, :, :], got_rows[:, k, :, :], ea[:, k, :, :], ALU.mult).then_inc(fwd_ready, 1)
                    for s in range(G):
                        if s % QUAD == 0:
                            blocks = windows(nc, dve, m, g, s // QUAD)
                        b = blocks[s % QUAD]
                        if s or late(g) or g:
                            dve.wait_ge(added, G * g + s)
                        if s % QUAD == 0:
                            dve.wait_ge(agg_psum, QUADS * g + s // QUAD + 1)
                        a = m.acc1[:, bass.ds(b, 1), :].rearrange("p b f -> p (b f)")
                        v.tensor_tensor(a, a, bank[2 + s // QUAD % 3][:, s % QUAD * P:(s % QUAD + 1) * P], ALU.add).then_inc(added, 1)

                all_groups(dve, work)

            @block.tensor
            def _(pe):
                def work(i, k):
                    g = 2 * i + k
                    pe.wait_ge(OT_ready, g + 1)

                    def spread(q, blocks):
                        if late(g) or g or q > 1:
                            pe.wait_ge(back_ready, QUADS * g + q - 1)
                        for u in range(QUAD):
                            last = nc.tensor.matmul(bank[q % 2][:, u * P:(u + 1) * P], OT[:, QUAD * q + u, :],
                                                    m.x1[:, bass.ds(blocks[u], 1), :].rearrange("p b f -> p (b f)"), start=True, stop=True)
                        last.then_inc(spread_done, 1)

                    spread(0, windows(nc, pe, m, g, 0))
                    pe.wait_ge(same_ready, g + 1)
                    if late(g) or g:
                        pe.wait_ge(sidx_ready, g)
                    for s in range(G):
                        last = nc.tensor.matmul(bank[5][:, s:s + 1], same[:, s, :], C[:, C_W3:C_W3 + 1], start=True, stop=True)
                    last.then_inc(rank_psum, 1)
                    for q in range(1, QUADS):
                        spread(q, windows(nc, pe, m, g, q))
                    for q in range(QUADS):
                        pe.wait_ge(back_ready, QUADS * g + q + 1)
                        if q > 1:
                            pe.wait_ge(merged_ready[q - 2], g + 1)
                        elif late(g) or g:
                            pe.wait_ge(merged_ready[q + 2], g)
                        for u in range(QUAD):
                            s = QUAD * q + u
                            last = nc.tensor.matmul(bank[6 + q % 2][:, u * P:(u + 1) * P], same[:, s, :], back[:, s, :], start=True, stop=True)
                        last.then_inc(merged_psum, 1)
                    pe.wait_ge(fwd_ready, g + 1)
                    for q in range(QUADS):
                        if q == QUADS - 1:
                            pe.wait_ge(added, G * g + QUAD)
                        elif late(g) or g:
                            pe.wait_ge(added, G * g)
                        for u in range(QUAD):
                            s = QUAD * q + u
                            last = nc.tensor.matmul(bank[2 + q % 3][:, u * P:(u + 1) * P], O[:, k, s, :], got_rows[:, k, s, :], start=True, stop=True)
                        last.then_inc(agg_psum, 1)

                all_groups(pe, work)


def gnn(nc, x, src, dst, ea, ea16, W_node, W_edge, attn, const, out, upto=99):
    m = Memory()
    m.x, m.src, m.dst, m.ea, m.ea16 = x, src, dst, ea, ea16
    m.W_node, m.W_edge, m.attn, m.in_const, m.out = W_node, W_edge, attn, const, out
    dram = lambda name, shape: nc.dram_tensor(name, shape, F32, kind="Internal").ap()
    m.H, m.X1 = dram("h_rows", (NODES, HW)), dram("x1_rows", (NODES, FEAT))
    m.Hs, m.meta = dram("h_of_src", (EDGES, FEAT)), dram("edge_rows", (EDGES, MW))
    m.table = [dram(f"table{t}", (TROWS, FEAT)) for t in range(TABLES)]
    m.tips, m.carries = dram("tips_d", (P, 2)), dram("carries_d", (P, 2))
    with ExitStack() as ctx:
        sb = lambda name, shape, dt=F32: ctx.enter_context(nc.sbuf_tensor(name, shape, dt))
        m.bank = [ctx.enter_context(nc.psum_tensor(f"bank{n}", [P, 512], F32)) for n in range(8)]
        m.begun = ctx.enter_context(nc.semaphore("begun"))
        m.got = [ctx.enter_context(nc.semaphore(f"got{s}")) for s in range(G)]
        m.norm = {n: ctx.enter_context(nc.semaphore(n)) for n in ("norm_chain", "dev_ready", "normed", "eps_ready")}
        m.const = sb("const", [P, C_WIDTH])
        m.spare = sb("spare", [P, 4])
        m.wtab, m.ttab = sb("wtab", [1, STEPS // QUAD], I32), sb("ttab", [1, RES], I32)
        m.baseB = sb("baseB", [P, STEPS])
        m.nodeB = sb("nodeB", [P, STEPS])
        m.wblock = sb("wblock", [P, 2, CHUNKS, HEADS])
        m.dstT, m.srcT = sb("dstT", [P, TILES]), sb("srcT", [P, TILES])
        m.sdst = sb("sdst", [P, BLOCKS, HEADS])
        m.acc = sb("acc", [P, BLOCKS, HW])
        m.acc_flat = m.acc[:, :, :].rearrange("p b f -> p (b f)")
        with ExitStack() as early:
            m.scratch = early.enter_context(nc.sbuf_tensor("scratch", [P, TILES // 2], F32))
            phase_nodes(nc, m)
        with ExitStack() as early:
            aT = early.enter_context(nc.sbuf_tensor("aT", [P, CHUNK], F32))
            phase_scores(nc, m, aT)
            amax = early.enter_context(nc.sbuf_tensor("amax", [P, CHUNK], F32))
            phase_scan(nc, m, aT, amax)
            phase_meta(nc, m, aT, amax)
        m.x1 = sb("x1", [P, BLOCKS, FEAT])
        with ExitStack() as first_layer:
            m.acc_odd = first_layer.enter_context(nc.sbuf_tensor("acc_odd", [P, BLOCKS, HW], F32))
            phase_attend(nc, m)
            phase_norm(nc, m, last_layer=False)
        m.acc1 = m.acc_flat[:, 0:BLOCKS * FEAT].rearrange("p (b f) -> p b f", b=BLOCKS)
        phase_messages(nc, m)
        phase_norm(nc, m, last_layer=True)


def kernel(x, src, dst, edge_attr_128, edge_attr_16, L0_gnn_W_node, L0_gnn_W_edge, L0_gnn_attn_vec):
    import concourse.bacc as bacc
    from concourse.bass_utils import run_bass_kernel_spmd

    def rows(a, n):
        a = np.asarray(a)
        return np.concatenate([a, np.zeros((n - a.shape[0],) + a.shape[1:], a.dtype)])

    def indices(a):
        a = np.asarray(a)
        return np.concatenate([a, np.full(EDGES - E_REAL, NODES - 1, a.dtype)])

    attn = np.asarray(L0_gnn_attn_vec).reshape(HEADS, 3, HDIM).transpose(0, 2, 1).reshape(P, 3)
    arrays = {
        "x": rows(x, NODES), "src": indices(src), "dst": indices(dst),
        "ea": rows(edge_attr_128, EDGES), "ea16": rows(edge_attr_16, EDGES),
        "W_node": np.ascontiguousarray(L0_gnn_W_node), "W_edge": np.ascontiguousarray(L0_gnn_W_edge),
        "attn": np.ascontiguousarray(attn), "const": shape_constants(),
    }
    nc = bacc.Bacc("TRN2", target_bir_lowering=False, num_devices=1)
    args = {n: nc.dram_tensor("in_" + n, a.shape, mybir.dt.from_np(a.dtype), kind="ExternalInput").ap() for n, a in arrays.items()}
    out = nc.dram_tensor("out_rows", (N_REAL, FEAT), F32, kind="ExternalOutput").ap()
    gnn(nc, out=out, **args)
    r = run_bass_kernel_spmd(nc, [{"in_" + n: a for n, a in arrays.items()}], core_ids=[0])
    return r.results[0]["out_rows"]
```

```python
from contextlib import ExitStack

import numpy as np

import concourse.bass as bass
from concourse import mybir

F32 = mybir.dt.float32
I32 = mybir.dt.int32
U32 = mybir.dt.uint32
ALU = mybir.AluOpType
ACT = mybir.ActivationFunctionType
AX = mybir.AxisListType

P = 128
N_REAL, E_REAL = 6250, 100000
BLOCKS = -(-N_REAL // P)
NODES = BLOCKS * P
HEADS, HDIM, FEAT, EDIM = 8, 16, 128, 16
CHUNKS = P // HEADS
GROUPS = -(-E_REAL // (CHUNKS * P))
EDGES = GROUPS * CHUNKS * P
TILES = EDGES // P
DG = 8
DOMAINS = GROUPS // DG
FULL = DOMAINS * DG
REST_G = GROUPS - FULL
FULL_EDGES = FULL * CHUNKS * P
DOMAIN = DG * CHUNKS
CHUNK = DG * P
assert REST_G == 1
RES = BLOCKS - 1
RGROUPS = RES // CHUNKS
STEPS = TILES + RES
ALLG = GROUPS + RGROUPS
G = CHUNKS
SLOPE, EPS_DEN, EPS_LN = 0.2, 1e-9, 1e-5
NEG = -1.0e30
FAR = 1.0e5
HW = FEAT + HEADS
MW = 2 * HEADS + 2
NODE_STEP = 7
NODE_ITERS = BLOCKS // NODE_STEP
NORM_SEMAPHORES = ("norm_chain", "dev_ready", "normed", "eps_ready", "norm_out", "norm_sum", "norm_merged", "exp_ready",
                   "sum_done", "min_ready", "norm_in0", "norm_in1")
TABLES = 4
TROWS = NODES + P
WORD_BITS = 6
WORD = 1 << WORD_BITS
TILE_BITS = 10
TILE_WORD = 1 << TILE_BITS
QUADS, QUAD = 4, 4

C_ID, C_IOTA, C_HEAD, C_BD = 0, P, 2 * P, 2 * P + HEADS
C_W3, C_THR = C_BD + 2 * CHUNKS, C_BD + 2 * CHUNKS + 1
C_DUMMY, C_BLK, C_ONE = C_THR + 1, C_THR + 2, C_THR + 3
C_WIDTH = C_ONE + P


def shape_constants():
    p = np.arange(P, dtype=np.float32)
    c = np.zeros((P, C_WIDTH), np.float32)
    c[:, C_ID:C_ID + P] = np.eye(P, dtype=np.float32)
    c[:, C_IOTA:C_IOTA + P] = p
    for lane in range(P):
        c[lane, C_HEAD + lane // HDIM] = 1.0
        for half in range(2):
            c[lane, C_BD + half * CHUNKS + lane // EDIM + 8 * half] = 1.0
    c[:, C_W3] = np.float32(3.0) ** (64 - p)
    c[:, C_THR] = np.float32(1.75) * c[:, C_W3]
    c[:, C_DUMMY] = NODES + p
    c[:, C_BLK] = P * (p + 1)
    c[:, C_ONE:] = 1.0
    return c


class Chain:

    def __init__(self, engine, sem):
        self.engine, self.sem, self.n = engine, sem, 0

    def __call__(self, instruction):
        self.n += 1
        instruction.then_inc(self.sem, 1)
        self.engine.wait_ge(self.sem, self.n)


class Memory:
    pass


class Edges:
    pass


def late(g):
    return not (isinstance(g, int) and g < 2)


def beside(engine, m):
    engine.wait_ge(m.begun, 1)


def take_waits(nc, m, sem):
    nc.gpsimd.tensor_tensor(m.spare[:, 0:1], m.spare[:, 1:2], m.spare[:, 2:3], ALU.add).then_inc(sem, 1)


def group_of(a, g, spread=False, j=None):
    n = FULL_EDGES
    if isinstance(g, int) and (g * DG if j is not None else g) >= FULL:
        return a[n:].rearrange("(c p) -> c p", p=P) if spread else a[n:].rearrange("(c p) f -> p c f", p=P)
    if j is None:
        d, j = g // DG, g % DG
    else:
        d = g
    kind = dict(c=CHUNKS, j=DG, p=P)
    if spread:
        v = a[0:n].rearrange("(d c j p) -> d j c p", **kind)
        one = "a b c p -> (a b c) p"
    else:
        v = a[0:n].rearrange("(d c j p) f -> d j p c f", **kind)
        one = "a b p c f -> (a b p) c f"
    if isinstance(d, int):
        return v[d, j]
    return v[bass.ds(d, 1), bass.ds(j, 1)].rearrange(one)


def windows(nc, engine, m, g, q):
    word = engine.value_load(m.wtab[0:1, bass.ds(QUADS * g + q, 1)], min_val=0, max_val=WORD ** QUAD - 1)
    return [nc.s_assert_within(engine.snap((word >> u * WORD_BITS) & (WORD - 1)), 0, BLOCKS - 1,
                               skip_runtime_bounds_check_because="each field is a block of nodes") for u in range(QUAD)]


def pairs(engine, groups, emit):
    for k in range(2):
        emit(0, k)
    with engine.Fori(1, groups // 2) as i:
        for k in range(2):
            emit(i, k)
    for g in range(groups // 2 * 2, groups):
        emit(g // 2, g % 2)


def phase_order(nc, m):
    with ExitStack() as ctx:
        sb = lambda name, shape, dt=F32: ctx.enter_context(nc.sbuf_tensor(name, shape, dt))
        sem = lambda name: ctx.enter_context(nc.semaphore(name))
        ROW = EDGES // P
        line = sb("line", [P, ROW + 1], I32)
        falls, count = sb("falls", [P, ROW]), sb("count", [P, 1])
        line_in, told, summed = sem("line_in"), sem("told"), sem("falls_summed")
        C = m.const
        dv = m.given.dst.rearrange("(p r) -> p r", p=P)

        with nc.Block() as block:
            @block.sync
            def _(sp):
                sp.dma_start(C[:, :], m.in_const).then_inc(m.c_in, 16)
                sp.dma_start(line[:, 0:ROW], dv).then_inc(line_in, 16)
                with nc.allow_non_contiguous_dma(reason="one edge for each partition"):
                    sp.dma_start(line[0:P - 1, ROW:ROW + 1], dv[1:P, 0:1]).then_inc(line_in, 16)
                sp.dma_start(line[P - 1:P, ROW:ROW + 1], dv[P - 1:P, ROW - 1:ROW]).then_inc(line_in, 16)

            @block.vector
            def _(dve):
                link = Chain(dve, told)
                dve.wait_ge(line_in, 48)
                link(nc.vector.memset(m.spare[:, :], 0.0))
                link(nc.vector.tensor_tensor(falls[:, :], line[:, 1:ROW + 1], line[:, 0:ROW], ALU.is_lt))
                link(nc.vector.tensor_reduce(count[:, :], falls[:, :], AX.X, ALU.add))
                dve.wait_ge(summed, 1)
                link(nc.vector.tensor_scalar(m.unsorted[:, :], m.bank[0][0:1, 0:1], 0.5, None, ALU.is_gt))

            @block.tensor
            def _(pe):
                pe.wait_ge(m.c_in, 16)
                pe.wait_ge(told, 3)
                nc.tensor.matmul(m.bank[0][0:1, 0:1], count[:, :], C[:, C_ONE:C_ONE + 1], start=True, stop=True).then_inc(summed, 1)

    with ExitStack() as ctx:
        sb = lambda name, shape, dt=F32: ctx.enter_context(nc.sbuf_tensor(name, shape, dt))
        sem = lambda name: ctx.enter_context(nc.semaphore(name))
        lane = sb("lane", [P, 1])
        below = sb("below", [P, P])
        above = sb("above", [P, P])
        zeros = sb("zeros", [P, TROWS // P])
        d_col, s_col, d_row = sb("d_col", [P, 1], I32), sb("s_col", [P, 1], I32), sb("d_row", [P, P], I32)
        d_f, old, new, mine, total, spot = (sb(n, [P, 1]) for n in ("d_f", "old", "new", "mine", "total", "spot"))
        alike, before = sb("alike", [P, P]), sb("before", [P, P])
        from_i, to_i = sb("from_i", [P, 1], U32), sb("to_i", [P, 1], U32)
        rank = sb("rank", [P, TILES])
        hist, cum, ones = (sb(n, [P, BLOCKS]) for n in ("hist", "cum", "ones"))
        ea_t, ea16_t = sb("ea_t", [P, FEAT]), sb("ea16_t", [P, EDIM])
        loaded, turn, fetched, stored, to_pool, link_sem, offsets = (
            sem(n) for n in ("o_loaded", "o_turn", "o_fetched", "o_stored", "o_pool", "o_link", "o_offsets"))
        C = m.const
        g, o = m.given, m.ordered
        hist_rows = m.hist.rearrange("(p r) f -> p (r f)", p=P)
        node_rows = m.hist[0:NODES, :].rearrange("(p r) f -> p (r f)", p=P)
        tile = lambda a, t: a.rearrange("(t p) f -> t p f", p=P)[bass.ds(t, 1)].rearrange("a p f -> (a p) f")
        as_rows = lambda a: a.rearrange("(e o) -> e o", o=1)
        PASS1, PASS2 = 2, 4
        LINKS1, LINKS2 = 9, 2
        SETUP, MIDDLE = 6, 6

        def is_unsorted(engine):
            return engine.value_load(m.unsorted[0:1, 0:1], min_val=0, max_val=1) > 0

        with nc.Block() as block:
            @block.sync
            def _(sp):
                with sp.If(is_unsorted(sp)):
                    sp.wait_ge(link_sem, SETUP)
                    sp.dma_start(hist_rows, zeros[:, :]).then_inc(offsets, 16)
                    sp.wait_ge(offsets, 16)
                    with sp.Fori(0, TILES) as t:
                        sp.wait_ge(turn, t + 1)
                        sp.dma_start(d_col[:, :], tile(as_rows(g.dst), t)).then_inc(loaded, 16)
                        sp.dma_start(d_row[:, :], g.dst.rearrange("(t p) -> t p", p=P)[bass.ds(t, 1)].to_broadcast([P, P])).then_inc(loaded, 16)
                    sp.wait_ge(turn, TILES + 1)
                    sp.dma_start(hist[:, :], node_rows).then_inc(offsets, 16)
                    sp.wait_ge(link_sem, SETUP + LINKS1 * TILES + MIDDLE)
                    sp.dma_start(node_rows, hist[:, :]).then_inc(offsets, 16)
                    sp.wait_ge(offsets, 48)
                    with sp.Fori(0, TILES) as t:
                        sp.wait_ge(turn, t + TILES + 1)
                        sp.dma_start(d_col[:, :], tile(as_rows(g.dst), t)).then_inc(loaded, 16)
                        sp.dma_start(s_col[:, :], tile(as_rows(g.src), t)).then_inc(loaded, 16)
                        sp.dma_start(ea_t[:, :], tile(g.ea, t)).then_inc(loaded, 16)
                        sp.dma_start(ea16_t[:, :], tile(g.ea16, t)).then_inc(loaded, 16)

            @block.gpsimd
            def _(pool):
                at = bass.IndirectOffsetOnAxis

                def after_vector(n):
                    pool.wait_ge(to_pool, n)
                    pool.wait_ge(taken, n)
                    take_waits(nc, m, taken)

                taken = m.taken
                with pool.If(is_unsorted(pool)):
                    take_waits(nc, m, taken)
                    pool.wait_ge(offsets, 16)
                    with pool.Fori(0, TILES) as t:
                        after_vector(2 * t + 1)
                        nc.gpsimd.indirect_dma_start(old[:, :], None, m.hist, at(ap=from_i[:, :], axis=0)).then_inc(fetched, 16)
                        after_vector(2 * t + 2)
                        nc.gpsimd.indirect_dma_start(m.hist, at(ap=to_i[:, :], axis=0), new[:, :], None).then_inc(stored, 16)
                        pool.wait_ge(stored, 16 * t + 16)
                        pool.wait_ge(taken, 2 * t + 3)
                        nc.gpsimd.tensor_tensor(m.spare[:, 3:4], m.spare[:, 1:2], m.spare[:, 2:3], ALU.add).then_inc(turn, 1)
                    with pool.Fori(0, TILES) as t:
                        after_vector(2 * t + 2 * TILES + 1)
                        nc.gpsimd.indirect_dma_start(old[:, :], None, m.hist, at(ap=from_i[:, :], axis=0)).then_inc(fetched, 16)
                        after_vector(2 * t + 2 * TILES + 2)
                        for rows, data in ((o.ea, ea_t), (o.ea16, ea16_t), (as_rows(o.dst), d_col), (as_rows(o.src), s_col)):
                            nc.gpsimd.indirect_dma_start(rows, at(ap=to_i[:, :], axis=0), data[:, :], None).then_inc(stored, 16)
                        pool.wait_ge(stored, 16 * TILES + 64 * t + 64)
                        pool.wait_ge(turn, t + TILES + 1)
                        nc.gpsimd.tensor_tensor(m.spare[:, 3:4], m.spare[:, 1:2], m.spare[:, 2:3], ALU.add).then_inc(turn, 1)

            @block.vector
            def _(dve):
                v = nc.vector
                with dve.If(is_unsorted(dve)):
                    link = Chain(dve, link_sem)
                    link(v.tensor_scalar(lane[:, :], C[:, C_DUMMY:C_DUMMY + 1], float(NODES), None, ALU.subtract))
                    link(v.tensor_scalar(below[:, :], C[:, C_IOTA:C_IOTA + P], lane[:, :], None, ALU.is_lt))
                    link(v.tensor_scalar(above[:, :], C[:, C_IOTA:C_IOTA + P], lane[:, :], None, ALU.is_gt))
                    link(v.memset(zeros[:, :], 0.0))
                    link(v.memset(ones[:, :], 1.0))
                    link(v.memset(rank[:, :], 0.0))
                    assert link.n == SETUP
                    v.memset(cum[:, :], 0.0).then_inc(turn, 1)

                    def steps(base):
                        done = [0]

                        def then(instruction):
                            done[0] += 1
                            instruction.then_inc(link_sem, 1)
                            dve.wait_ge(link_sem, base + done[0])
                        return then

                    with dve.Fori(0, TILES) as t:
                        then = steps(LINKS1 * t + SETUP)
                        dve.wait_ge(loaded, 16 * PASS1 * (t + 1))
                        then(v.tensor_copy(d_f[:, :], d_col[:, :]))
                        v.tensor_copy(from_i[:, :], d_f[:, :]).then_inc(to_pool, 1)
                        then(v.tensor_tensor(alike[:, :], d_row[:, :], d_f[:, :].to_broadcast([P, P]), ALU.is_equal))
                        then(v.tensor_tensor(before[:, :], alike[:, :], below[:, :], ALU.mult))
                        then(v.tensor_reduce(mine[:, :], before[:, :], AX.X, ALU.add))
                        then(v.tensor_reduce(total[:, :], alike[:, :], AX.X, ALU.add))
                        then(v.tensor_scalar(spot[:, :], mine[:, :], 0.5, None, ALU.is_gt))
                        then(v.scalar_tensor_tensor(before[:, 0:1], d_f[:, :], -1.0, C[:, C_DUMMY:C_DUMMY + 1], ALU.mult, ALU.add))
                        then(v.tensor_tensor(spot[:, :], spot[:, :], before[:, 0:1], ALU.mult))
                        dve.wait_ge(fetched, 16 * (t + 1))
                        v.tensor_tensor(to_i[:, :], spot[:, :], d_f[:, :], ALU.add)
                        v.tensor_tensor(new[:, :], old[:, :], total[:, :], ALU.add).then_inc(to_pool, 1)
                        then(v.tensor_tensor(rank[:, bass.ds(t, 1)], old[:, :], mine[:, :], ALU.add))

                    link.n = SETUP + LINKS1 * TILES
                    dve.wait_ge(offsets, 32)
                    link(v.tensor_tensor_scan(cum[:, :], ones[:, :], hist[:, :], 0.0, ALU.mult, ALU.add))
                    link(v.tensor_copy(total[:, :], cum[:, BLOCKS - 1:BLOCKS]))
                    dve.wait_ge(m.placed, 1)
                    link(v.tensor_copy(spot[:, :], m.bank[0][:, 0:1]))
                    link(v.tensor_tensor(cum[:, :], cum[:, :], hist[:, :], ALU.subtract))
                    link(v.tensor_scalar(hist[:, :], cum[:, :], spot[:, :], None, ALU.add))
                    link(v.memset(old[:, :], 0.0))
                    with dve.Fori(0, TILES) as t:
                        then = steps(LINKS2 * t + SETUP + LINKS1 * TILES + MIDDLE)
                        dve.wait_ge(loaded, 16 * PASS2 * t + 16 * (PASS1 * TILES + PASS2))
                        then(v.tensor_copy(d_f[:, :], d_col[:, :]))
                        v.tensor_copy(from_i[:, :], d_f[:, :]).then_inc(to_pool, 1)
                        dve.wait_ge(fetched, 16 * t + 16 * TILES + 16)
                        then(v.tensor_tensor(new[:, :], old[:, :], rank[:, bass.ds(t, 1)], ALU.add))
                        v.tensor_copy(to_i[:, :], new[:, :]).then_inc(to_pool, 1)

            @block.tensor
            def _(pe):
                with pe.If(is_unsorted(pe)):
                    pe.wait_ge(link_sem, SETUP + LINKS1 * TILES + 2)
                    nc.tensor.matmul(m.bank[0][:, 0:1], above[:, :], total[:, :], start=True, stop=True).then_inc(m.placed, 1)


def from_edges(sp, m, emit):
    unsorted = sp.value_load(m.unsorted[0:1, 0:1], min_val=0, max_val=1)
    with sp.If(unsorted > 0):
        emit(m.ordered)
    with sp.Else():
        emit(m.given)


def phase_nodes(nc, m):
    with ExitStack() as ctx:
        sb = lambda name, shape, dt=F32: ctx.enter_context(nc.sbuf_tensor(name, shape, dt))
        sem = lambda name: ctx.enter_context(nc.semaphore(name))
        wn, we, av = sb("wn", [P, P]), sb("we", [P, EDIM]), sb("av", [P, 3])
        amask = sb("amask", [P, 3, HEADS])
        waug = sb("waug", [P, FEAT + 2 * HEADS])
        wrep = sb("wrep", [P, HEADS, EDIM])
        wedge = sb("wedge", [P, HEADS])
        xs, xt = sb("xs", [P, 2, NODE_STEP, P]), sb("xt", [P, NODE_STEP, P])
        hrow = sb("hrow", [P, 2, NODE_STEP, HW])
        ii, ff = sb("ii", [P, 2, DOMAINS + 1, P], I32), sb("ff", [P, 2, DOMAINS + 1, P])
        assert DOMAIN == P and 2 * (DOMAINS + 1) <= 16
        first_t = sb("first_t", [1, TILES], I32)
        first_i, first_f = sb("first_i", [1, TILES], I32), sb("first_f", [1, TILES])
        block_i = sb("block_i", [1, TILES], I32)
        base = sb("base", [1, STEPS])
        block_f, word_f = sb("block_f", [1, STEPS]), sb("word_f", [1, STEPS // QUAD])
        cnt, crow, pair_f = sb("cnt", [RES, 3]), sb("crow", [1, 4, RES]), sb("pair_f", [1, RES // 2])
        w_in, i_in, f_in = (sem(n) for n in ("w_in", "i_in", "f_in"))
        x_in, h_out = [sem(f"x_in{k}") for k in range(2)], [sem(f"h_out{k}") for k in range(2)]
        chain, pe_w, pe_i, pe_f, pe_c, pe_b = (sem(n) for n in ("n_chain", "pe_w", "pe_i", "pe_f", "pe_c", "pe_b"))
        base_ready, waug_ready, xt_psum, xt_ready, h_psum, h_ready = (
            sem(n) for n in ("base_ready", "waug_ready", "xt_psum", "xt_ready", "h_psum", "h_ready"))
        amask_ready, ff_ready, first_ready, cnt_ready, idx_done = (
            sem(n) for n in ("amask_ready", "ff_ready", "first_ready", "cnt_ready", "idx_done"))
        C = m.const
        bank = m.bank
        ident = C[:, C_ID:C_ID + P]

        with nc.Block() as block:
            @block.sync
            def _(sp):
                sp.dma_start(wn[:, :], m.W_node).then_inc(w_in, 16)
                sp.dma_start(we[:, :], m.W_edge).then_inc(w_in, 16)
                sp.dma_start(av[:, :], m.attn).then_inc(w_in, 16)

                def load_indices(edges):
                    with nc.allow_non_contiguous_dma(reason="first edge of each tile"):
                        sp.dma_start(first_t[0:1, :], edges.dst.rearrange("(t e) -> e t", e=P)[0:1, :]).then_inc(f_in, 16)
                    for w, a in enumerate((edges.dst, edges.src)):
                        sp.dma_start(ii[:, w, 0:DOMAINS, :], a[0:FULL_EDGES].rearrange("(q r e) -> r q e", r=DOMAIN, e=P)).then_inc(i_in, 16)
                        sp.dma_start(ii[0:CHUNKS, w, DOMAINS, :], a[FULL_EDGES:].rearrange("(r e) -> r e", e=P)).then_inc(i_in, 16)

                from_edges(sp, m, load_indices)
                xv = m.x.rearrange("(b p) f -> p b f", p=P)
                hv = m.H.rearrange("(b p) f -> p b f", p=P)
                for k in range(2):
                    sp.dma_start(xs[:, k, :, :], xv[:, NODE_STEP * k:NODE_STEP * (k + 1), :]).then_inc(x_in[k], 16)

                def move(i, k):
                    n = 2 * i + k
                    sp.wait_ge(h_ready, n + 1)
                    sp.dma_start(hv[:, bass.ds(NODE_STEP * n, NODE_STEP), :], hrow[:, k, :, :]).then_inc(h_out[k], 16)
                    if not (isinstance(n, int) and n + 2 >= NODE_ITERS):
                        sp.dma_start(xs[:, k, :, :], xv[:, bass.ds(NODE_STEP * n + 2 * NODE_STEP, NODE_STEP), :]).then_inc(x_in[k], 16)

                for n in range(NODE_ITERS):
                    move(n // 2, n % 2)
                for k in range(2):
                    sp.wait_ge(h_out[k], 16 * ((NODE_ITERS + 1 - k) // 2))

            @block.vector
            def _(dve):
                link = Chain(dve, chain)
                nc.vector.memset(base[:, :], 0.0).then_inc(m.begun, 1)
                dve.wait_ge(m.c_in, 16)
                dve.wait_ge(w_in, 48)
                for w in range(3):
                    last = nc.vector.tensor_scalar(amask[:, w, :], C[:, C_HEAD:C_HEAD + HEADS], av[:, w:w + 1], None, ALU.mult)
                last.then_inc(amask_ready, 1)
                link(nc.vector.tensor_copy(wrep[:, :, :], we[:, :].unsqueeze(1).to_broadcast([P, HEADS, EDIM])))
                dve.wait_ge(f_in, 16)
                nc.vector.tensor_copy(first_i[0:1, 0:FULL * CHUNKS].rearrange("p (d j c) -> p d j c", j=DG, c=CHUNKS),
                                      first_t[0:1, 0:FULL * CHUNKS].rearrange("p (d c j) -> p d j c", j=DG, c=CHUNKS))
                link(nc.vector.tensor_copy(first_i[0:1, FULL * CHUNKS:], first_t[0:1, FULL * CHUNKS:]))
                link(nc.vector.tensor_scalar(block_i[:, :], first_i[:, :], 7, None, ALU.arith_shift_right))
                nc.vector.tensor_copy(block_f[0:1, 0:TILES], block_i[:, :])
                nc.vector.tensor_scalar(base[0:1, 0:TILES], block_i[:, :], float(P), None, ALU.mult)
                nc.vector.tensor_copy(first_f[:, :], first_i[:, :]).then_inc(first_ready, 1)
                dve.wait_ge(i_in, 64)
                nc.vector.tensor_copy(ff[:, :, 0:DOMAINS, :], ii[:, :, 0:DOMAINS, :])
                nc.vector.tensor_copy(ff[0:CHUNKS, :, DOMAINS, :], ii[0:CHUNKS, :, DOMAINS, :]).then_inc(ff_ready, 1)
                dve.wait_ge(pe_w, 1)
                nc.vector.tensor_copy(waug[:, 0:FEAT], bank[6][:, 0:FEAT])
                nc.vector.tensor_copy(waug[:, FEAT:], bank[6][:, FEAT:FEAT + 2 * HEADS]).then_inc(waug_ready, 1)
                link(nc.vector.tensor_copy(wedge[:, :], bank[6][:, 256:256 + HEADS]))
                for half in range(2):
                    nc.vector.tensor_tensor(m.wblock[:, half, :, :], wedge[:, :].unsqueeze(1).to_broadcast([P, CHUNKS, HEADS]),
                                            C[:, C_BD + half * CHUNKS:C_BD + (half + 1) * CHUNKS].unsqueeze(2).to_broadcast([P, CHUNKS, HEADS]),
                                            ALU.mult)
                dve.wait_ge(pe_i, 1)
                for w, cols in enumerate((m.dstT, m.srcT)):
                    for q in range(DOMAINS + 1):
                        n = w * (DOMAINS + 1) + q
                        tiles = DG if q < DOMAINS else REST_G
                        last = nc.vector.tensor_copy(cols[:, q * DOMAIN:q * DOMAIN + tiles * CHUNKS].rearrange("p (j c) -> p c j", c=CHUNKS),
                                                     bank[n // 4][:, n % 4 * P:n % 4 * P + tiles * CHUNKS].rearrange("p (c j) -> p c j", c=CHUNKS))
                last.then_inc(idx_done, 1)
                dve.wait_ge(pe_f, 1)
                half = TILES // 2
                for w in range(2):
                    last = nc.vector.tensor_scalar(m.scratch[0:RES, 0:half], bank[4 + w][0:RES, 0:half], C[0:RES, C_BLK:C_BLK + 1], 0.0,
                                                   ALU.is_lt, ALU.add, accum_out=cnt[:, w:w + 1])
                    link(last)
                nc.vector.tensor_tensor(cnt[:, 2:3], cnt[:, 0:1], cnt[:, 1:2], ALU.add).then_inc(cnt_ready, 1)
                dve.wait_ge(pe_c, 1)
                link(nc.vector.tensor_copy(crow[0:1, 0, :], bank[7][0:1, 0:RES]))
                link(nc.vector.tensor_scalar(crow[0:1, 1, :], crow[0:1, 0, :], -1.0, 0.0, ALU.add, ALU.max))
                tv = crow[0:1, 1, :].rearrange("p (w u) -> p u w", u=2)
                link(nc.vector.scalar_tensor_tensor(pair_f[:, :], tv[:, 1, :], float(TILE_WORD), tv[:, 0, :], ALU.mult, ALU.add))
                nc.vector.tensor_copy(m.ttab[0:1, :], pair_f[:, :])
                link(nc.vector.tensor_scalar(crow[0:1, 2, :], crow[0:1, 0, :], 0.5, FAR, ALU.is_lt, ALU.mult))
                link(nc.vector.tensor_scalar(crow[0:1, 3, :], C[0:1, C_IOTA:C_IOTA + RES], 1.0, None, ALU.add))
                link(nc.vector.tensor_copy(block_f[0:1, TILES:STEPS], crow[0:1, 3, :]))
                bv = block_f[0:1, :].rearrange("p (w u) -> p u w", u=QUAD)
                link(nc.vector.tensor_copy(word_f[:, :], bv[:, QUAD - 1, :]))
                for u in range(QUAD - 2, -1, -1):
                    link(nc.vector.scalar_tensor_tensor(word_f[:, :], word_f[:, :], float(WORD), bv[:, u, :], ALU.mult, ALU.add))
                nc.vector.tensor_copy(m.wtab[:, :], word_f[:, :])
                nc.vector.scalar_tensor_tensor(base[0:1, TILES:STEPS], crow[0:1, 3, :], float(P), crow[0:1, 2, :],
                                               ALU.mult, ALU.add).then_inc(base_ready, 1)
                dve.wait_ge(pe_b, 1)
                for w in range(2):
                    last = nc.vector.tensor_copy(m.baseB[:, w * STEPS // 2:(w + 1) * STEPS // 2], bank[6 + w][:, 0:STEPS // 2])
                link(last)
                nc.vector.tensor_scalar(m.nodeB[:, :], m.baseB[:, :], C[:, C_DUMMY:C_DUMMY + 1], float(NODES), ALU.add, ALU.subtract)
                nc.vector.memset(m.acc_flat[:, :], 0.0)
                def node_rows(i, k):
                    g = 2 * i + k
                    dve.wait_ge(h_psum, g + 1)
                    if late(g):
                        dve.wait_ge(h_out[k], 16 * i)
                    for n in range(4):
                        w = min(2, NODE_STEP - 2 * n)
                        hp = bank[2 + n][:, 0:512].rearrange("p (s f) -> p s f", s=2)
                        nc.vector.tensor_copy(hrow[:, k, 2 * n:2 * n + w, :], hp[:, 0:w, 0:HW])
                        last = nc.vector.tensor_copy(m.sdst[:, bass.ds(NODE_STEP * g + 2 * n, w), 0:HEADS], hp[:, 0:w, HW:HW + HEADS])
                    last.then_inc(h_ready, 1)

                pairs(dve, NODE_ITERS, node_rows)

            @block.scalar
            def _(act):
                def copy_xt(i, k):
                    g = 2 * i + k
                    act.wait_ge(xt_psum, g + 1)
                    if late(g) or g:
                        act.wait_ge(h_psum, g)
                    nc.scalar.copy(xt[:, 0:4, :], bank[0][:, :].rearrange("p (s f) -> p s f", s=4))
                    nc.scalar.copy(xt[:, 4:7, :], bank[1][:, 0:3 * P].rearrange("p (s f) -> p s f", s=3)).then_inc(xt_ready, 1)

                pairs(act, NODE_ITERS, copy_xt)

            @block.tensor
            def _(pe):
                pe.wait_ge(amask_ready, 1)
                pe.wait_ge(chain, 1)
                nc.tensor.transpose(bank[6][:, 0:P], wn[:, :], ident)
                nc.tensor.matmul(bank[6][:, FEAT:FEAT + 2 * HEADS], wn[:, :], amask[:, 0:2, :].rearrange("p a h -> p (a h)"), start=True, stop=True)
                nc.tensor.matmul(bank[6][:, 256:256 + HEADS], wrep[:, :, :].rearrange("p a i -> p (a i)"), amask[:, 2, :], start=True, stop=True).then_inc(pe_w, 1)
                pe.wait_ge(ff_ready, 1)
                for w in range(2):
                    for q in range(DOMAINS + 1):
                        n = w * (DOMAINS + 1) + q
                        k = DOMAIN if q < DOMAINS else CHUNKS
                        last = nc.tensor.transpose(bank[n // 4][:, n % 4 * P:n % 4 * P + k], ff[0:k, w, q, :], C[0:k, C_ID:C_ID + k])
                last.then_inc(pe_i, 1)
                pe.wait_ge(first_ready, 1)
                for w in range(2):
                    last = nc.tensor.matmul(bank[4 + w][0:RES, 0:TILES // 2], C[0:1, C_ONE:C_ONE + RES],
                                            first_f[0:1, w * TILES // 2:(w + 1) * TILES // 2], start=True, stop=True)
                last.then_inc(pe_f, 1)
                pe.wait_ge(cnt_ready, 1)
                nc.tensor.matmul(bank[7][0:1, 0:RES], cnt[:, 2:3], C[0:RES, C_ID:C_ID + RES], start=True, stop=True).then_inc(pe_c, 1)
                pe.wait_ge(base_ready, 1)
                pe.wait_ge(waug_ready, 1)
                for w in range(2):
                    last = nc.tensor.matmul(bank[6 + w][:, 0:STEPS // 2], C[0:1, C_ONE:C_ONE + P],
                                            base[0:1, w * STEPS // 2:(w + 1) * STEPS // 2], start=True, stop=True)
                last.then_inc(pe_b, 1)
                pe.wait_ge(idx_done, 1)
                def turn(i, k):
                    g = 2 * i + k
                    pe.wait_ge(x_in[k], 16 * i + 16)
                    if late(g) or g:
                        pe.wait_ge(xt_ready, g)
                    for u in range(NODE_STEP):
                        last = nc.tensor.transpose(bank[u // 4][:, u % 4 * P:(u % 4 + 1) * P], xs[:, k, u, :], ident)
                    last.then_inc(xt_psum, 1)

                def project(i, k):
                    g = 2 * i + k
                    turn(i, k)
                    pe.wait_ge(xt_ready, g + 1)
                    if late(g) or g:
                        pe.wait_ge(h_ready, g)
                    for u in range(NODE_STEP):
                        last = nc.tensor.matmul(bank[2 + u // 2][:, u % 2 * 256:u % 2 * 256 + HW + HEADS], xt[:, u, :], waug[:, :], start=True, stop=True)
                    last.then_inc(h_psum, 1)

                pairs(pe, NODE_ITERS, project)


def load_steps(nc, sp, m, i, k, parts, sem, residual):
    g = 2 * i + k
    for rows, slot in parts:
        if residual:
            continue
        if isinstance(g, int):
            v = group_of(rows, g, spread=len(rows.shape) == 1)
        else:
            d, j = i // (DG // 2), i % (DG // 2) * 2 + k
            v = group_of(rows, sp.snap(d), spread=len(rows.shape) == 1, j=sp.snap(j))
        for half in range(2):
            cs = slice(half * G // 2, (half + 1) * G // 2)
            if len(rows.shape) == 1:
                sp.dma_start(slot[:, cs, :], v[cs, :].unsqueeze(0).to_broadcast([P, G // 2, P])).then_inc(sem, 16)
            else:
                sp.dma_start(slot[:, cs, :], v[:, cs, :]).then_inc(sem, 16)
    for s in range(G) if residual else ():
        r = (g - GROUPS) * G + s
        if s % 2 == 0:
            word = sp.value_load(m.ttab[0:1, r // 2:r // 2 + 1], min_val=0, max_val=TILE_WORD ** 2 - 1)
        tile = nc.s_assert_within(sp.snap((word >> s % 2 * TILE_BITS) & (TILE_WORD - 1)), 0, TILES - 1, skip_runtime_bounds_check_because="each field is a tile")
        for rows, slot in parts:
            if len(rows.shape) == 1:
                v = rows.rearrange("(t p) -> t p", p=P)[bass.ds(tile, 1)]
                sp.dma_start(slot[:, s, :], v.to_broadcast([P, P])).then_inc(sem, 16)
            else:
                v = rows.rearrange("(t p) f -> t p f", p=P)
                sp.dma_start(slot[:, s, :], v[bass.ds(tile, 1)].rearrange("a p f -> (a p) f")).then_inc(sem, 16)


def arrived(engine, main, rest, i, k, parts):
    g = 2 * i + k
    if isinstance(g, int) and g >= GROUPS:
        engine.wait_ge(rest[g - GROUPS], 16 * G * parts)
    else:
        engine.wait_ge(main[k], 2 * 16 * parts * (i + 1))




def phase_attend(nc, m):
    with ExitStack() as ctx:
        sb = lambda name, shape, dt=F32: ctx.enter_context(nc.sbuf_tensor(name, shape, dt))
        sem = lambda name: ctx.enter_context(nc.semaphore(name))
        H2 = 2 * HEADS
        L = DG * P
        rows = sb("rows", [P, 2, G, HW])
        ef, efT = sb("ef", [P, 2, G, EDIM]), sb("efT", [P, 2, P])
        s_src = sb("s_src", [P, G * HEADS])
        idx = [sb(f"idx{k}", [P, G], U32) for k in range(2)]
        aT, amax, fwd = sb("aT", [P, L]), sb("amax", [P, L]), sb("fwd", [P, L])
        di = sb("di", [P, L], I32)
        pen = sb("pen", [P, L + 1])
        tips, carryT = sb("tips", [P, 2]), sb("carryT", [P, 2])
        ends_i, ends = sb("ends_i", [1, 2, CHUNKS], I32), sb("ends", [1, 2, CHUNKS])
        last_i, last_f, block_i, block_f = sb("last_i", [P, 1], I32), sb("last_f", [P, 1]), sb("block_l", [P, 1], I32), sb("block_lf", [P, 1])
        whole, joint, open_in, stay = sb("whole", [1, CHUNKS]), sb("joint", [1, CHUNKS]), sb("joint_in", [1, 1]), sb("first_link", [1, 1])
        both = sb("both", [1, 2, HEADS, CHUNKS])
        tip, run, carry = (sb(n, [1, 2, HEADS, CHUNKS]) for n in ("tip", "run", "carry"))
        carry_c = sb("carry_c", [1, 2, CHUNKS, HEADS])
        top, pair, enter = sb("top", [1, HEADS]), sb("top_pair", [1, 2, HEADS]), sb("enter", [1, HEADS])
        lane, mine, off = sb("lane_b", [P, 1]), sb("mine_b", [P, 1]), sb("off_b", [P, 1])
        tops, capped, factor, lift = sb("tops", [P, H2]), sb("capped", [P, 2, HEADS]), sb("factor", [P, HEADS]), sb("lift", [P, HEADS])
        meta = sb("meta", [P, DG, G, MW])
        h, meta_r = sb("h_b", [P, 2, G, FEAT]), sb("meta_r", [P, 2, G, MW])
        rel = sb("rel_b", [P, 2, G])
        O, OT = sb("O_b", [P, 2, G, P]), sb("OT_b", [P, 2, QUAD, P])
        msg = sb("msg_b", [P, 2, G, HW])
        z, zm, lz, gap = (sb(n, [P, G, HEADS]) for n in ("z_b", "zm_b", "lz_b", "gap_b"))

        ef_in = [sem(f"ef_in{k}") for k in range(2)]
        rows_out = [sem(f"rows_out{k}") for k in range(2)]
        main = [sem(f"b_in{k}") for k in range(2)]
        rest = [sem(f"b_rest{r}") for r in range(RGROUPS)]
        got = m.got
        idx_ready, efT_psum, efT_ready, a_psum, a_ready, packed, taken = (
            sem(n) for n in ("idx_ready", "efT_psum", "efT_ready", "a_psum", "a_ready", "packed", "s_taken"))
        d_in, prepared, tips_ready, tips_psum, carry_ready, carry_psum, scanned = (
            sem(n) for n in ("d_in", "prepared", "tips_ready", "tips_psum", "carry_ready", "carry_psum", "scanned"))
        turned, filled, meta_out, s_chain, p_chain, o_chain, border_ready, factor_ready = (
            sem(n) for n in ("turned", "filled", "meta_out", "s_chain", "p_chain", "o_chain", "border_ready", "factor_ready"))
        odd_zero, rel_ready, lifted, O_ready, OT_psum, OT_ready, spread_done, ex_ready, msg_ready, msg_full, chain = (
            sem(n) for n in ("odd_zero", "rel_ready", "lifted", "bO_ready", "bOT_psum", "bOT_ready", "spread_done", "ex_ready", "msg_ready", "msg_full", "b_chain"))
        agg_psum, added = [sem(f"bagg{u}") for u in range(QUAD)], [sem(f"badded{u}") for u in range(QUAD)]
        bank = m.bank
        C = m.const
        ident = C[:, C_ID:C_ID + P]
        iota = C[:, C_IOTA:C_IOTA + P]
        one = C[0:1, C_ONE:C_ONE + 1]
        slot = lambda s: bank[4 + s % 4][:, 0:HW]
        tips_bank = bank[6][0:1, 0:2 * P]
        carry_bank, tops_bank = bank[7][:, 0:2], bank[7][:, 4:4 + H2]
        WEIGHED = 4
        META_PARTS = DG // 2
        SCAN_LINKS, PREPARE_LINKS, BORDER_LINKS = 11, 5, 5
        FILLED_ALL = META_PARTS * DOMAINS + 1

        class Beat:

            def __init__(self, r, j):
                self.r, self.j, self.k = r, j, j % 2
                known = isinstance(r, int)
                self.x = x = DG * r + j
                self.i = DG // 2 * r + j // 2
                self.a = DG * r + (j - DG)
                self.ai = DG // 2 * r + (j // 2 - DG // 2)
                self.d = r - 1 if known else r + (-1)
                self.s = DG * r + (j - 1)
                self.gathers = not known or x < GROUPS
                self.scores = not known or 0 < x <= GROUPS
                self.starts = not known or DG <= x < DG + ALLG
                self.ends = not known or DG < x
                self.scans = j == 0 and (not known or 0 < r <= DOMAINS + 1)
                self.residual = known and self.a >= GROUPS
                self.length = P if known and r > DOMAINS else L
                self.border = self.scans and (not known or r > 1)

        def beats(engine, emit):
            for x in range(2 * DG):
                emit(Beat(x // DG, x % DG))
            with engine.Fori(2, DOMAINS) as r:
                for j in range(DG):
                    emit(Beat(r, j))
            for x in range(DOMAINS * DG, DG + ALLG + 1):
                emit(Beat(x // DG, x % DG))

        def gathered(engine, g):
            for s in range(G):
                engine.wait_ge(got[s], 16 * (g + 1))

        def weigh(engine, b, steps):
            k, n = 1 - b.k, steps.stop - steps.start
            return engine.tensor_tensor(msg[:, k, steps, 0:FEAT].rearrange("p s (h d) -> p s h d", h=HEADS),
                                        h[:, k, steps, :].rearrange("p s (h d) -> p s h d", h=HEADS),
                                        msg[:, k, steps, FEAT:HW].unsqueeze(3).to_broadcast([P, n, HEADS, HDIM]), ALU.mult)

        with nc.Block() as block:
            @block.sync
            def _(sp):
                def beat(edges, b):
                    if b.gathers:
                        if late(b.x):
                            sp.wait_ge(efT_psum, b.x - 1)
                        sp.dma_start(ef[:, b.k, :, :], group_of(edges.ea16, b.r, j=b.j)).then_inc(ef_in[b.k], 16)
                    if isinstance(b.r, int) and 2 <= b.x < 2 + TABLES:
                        sp.dma_start(m.table[b.x - 2].rearrange("(p r) f -> p (r f)", p=P),
                                     m.acc_flat[:, 0:TROWS // P * FEAT]).then_inc(m.z_out, 16)
                    if b.starts:
                        if late(b.a):
                            beside(sp, m)
                            sp.wait_ge(msg_full, b.a - 1)
                        if b.residual:
                            if b.a == GROUPS:
                                sp.wait_ge(meta_out, 16 * GROUPS)
                            load_steps(nc, sp, m, b.ai, b.k, [(m.Hs, h[:, b.k, :, :]), (m.meta, meta_r[:, b.k, :, :])], rest[b.a - GROUPS], True)
                        else:
                            beside(sp, m)
                            sp.wait_ge(rows_out[b.k], 16 * b.ai + 16)
                            v = group_of(m.Hs, b.d, j=b.j)
                            for cs in (slice(0, G // 2), slice(G // 2, G)):
                                sp.dma_start(h[:, b.k, cs, :], v[:, cs, :]).then_inc(main[b.k], 16)
                    if b.scans:
                        beside(sp, m)
                        sp.wait_ge(filled, FILLED_ALL if b.length < L else META_PARTS * b.r)
                        for j in range(DG):
                            if b.length == L or j < REST_G:
                                sp.dma_start(group_of(m.meta, b.d, j=j), meta[:, j, :, :]).then_inc(meta_out, 16)
                    if b.j == 2 and b.gathers or (isinstance(b.r, int) and b.x == FULL + 2):
                        whole_domain = not (isinstance(b.r, int) and b.r == DOMAINS)
                        if not (isinstance(b.r, int) and b.r == 0):
                            beside(sp, m)
                            sp.wait_ge(prepared, b.r)
                        n = L if whole_domain else P
                        if not whole_domain:
                            dv = edges.dst[FULL_EDGES:].rearrange("(c e) -> c e", c=CHUNKS)
                        elif isinstance(b.r, int):
                            dv = edges.dst[0:FULL_EDGES].rearrange("(d c e) -> d c e", d=DOMAINS, c=CHUNKS)[b.r]
                        else:
                            dv = edges.dst[0:FULL_EDGES].rearrange("(d c e) -> d c e", d=DOMAINS, c=CHUNKS)[bass.ds(b.r, 1)].rearrange("a c e -> (a c) e")
                        for c in range(CHUNKS):
                            sp.dma_start(di[c * HEADS:(c + 1) * HEADS, 0:n], dv[c:c + 1, :].to_broadcast([HEADS, n])).then_inc(d_in, 16)
                        with nc.allow_non_contiguous_dma(reason="ends of the chunks"):
                            for w, e in enumerate((0, n - 1)):
                                sp.dma_start(ends_i[:, w, :], dv[:, e:e + 1].rearrange("c e -> e c")).then_inc(d_in, 16)
                            if isinstance(b.r, int):
                                lv = edges.dst[max(b.r, 1) * L * CHUNKS - 1:max(b.r, 1) * L * CHUNKS]
                            else:
                                lv = edges.dst[0:FULL_EDGES].rearrange("(d e) -> d e", e=L * CHUNKS)[bass.ds(b.r + (-1), 1), L * CHUNKS - 1:L * CHUNKS].rearrange("a e -> (a e)")
                            sp.dma_start(last_i[:, :], lv.unsqueeze(0).to_broadcast([P, 1])).then_inc(d_in, 16)

                from_edges(sp, m, lambda edges: beats(sp, lambda b: beat(edges, b)))
                sp.wait_ge(meta_out, 16 * GROUPS)

            @block.gpsimd
            def _(pool):
                def beat(b):
                    if b.gathers:
                        pool.wait_ge(idx_ready, b.x + 1)
                        if late(b.x):
                            pool.wait_ge(rows_out[b.k], 16 * b.i)
                            pool.wait_ge(packed, b.x - 1)
                        if late(b.x) or b.x:
                            pool.wait_ge(got[0], 16 * b.x)
                            pool.wait_ge(taken, b.x)
                        take_waits(nc, m, taken)
                        for s in range(G):
                            if late(b.x) or b.x:
                                beside(pool, m)
                                pool.wait_ge(got[s], 16 * b.x)
                            nc.gpsimd.indirect_dma_start(rows[:, b.k, s, :], None, m.H, bass.IndirectOffsetOnAxis(ap=idx[b.k][:, s:s + 1], axis=0)).then_inc(got[s], 16)

                    if b.ends:
                        pool.wait_ge(ex_ready, b.a)
                        weigh(nc.gpsimd, b, slice(0, WEIGHED)).then_inc(msg_ready, 1)

                beats(pool, beat)

            @block.scalar
            def _(act):
                def index(x, k):
                    nc.scalar.copy(idx[k][:, :], m.srcT[:, bass.ds(G * x, G)]).then_inc(idx_ready, 1)

                def take_scores(b):
                    if b.scores:
                        act.wait_ge(a_psum, b.s + 1)
                        if b.j == 1 and (late(b.s) or b.s):
                            act.wait_ge(turned, META_PARTS * b.r)
                        j = (b.j - 1) % DG
                        nc.scalar.copy(aT[:, P * j:P * (j + 1)], bank[3][:, 2 * P:3 * P]).then_inc(a_ready, 1)

                def beat(b):
                    if b.scores:
                        gathered(act, b.s)
                        k = 1 - b.k
                        if late(b.s) or b.s:
                            act.wait_ge(a_psum, b.s)
                        nc.scalar.copy(s_src[:, :].rearrange("p (c h) -> p c h", h=HEADS), rows[:, k, :, FEAT:HW]).then_inc(packed, 1)
                        i = DG // 2 * b.r + (b.j - 1) // 2 if b.j else DG // 2 * b.r + (-1)
                        if late(b.s):
                            act.wait_ge(rows_out[k], 16 * i)
                        v = group_of(m.Hs, b.r, j=b.j - 1) if b.j else group_of(m.Hs, b.d, j=DG - 1)
                        act.dma_start(v, rows[:, k, :, 0:FEAT]).then_inc(rows_out[k], 16)
                    if b.gathers and not (isinstance(b.x, int) and b.x + 1 >= GROUPS):
                        index(b.x + 1, 1 - b.k)
                    if b.j == 1 and (not isinstance(b.r, int) or 1 < b.r <= DOMAINS + 1):
                        act.wait_ge(border_ready, b.d)
                        nc.scalar.activation(factor[:, :], factor[:, :], ACT.Exp).then_inc(factor_ready, 1)
                    if b.scores:
                        act.wait_ge(efT_psum, b.s + 1)
                        nc.scalar.copy(efT[:, :, :], bank[3][:, 0:2 * P].rearrange("p (a e) -> p a e", a=2)).then_inc(efT_ready, 1)
                    if b.j == 0:
                        take_scores(b)
                    if b.starts:
                        for q in range(QUADS):
                            act.wait_ge(OT_psum, QUADS * b.a + q + 1)
                            if late(b.a) or b.a or q > 1:
                                act.wait_ge(spread_done, QUADS * b.a + q - 1)
                            nc.scalar.copy(OT[:, q % 2, :, :], bank[q % 2][:, :].rearrange("p (s e) -> p s e", s=QUAD)).then_inc(OT_ready, 1)
                    if b.j:
                        take_scores(b)
                    if b.starts:
                        if not b.residual:
                            act.wait_ge(main[b.k], 32 * b.ai + 32)
                        act.wait_ge(chain, 3 * b.a + 3)
                        if late(b.a):
                            act.wait_ge(agg_psum[QUAD - 1], QUADS * (b.a - 1))
                        nc.scalar.activation(msg[:, b.k, :, FEAT:HW], gap[:, :, :], ACT.Exp, scale=-1.0).then_inc(ex_ready, 1)

                index(0, 0)
                beats(act, beat)
                act.wait_ge(rows_out[0], 16 * (GROUPS - GROUPS // 2))
                act.wait_ge(rows_out[1], 16 * (GROUPS // 2))

            @block.vector
            def _(dve):
                v = nc.vector
                v.memset(m.acc_odd[:, :, :], 0.0)
                v.memset(m.sdst[:, :, HEADS:H2], NEG)
                v.memset(top[:, :], NEG)
                v.memset(both[:, :, :, :], NEG)
                v.memset(carry[:, :, :, :], NEG)
                v.memset(joint[:, :], NEG)
                v.tensor_scalar(lane[:, :], C[:, C_DUMMY:C_DUMMY + 1], float(NODES), None, ALU.subtract)
                v.memset(pen[:, :], 0.0).then_inc(odd_zero, 1)
                dve.wait_ge(odd_zero, 1)

                def linked(sem, base):
                    done = [0]

                    def link(instruction):
                        done[0] += 1
                        instruction.then_inc(sem, 1)
                        dve.wait_ge(sem, base + done[0])
                    link.done = done
                    return link

                N = CHUNKS - 1

                def prepare(b):
                    n = P if isinstance(b.r, int) and b.r == DOMAINS else L
                    link = linked(p_chain, PREPARE_LINKS * b.r)
                    dve.wait_ge(d_in, 16 * (CHUNKS + 3) * b.r + 16 * (CHUNKS + 3))
                    v.memset(pen[:, n:n + 1], 0.0)
                    link(v.tensor_tensor(pen[:, 1:n], di[:, 1:n], di[:, 0:n - 1], ALU.not_equal))
                    v.tensor_scalar(pen[:, 1:n], pen[:, 1:n], NEG, None, ALU.mult)
                    v.tensor_scalar(block_i[:, :], last_i[:, :], 7, None, ALU.arith_shift_right)
                    v.tensor_copy(last_f[:, :], last_i[:, :])
                    link(v.tensor_copy(ends[:, :, :], ends_i[:, :, :]))
                    v.tensor_copy(block_f[:, :], block_i[:, :])
                    v.tensor_tensor(open_in[:, :], ends[:, 0, 0:1], last_f[0:1, :], ALU.not_equal)
                    v.tensor_tensor(whole[:, :], ends[:, 0, :], ends[:, 1, :], ALU.not_equal)
                    link(v.tensor_tensor(joint[:, 0:N], ends[:, 1, 0:N], ends[:, 0, 1:CHUNKS], ALU.not_equal))
                    v.tensor_scalar(open_in[:, :], open_in[:, :], NEG, None, ALU.mult)
                    v.tensor_scalar(whole[:, :], whole[:, :], NEG, None, ALU.mult)
                    v.scalar_tensor_tensor(mine[:, :], block_f[:, :], float(-P), last_f[:, :], ALU.mult, ALU.add)
                    link(v.tensor_scalar(joint[:, 0:N], joint[:, 0:N], NEG, None, ALU.mult))
                    h_of = lambda a: a.unsqueeze(1).to_broadcast([1, HEADS, N])
                    v.tensor_tensor(stay[:, :], whole[:, 0:1], open_in[:, :], ALU.add)
                    v.tensor_tensor(both[:, 0, :, 1:CHUNKS], h_of(whole[:, 1:CHUNKS]), h_of(joint[:, 0:N]), ALU.add)
                    v.tensor_tensor(both[:, 1, :, 0:N], h_of(whole[:, 0:N]), h_of(joint[:, 0:N]), ALU.add)
                    link(v.tensor_tensor(off[:, :], mine[:, :], lane[:, :], ALU.not_equal))
                    v.tensor_tensor(mine[:, :], mine[:, :], lane[:, :], ALU.is_equal)
                    v.tensor_scalar(off[:, :], off[:, :], NEG, None, ALU.mult).then_inc(prepared, 1)
                    assert link.done[0] == PREPARE_LINKS

                def border(b):
                    link = linked(o_chain, BORDER_LINKS * (b.d - 1) if isinstance(b.d, int) else BORDER_LINKS * b.r + (-2 * BORDER_LINKS))
                    word = dve.value_load(block_i[0:1, 0:1], min_val=0, max_val=BLOCKS - 1)
                    here = bass.ds(word, 1)
                    for u in range(2, QUAD):
                        dve.wait_ge(added[u], QUADS * b.a)
                    sd = m.sdst[:, here, 0:HEADS].to_broadcast([P, 2, HEADS])
                    link(v.tensor_tensor(capped[:, :, :], tops[:, :].rearrange("p (w h) -> p w h", w=2), sd, ALU.add))
                    link(v.tensor_scalar(capped[:, :, :], capped[:, :, :], 0.0, None, ALU.max))
                    link(v.tensor_tensor(factor[:, :], capped[:, 0, :], capped[:, 1, :], ALU.subtract))
                    v.tensor_scalar(factor[:, :], factor[:, :], mine[:, :], None, ALU.mult).then_inc(border_ready, 1)
                    link(v.tensor_scalar(lift[:, :], tops[:, HEADS:H2], off[:, :], None, ALU.add))
                    t = m.sdst[:, here, HEADS:H2].rearrange("p b h -> p (b h)")
                    v.tensor_tensor(t, t, lift[:, :], ALU.max)
                    dve.wait_ge(factor_ready, b.d)
                    for acc in (m.acc, m.acc_odd):
                        a = acc[:, here, 0:FEAT].rearrange("p b (h e) -> p (b h) e", h=HEADS)
                        v.tensor_tensor(a, a, factor[:, :].unsqueeze(2).to_broadcast([P, HEADS, HDIM]), ALU.mult)
                        w = acc[:, here, FEAT:HW].rearrange("p b h -> p (b h)")
                        last = v.tensor_tensor(w, w, factor[:, :], ALU.mult)
                    link(last)

                def scan(b):
                    n = b.length
                    link = linked(s_chain, SCAN_LINKS * b.d)
                    dve.wait_ge(prepared, b.r)
                    dve.wait_ge(a_ready, GROUPS if n < L else DG * b.r)
                    link(v.tensor_tensor_scan(fwd[:, 0:n], pen[:, 0:n], aT[:, 0:n], NEG, ALU.add, ALU.max))
                    v.tensor_copy(tips[:, 0:1], fwd[:, n - 1:n])
                    link(v.tensor_tensor_scan(amax[:, 0:n][:, ::-1], pen[:, 1:n + 1][:, ::-1], aT[:, 0:n][:, ::-1], NEG, ALU.add, ALU.max))
                    v.tensor_copy(tips[:, 1:2], amax[:, 0:1]).then_inc(tips_ready, 1)
                    v.tensor_scalar(enter[:, :], top[:, :], stay[:, :], None, ALU.add)
                    dve.wait_ge(tips_psum, b.r)
                    link(v.tensor_copy(tip[:, :, :, :], tips_bank.rearrange("p (w c h) -> p w h c", w=2, c=CHUNKS)))
                    link(v.tensor_tensor(tip[:, 0, :, 0], tip[:, 0, :, 0], enter[:, :], ALU.max))
                    flat = lambda a, w: a[:, w, :, :].rearrange("p h c -> p (h c)")
                    link(v.tensor_tensor_scan(flat(run, 0), flat(both, 0), flat(tip, 0), NEG, ALU.add, ALU.max))
                    link(v.tensor_tensor_scan(flat(run, 1)[:, ::-1], flat(both, 1)[:, ::-1], flat(tip, 1)[:, ::-1], NEG, ALU.add, ALU.max))
                    h_of = joint[:, 0:N].unsqueeze(1).to_broadcast([1, HEADS, N])
                    v.tensor_scalar(carry[:, 0, :, 0], top[:, :], open_in[:, :], None, ALU.add)
                    v.tensor_scalar(pair[:, 1, :], run[:, 1, :, 0], open_in[:, :], None, ALU.add)
                    v.tensor_copy(pair[:, 0, :], top[:, :])
                    v.tensor_tensor(carry[:, 0, :, 1:CHUNKS], run[:, 0, :, 0:N], h_of, ALU.add)
                    link(v.tensor_tensor(carry[:, 1, :, 0:N], run[:, 1, :, 1:CHUNKS], h_of, ALU.add))
                    v.tensor_tensor(pair[:, 1, :], pair[:, 1, :], top[:, :], ALU.max)
                    link(v.tensor_copy(carry_c[:, :, :, :].rearrange("p w c h -> p w h c"), carry[:, :, :, :]))
                    v.tensor_copy(top[:, :], run[:, 0, :, N]).then_inc(carry_ready, 1)
                    dve.wait_ge(carry_psum, b.r)
                    if b.border:
                        v.tensor_copy(tops[:, :], tops_bank)
                    link(v.tensor_copy(carryT[:, :], carry_bank))
                    link(v.tensor_tensor_scan(fwd[:, 0:n], pen[:, 0:n], aT[:, 0:n], carryT[:, 0:1], ALU.add, ALU.max))
                    link(v.tensor_tensor_scan(amax[:, 0:n][:, ::-1], pen[:, 1:n + 1][:, ::-1], aT[:, 0:n][:, ::-1], carryT[:, 1:2], ALU.add, ALU.max))
                    v.tensor_tensor(amax[:, 0:n], amax[:, 0:n], fwd[:, 0:n], ALU.max).then_inc(scanned, 1)
                    assert link.done[0] == SCAN_LINKS, link.done
                    if not (isinstance(b.r, int) and b.r == 1):
                        dve.wait_ge(meta_out, 16 * DG * b.d)
                    for t in range(META_PARTS):
                        if 2 * t * P < n:
                            w = min(2, n // P - 2 * t)
                            dve.wait_ge(turned, META_PARTS * b.d + t + 1)
                            for u in range(w):
                                v.tensor_copy(meta[:, 2 * t + u, :, 0:H2].rearrange("p c (w h) -> p w c h", w=2),
                                              bank[4 + t % 2][:, u * 2 * P:(u + 1) * 2 * P].rearrange("p (w c h) -> p w c h", w=2, c=CHUNKS))
                                cols = bass.ds(DOMAIN * b.d + G * (2 * t + u), G)
                                v.tensor_copy(meta[:, 2 * t + u, :, H2], m.dstT[:, cols])
                                last = v.tensor_copy(meta[:, 2 * t + u, :, H2 + 1], m.srcT[:, cols])
                            last.then_inc(filled, 1)
                    dve.wait_ge(filled, FILLED_ALL if n < L else META_PARTS * b.r)

                def hot(b):
                    if b.residual:
                        dve.wait_ge(rest[b.a - GROUPS], 16 * G * 2)
                    if late(b.a):
                        dve.wait_ge(agg_psum[QUAD - 1], QUADS * (b.a - 1))
                    base = m.baseB[:, bass.ds(G * b.a, G)]
                    dst = meta_r[:, b.k, :, H2] if b.residual else m.dstT[:, bass.ds(G * b.a, G)]
                    v.tensor_tensor(rel[:, b.k, :], dst, base, ALU.subtract).then_inc(rel_ready, 1)
                    dve.wait_ge(rel_ready, b.a + 1)
                    v.tensor_tensor(O[:, b.k, :, :], iota.unsqueeze(1).to_broadcast([P, G, P]), rel[:, b.k, :].unsqueeze(2).to_broadcast([P, G, P]), ALU.is_equal).then_inc(O_ready, 1)

                def scores(b):
                    dve.wait_ge(spread_done, QUADS * b.a + QUADS)
                    if late(b.a) or b.a:
                        dve.wait_ge(ex_ready, b.a)
                    if b.residual:
                        sd2 = bank[2][:, 0:G * H2].rearrange("p (s h) -> p s h", s=G)
                        sd = sd2[:, :, 0:HEADS]
                        a, amax_e = meta_r[:, b.k, :, 0:HEADS], meta_r[:, b.k, :, HEADS:H2]
                        v.tensor_tensor(lz[:, :, :], amax_e, sd2[:, :, HEADS:H2], ALU.max).then_inc(lifted, 1)
                        dve.wait_ge(lifted, b.a - GROUPS + 1)
                        amax_e = lz[:, :, :]
                    else:
                        sd = bank[2][:, 0:G * HEADS].rearrange("p (s h) -> p s h", s=G)
                        a, amax_e = meta[:, b.j, :, 0:HEADS], meta[:, b.j, :, HEADS:H2]
                    v.tensor_tensor(zm[:, :, :], amax_e, sd, ALU.add)
                    v.tensor_tensor(z[:, :, :], a, sd, ALU.add).then_inc(chain, 1)
                    dve.wait_ge(chain, 3 * b.a + 1)
                    v.scalar_tensor_tensor(lz[:, :, :], z[:, :, :], SLOPE, z[:, :, :], ALU.mult, ALU.max).then_inc(chain, 1)
                    dve.wait_ge(chain, 3 * b.a + 2)
                    v.scalar_tensor_tensor(gap[:, :, :], zm[:, :, :], 0.0, lz[:, :, :], ALU.max, ALU.subtract).then_inc(chain, 1)

                def sums(g, k):
                    if isinstance(g, int) and g == 0:
                        dve.wait_ge(m.z_out, 16 * TABLES)
                    for q in range(QUADS):
                        blocks = windows(nc, dve, m, g, q)
                        for u in range(QUAD):
                            if u >= 2:
                                dve.wait_ge(added[u - 2], QUADS * g + q + 1)
                            elif q or not (isinstance(g, int) and g < 1):
                                dve.wait_ge(added[u + 2], QUADS * g + q)
                            dve.wait_ge(agg_psum[u], QUADS * g + q + 1)
                            a = (m.acc, m.acc_odd)[u % 2][:, bass.ds(blocks[u], 1), :].rearrange("p b f -> p (b f)")
                            v.tensor_tensor(a, a, slot(u), ALU.add).then_inc(added[u], 1)

                def beat(b):
                    if b.j == DG - 2 and (not isinstance(b.r, int) or b.r <= DOMAINS):
                        prepare(b)
                    if b.starts:
                        hot(b)
                    if b.ends:
                        dve.wait_ge(msg_ready, b.a)
                        weigh(v, b, slice(WEIGHED, G)).then_inc(msg_full, 1)
                    if b.scans:
                        scan(b)
                        scores(b)
                    if b.ends:
                        sums(b.a - 1 if isinstance(b.a, int) else DG * b.r + (b.j - DG - 1), 1 - b.k)
                    if b.border:
                        border(b)
                    if b.starts and b.j:
                        scores(b)

                beats(dve, beat)

            @block.tensor
            def _(pe):
                def turn(b, q):
                    if late(b.a) or b.a or q > 1:
                        pe.wait_ge(OT_ready, QUADS * b.a + q - 1)
                    for u in range(QUAD):
                        last = nc.tensor.transpose(bank[q % 2][:, u * P:(u + 1) * P], O[:, b.k, QUAD * q + u, :], ident)
                    last.then_inc(OT_psum, 1)

                def spread(b, q):
                    W = H2 if b.residual else HEADS
                    blocks = windows(nc, pe, m, b.a, q)
                    pe.wait_ge(OT_ready, QUADS * b.a + q + 1)
                    for u in range(QUAD):
                        s = QUAD * q + u
                        last = nc.tensor.matmul(bank[2][:, s * W:(s + 1) * W], OT[:, q % 2, u, :],
                                                m.sdst[:, bass.ds(blocks[u], 1), 0:W].rearrange("p b h -> p (b h)"), start=True, stop=True)
                    last.then_inc(spread_done, 1)

                def total(g, k, q):
                    if q == WEIGHED // QUAD:
                        pe.wait_ge(msg_full, g + 1)
                    for u in range(QUAD):
                        s = QUAD * q + u
                        if q or not (isinstance(g, int) and g < 1):
                            pe.wait_ge(added[u], QUADS * g + q)
                        nc.tensor.matmul(slot(u), O[:, k, s, :], msg[:, k, s, :], start=True, stop=True).then_inc(agg_psum[u], 1)

                def products(b):
                    if b.scores:
                        pe.wait_ge(efT_ready, b.s + 1)
                        for half in range(2):
                            nc.tensor.matmul(bank[3][:, 2 * P:3 * P], m.wblock[:, half, :, :].rearrange("p c h -> p (c h)"), efT[:, half, :], start=(half == 0), stop=False)
                        pe.wait_ge(packed, b.s + 1)
                        nc.tensor.matmul(bank[3][:, 2 * P:3 * P], s_src[:, :], ident, start=False, stop=True).then_inc(a_psum, 1)

                def tips_across(b):
                    pe.wait_ge(tips_ready, b.r)
                    for w in range(2):
                        last = nc.tensor.matmul(tips_bank[:, w * P:(w + 1) * P], tips[:, w:w + 1], ident, start=True, stop=True)
                    last.then_inc(tips_psum, 1)

                def carries_back(b):
                    pe.wait_ge(carry_ready, b.r)
                    for w in range(2):
                        last = nc.tensor.matmul(carry_bank[:, w:w + 1], carry_c[:, w, :, :].rearrange("p c h -> p (c h)"), one, start=True, stop=True)
                    if b.border:
                        last = nc.tensor.matmul(tops_bank, C[0:1, C_ONE:C_ONE + P], pair[:, :, :].rearrange("p w h -> p (w h)"), start=True, stop=True)
                    last.then_inc(carry_psum, 1)

                def turn_edge_data(b):
                    pe.wait_ge(scanned, b.r)
                    for t in range(META_PARTS):
                        if 2 * t * P < b.length:
                            if t > 1:
                                pe.wait_ge(filled, META_PARTS * b.d + t - 1)
                            for u in range(min(2, b.length // P - 2 * t)):
                                for w, a in enumerate((aT, amax)):
                                    last = nc.tensor.transpose(bank[4 + t % 2][:, (2 * u + w) * P:(2 * u + w + 1) * P], a[:, (2 * t + u) * P:(2 * t + u + 1) * P], ident)
                            last.then_inc(turned, 1)

                def beat(b):
                    before = b.a - 1 if isinstance(b.a, int) else DG * b.r + (b.j - DG - 1)
                    if b.starts and b.j:
                        pe.wait_ge(O_ready, b.a + 1)
                        turn(b, 0)
                    if b.scores:
                        k = 1 - b.k
                        i = DG // 2 * b.r + (b.j - 1) // 2 if b.j else DG // 2 * b.r + (-1)
                        pe.wait_ge(ef_in[k], 16 * i + 16)
                        if late(b.s) or b.s:
                            pe.wait_ge(a_ready, b.s)
                        e2 = ef[:, k, :, :].rearrange("p (a c) f -> p a (c f)", a=2)
                        for half in range(2):
                            last = nc.tensor.transpose(bank[3][:, half * P:(half + 1) * P], e2[:, half, :], ident)
                        last.then_inc(efT_psum, 1)
                    if b.scans:
                        if b.scores:
                            products(b)
                        pe.wait_ge(O_ready, b.a + 1)
                        turn(b, 0)
                        tips_across(b)
                        turn(b, 1)
                        spread(b, 0)
                        carries_back(b)
                        for q in range(1, QUADS):
                            if q + 1 < QUADS:
                                turn(b, q + 1)
                            spread(b, q)
                        turn_edge_data(b)
                        if b.ends:
                            pe.wait_ge(filled, FILLED_ALL if b.length < L else META_PARTS * b.r)
                            pe.wait_ge(msg_ready, b.a)
                            for q in range(QUADS):
                                total(before, 1 - b.k, q)
                        return
                    if b.ends:
                        pe.wait_ge(msg_ready, b.a)
                    for q in range(QUADS):
                        if b.ends:
                            total(before, 1 - b.k, q)
                        if b.starts and q + 1 < QUADS:
                            turn(b, q + 1)
                        if b.starts:
                            spread(b, q)
                    if b.scores:
                        products(b)

                beats(pe, beat)


def phase_norm(nc, m, last_layer):
    number = "2" if last_layer else "1"
    with ExitStack() as ctx:
        sb = lambda name, shape, dt=F32: ctx.enter_context(nc.sbuf_tensor(name + number, shape, dt))
        sem = lambda name: ctx.enter_context(nc.semaphore(name + number))
        S = NODE_STEP
        PARTS = TABLES if last_layer else 1
        y, e, sq = sb("y", [P, 2, S, FEAT]), sb("e", [P, S, FEAT]), sb("sq", [P, S, FEAT])
        rec = sb("rec", [P, S, HEADS])
        add = sb("add", [P, 2, PARTS, S, FEAT])
        mean, var, dev = sb("mean", [P, S]), sb("var", [P, S]), sb("dev", [P, 2, S])
        eps = sb("eps", [P, 1])
        chain, dev_ready, normed, ready, out, sum_chain, merged, exp_ready, sum_done, min_ready = (m.norm[n] for n in NORM_SEMAPHORES[:-2])
        x_in = [m.norm[n] for n in NORM_SEMAPHORES[-2:]]
        BEFORE = NODE_ITERS if last_layer else 0
        LOADS_BEFORE = [(BEFORE + 1) // 2, BEFORE // 2]
        LINKS = 6
        SUM_LINKS = 5
        xv = m.x.rearrange("(b p) f -> p b f", p=P)
        REST = N_REAL - (BLOCKS - 1) * P

        with nc.Block() as block:
            @block.sync
            def _(sp):
                def load(n, i, k):
                    here = bass.ds(S * n, S)
                    sources = [t[0:NODES, :].rearrange("(b p) f -> p b f", p=P) for t in m.table] if last_layer else [xv]
                    for t, v in enumerate(sources):
                        sp.dma_start(add[:, k, t, :, :], v[:, here, :]).then_inc(x_in[k], 16)

                def work(i, k):
                    n = 2 * i + k
                    sp.wait_ge(normed, n + 1 + BEFORE)
                    if not last_layer:
                        sp.dma_start(m.X1.rearrange("(b p) f -> p b f", p=P)[:, bass.ds(S * n, S), :], m.x1[:, bass.ds(S * n, S), :]).then_inc(out, 16)
                    elif isinstance(n, int) and n == NODE_ITERS - 1:
                        first = S * n
                        sp.dma_start(m.out[first * P:(BLOCKS - 1) * P, :].rearrange("(b p) f -> p b f", p=P), m.x1[:, first:BLOCKS - 1, :]).then_inc(out, 16)
                        sp.dma_start(m.out[(BLOCKS - 1) * P:N_REAL, :], m.x1[0:REST, BLOCKS - 1, :]).then_inc(out, 16)
                    else:
                        sp.dma_start(m.out[0:(BLOCKS - 1) * P, :].rearrange("(b p) f -> p b f", p=P)[:, bass.ds(S * n, S), :], m.x1[:, bass.ds(S * n, S), :]).then_inc(out, 16)
                    if not (isinstance(n, int) and n + 2 >= NODE_ITERS):
                        load(n + 2, i, k)

                for k in range(2):
                    load(k, 0, k)
                for n in range(NODE_ITERS):
                    work(n // 2, n % 2)
                sp.wait_ge(out, 16 * (NODE_ITERS + (BEFORE + 1 if last_layer else 0)))

            @block.gpsimd
            def _(pool):
                def tables(i, k):
                    n = 2 * i + k
                    pool.wait_ge(x_in[k], 16 * TABLES * i + 16 * (TABLES + LOADS_BEFORE[k]))
                    a = lambda t: add[:, k, t, :, :]
                    nc.gpsimd.tensor_tensor(a(0), a(0), a(1), ALU.add)
                    nc.gpsimd.tensor_tensor(a(2), a(2), a(3), ALU.add).then_inc(min_ready, 1)
                    pool.wait_ge(min_ready, n + 1 + BEFORE)
                    nc.gpsimd.tensor_tensor(a(0), a(0), a(2), ALU.add).then_inc(merged, 1)

                def halves(i, k):
                    here = bass.ds(S * (2 * i + k), S)
                    nc.gpsimd.tensor_tensor(m.acc[:, here, :], m.acc[:, here, :], m.acc_odd[:, here, :], ALU.add).then_inc(merged, 1)

                pairs(pool, NODE_ITERS, tables if last_layer else halves)

            @block.scalar
            def _(act):
                act.wait_ge(ready, 2 if last_layer else 1)

                def root(n, k):
                    act.wait_ge(chain, LINKS * (n + BEFORE) + 5)
                    nc.scalar.activation(dev[:, k, :], var[:, :], ACT.Sqrt, bias=eps[:, 0:1], scale=1.0 / FEAT).then_inc(dev_ready, 1)

                def work(i, k):
                    n = 2 * i + k
                    if last_layer:
                        root(n, k)
                        return
                    act.wait_ge(min_ready, n + 1)
                    nc.scalar.activation(e[:, :, :], e[:, :, :], ACT.Exp).then_inc(exp_ready, 1)
                    if late(n) or n:
                        root(n - 1, 1 - k)

                pairs(act, NODE_ITERS, work)
                if not last_layer:
                    root(NODE_ITERS - 1, (NODE_ITERS - 1) % 2)

            @block.vector
            def _(dve):
                v = nc.vector
                v.memset(eps[:, :], EPS_LN).then_inc(ready, 1)

                def linked(sem, base):
                    done = [0]

                    def link(instruction):
                        done[0] += 1
                        instruction.then_inc(sem, 1)
                        dve.wait_ge(sem, base + done[0])
                    link.done = done
                    return link

                def center(n, k):
                    link = linked(chain, LINKS * (n + BEFORE))
                    yk = y[:, k, :, :]
                    link(v.tensor_reduce(mean[:, :], yk, AX.X, ALU.add))
                    link(v.tensor_scalar(mean[:, :], mean[:, :], 1.0 / FEAT, None, ALU.mult))
                    link(v.tensor_tensor(yk, yk, mean[:, :].unsqueeze(2).to_broadcast([P, S, FEAT]), ALU.subtract))
                    link(v.tensor_tensor(sq[:, :, :], yk, yk, ALU.mult))
                    link(v.tensor_reduce(var[:, :], sq[:, :, :], AX.X, ALU.add))

                def scale(n, k):
                    dve.wait_ge(dev_ready, n + 1 + BEFORE)
                    v.reciprocal(dev[:, k, :], dev[:, k, :]).then_inc(chain, 1)
                    dve.wait_ge(chain, LINKS * (n + BEFORE) + LINKS)
                    v.tensor_tensor(m.x1[:, bass.ds(S * n, S), :], y[:, k, :, :], dev[:, k, :].unsqueeze(2).to_broadcast([P, S, FEAT]), ALU.mult).then_inc(normed, 1)

                def second(i, k):
                    n = 2 * i + k
                    here = bass.ds(S * n, S)
                    link = linked(sum_chain, 2 * n + SUM_LINKS * BEFORE)
                    link(v.tensor_tensor(y[:, k, :, :], m.x1[:, here, :], m.acc1[:, here, :], ALU.add))
                    dve.wait_ge(merged, n + 1 + BEFORE)
                    link(v.tensor_tensor(y[:, k, :, :], y[:, k, :, :], add[:, k, 0, :, :], ALU.add))
                    center(n, k)
                    scale(n, k)

                def first(i, k):
                    n = 2 * i + k
                    before = late(n) or n
                    here = bass.ds(S * n, S)
                    link = linked(sum_chain, SUM_LINKS * n)
                    dve.wait_ge(merged, n + 1)
                    link(v.tensor_scalar(rec[:, :, :], m.acc[:, here, FEAT:HW], EPS_DEN, None, ALU.add))
                    link(v.reciprocal(rec[:, :, :], rec[:, :, :]))
                    yk = y[:, k, :, :]
                    y4 = yk.rearrange("p s (h d) -> p s h d", h=HEADS)
                    for s in range(S):
                        a = m.acc[:, bass.ds(S * n + s, 1), 0:FEAT].rearrange("p b (h d) -> p (b h) d", h=HEADS)
                        last = v.tensor_tensor(y4[:, s, :, :], a, rec[:, s, :].unsqueeze(2).to_broadcast([P, HEADS, HDIM]), ALU.mult)
                    link(last)
                    v.tensor_scalar(e[:, :, :], yk, 0.0, None, ALU.min).then_inc(min_ready, 1)
                    if before:
                        center(n - 1, 1 - k)
                    dve.wait_ge(exp_ready, n + 1)
                    link(v.tensor_scalar(e[:, :, :], e[:, :, :], -1.0, None, ALU.add))
                    link(v.scalar_tensor_tensor(yk, yk, 0.0, e[:, :, :], ALU.max, ALU.add))
                    assert link.done[0] == SUM_LINKS
                    dve.wait_ge(x_in[k], 16 * (i + 1))
                    v.tensor_tensor(yk, yk, add[:, k, 0, :, :], ALU.add).then_inc(sum_done, 1)
                    if before:
                        scale(n - 1, 1 - k)
                    dve.wait_ge(sum_done, n + 1)

                if last_layer:
                    pairs(dve, NODE_ITERS, second)
                else:
                    pairs(dve, NODE_ITERS, first)
                    center(NODE_ITERS - 1, (NODE_ITERS - 1) % 2)
                    scale(NODE_ITERS - 1, (NODE_ITERS - 1) % 2)


def phase_messages(nc, m):
    with ExitStack() as ctx:
        sb = lambda name, shape, dt=F32: ctx.enter_context(nc.sbuf_tensor(name, shape, dt))
        sem = lambda name: ctx.enter_context(nc.semaphore(name))
        ea, got_rows = sb("ea", [P, 2, G, FEAT]), sb("got_rows", [P, 2, G, FEAT])
        ends = sb("ends_l", [P, 2, G, 2])
        rel = sb("rel_l", [P, 2, G])
        dstR, srcR = sb("dstR", [P, 2, G, P], I32), sb("srcR", [P, 2, G, P], I32)
        O, OT = sb("O_l", [P, 2, G, P]), sb("OT_l", [P, G, P])
        same = sb("same", [P, G, P])
        back = sb("back", [P, G, FEAT])
        merged = sb("merged", [P, 2, G, FEAT])
        dup, far = sb("dup", [P, G]), sb("far", [P, G])
        idx = [sb(f"gidx{k}", [P, G], U32) for k in range(2)]
        sidx = [sb(f"sidx{k}", [P, G], U32) for k in range(2)]
        main = [sem(f"l_in{k}") for k in range(2)]
        rest = [sem(f"l_rest{r}") for r in range(RGROUPS)]
        got = m.got
        put = [sem(f"put{s}") for s in range(G)]
        merged_ready = [sem(f"l_merged{q}") for q in range(QUADS)]
        (idx_ready, O_ready, OT_ready, same_ready, rank_psum, sidx_ready, spread_done, back_ready,
         merged_psum, fwd_ready, agg_psum, added, chain, taken) = (
            sem(n) for n in ("l_idx", "l_O", "l_OT", "l_same", "l_rank", "l_sidx", "l_spread", "l_back",
                             "l_mergedp", "l_fwd", "l_agg", "l_added", "l_chain", "l_taken"))
        bank = m.bank
        C = m.const
        ident = C[:, C_ID:C_ID + P]
        iota = C[:, C_IOTA:C_IOTA + P]
        quad_of = lambda t, q: t[:, QUAD * q:QUAD * (q + 1), :]
        as_quad = lambda b: b[:, :].rearrange("p (s e) -> p s e", s=QUAD)

        def gathered(engine, g):
            for s in range(G):
                engine.wait_ge(got[s], 16 * (g + GROUPS + 1))

        def scattered(engine, g):
            for s in range(G):
                engine.wait_ge(put[s], 16 * (g + 1))

        def all_groups(engine, emit):
            pairs(engine, GROUPS, emit)
            for g in range(GROUPS, ALLG):
                emit(g // 2, g % 2)

        with nc.Block() as block:
            @block.sync
            def _(sp):
                def load(edges, i, k):
                    g = 2 * i + k
                    residual = isinstance(g, int) and g >= GROUPS
                    if late(g):
                        beside(sp, m)
                        sp.wait_ge(fwd_ready, g - 1)
                    load_steps(nc, sp, m, i, k, [(m.meta[:, 2 * HEADS:MW], ends[:, k, :, :]), (edges.dst, dstR[:, k, :, :]),
                                                 (edges.src, srcR[:, k, :, :]), (edges.ea, ea[:, k, :, :])],
                               rest[g - GROUPS] if residual else main[k], residual)

                from_edges(sp, m, lambda edges: all_groups(sp, lambda i, k: load(edges, i, k)))

            @block.gpsimd
            def _(pool):
                def gather(g, k, s):
                    if late(g) or g:
                        beside(pool, m)
                        pool.wait_ge(got[s], 16 * (g + GROUPS))
                    nc.gpsimd.indirect_dma_start(got_rows[:, k, s, :], None, m.X1, bass.IndirectOffsetOnAxis(ap=idx[k][:, s:s + 1], axis=0)).then_inc(got[s], 16)

                def scatter(after, k, s):
                    if s % QUAD == 0:
                        beside(pool, m)
                        pool.wait_ge(merged_ready[s // QUAD], after)
                    if s >= TABLES:
                        beside(pool, m)
                        pool.wait_ge(put[s - TABLES], 16 * after)
                    elif late(after):
                        beside(pool, m)
                        pool.wait_ge(put[s - TABLES + G], 16 * after - 16)
                    nc.gpsimd.indirect_dma_start(m.table[s % TABLES], bass.IndirectOffsetOnAxis(ap=sidx[k][:, s:s + 1], axis=0), merged[:, k, s, :], None,
                                                 compute_op=ALU.add).then_inc(put[s], 16)

                def work(i, k):
                    g = 2 * i + k
                    pool.wait_ge(idx_ready, g + 1)
                    pool.wait_ge(sidx_ready, g)
                    pool.wait_ge(got[0], 16 * g)
                    pool.wait_ge(got[0], 16 * (g + GROUPS))
                    if late(g):
                        pool.wait_ge(agg_psum, QUADS * (g - 1))
                        pool.wait_ge(put[G - TABLES], 16 * g - 16)
                        pool.wait_ge(taken, g - 1)
                    take_waits(nc, m, taken)
                    for s in range(G):
                        gather(g, k, s)
                        scatter(g, 1 - k, s)

                pool.wait_ge(idx_ready, 1)
                for s in range(G):
                    gather(0, 0, s)
                work(0, 1)
                with pool.Fori(1, GROUPS // 2) as i:
                    for k in range(2):
                        work(i, k)
                for g in range(GROUPS // 2 * 2, ALLG):
                    work(g // 2, g % 2)
                pool.wait_ge(sidx_ready, ALLG)
                for s in range(G):
                    scatter(ALLG, (ALLG - 1) % 2, s)
                scattered(pool, ALLG - 1)

            @block.scalar
            def _(act):
                def index(i, k):
                    g = 2 * i + k
                    arrived(act, main, rest, i, k, 4)
                    if late(g):
                        gathered(act, g - 2)
                    nc.scalar.copy(idx[k][:, :], ends[:, k, :, 1]).then_inc(idx_ready, 1)

                def work(i, k):
                    g = 2 * i + k
                    for q in range(QUADS):
                        if q == 0 and late(g):
                            scattered(act, g - 2)
                        act.wait_ge(merged_psum, QUADS * g + q + 1)
                        nc.scalar.copy(merged[:, k, QUAD * q:QUAD * (q + 1), :], as_quad(bank[6 + q % 2])).then_inc(merged_ready[q], 1)

                index(0, 0)
                index(0, 1)
                work(0, 0)
                with act.Fori(1, GROUPS // 2) as i:
                    index(i, 0)
                    work(i - 1, 1)
                    index(i, 1)
                    work(i, 0)
                for g in range(GROUPS // 2 * 2, ALLG):
                    index(g // 2, g % 2)
                    work((g - 1) // 2, (g - 1) % 2)
                work((ALLG - 1) // 2, (ALLG - 1) % 2)

            @block.vector
            def _(dve):
                v = nc.vector
                v.memset(m.acc1[:, :, :], 0.0).then_inc(chain, 1)
                LINKS = 3

                def forward(g, k):
                    gathered(dve, g)
                    v.tensor_tensor(got_rows[:, k, :, :], got_rows[:, k, :, :], ea[:, k, :, :], ALU.mult).then_inc(fwd_ready, 1)

                def sums(g, steps=range(G)):
                    for s in steps:
                        if s % QUAD == 0:
                            blocks = windows(nc, dve, m, g, s // QUAD)
                        b = blocks[s % QUAD]
                        if s or late(g) or g:
                            dve.wait_ge(added, G * g + s)
                        if s % QUAD == 0:
                            dve.wait_ge(agg_psum, QUADS * g + s // QUAD + 1)
                        a = m.acc1[:, bass.ds(b, 1), :].rearrange("p b f -> p (b f)")
                        v.tensor_tensor(a, a, bank[2 + s // QUAD % 3][:, s % QUAD * P:(s % QUAD + 1) * P], ALU.add).then_inc(added, 1)

                def work(i, k):
                    g = 2 * i + k
                    if late(g) or g:
                        forward(g - 1, 1 - k)
                    arrived(dve, main, rest, i, k, 4)
                    if late(g) or g:
                        dve.wait_ge(merged_psum, QUADS * g)
                    v.tensor_tensor(same[:, :, :], srcR[:, k, :, :], ends[:, k, :, 1:2].to_broadcast([P, G, P]), ALU.is_equal).then_inc(same_ready, 1)
                    if late(g) or g:
                        dve.wait_ge(spread_done, QUADS * g)
                    v.tensor_tensor(OT[:, :, :], dstR[:, k, :, :], m.nodeB[:, bass.ds(G * g, G)].unsqueeze(2).to_broadcast([P, G, P]), ALU.is_equal).then_inc(OT_ready, 1)
                    if late(g):
                        dve.wait_ge(agg_psum, QUADS * (g - 1))
                    v.tensor_tensor(rel[:, k, :], ends[:, k, :, 0], m.baseB[:, bass.ds(G * g, G)], ALU.subtract).then_inc(chain, 1)
                    dve.wait_ge(chain, LINKS * g + 2)
                    v.tensor_tensor(O[:, k, :, :], iota.unsqueeze(1).to_broadcast([P, G, P]), rel[:, k, :].unsqueeze(2).to_broadcast([P, G, P]), ALU.is_equal).then_inc(O_ready, 1)
                    if late(g) or g:
                        sums(g - 1, range(QUAD))
                    dve.wait_ge(rank_psum, g + 1)
                    v.tensor_scalar(far[:, :], ends[:, k, :, 1], -1.0, C[:, C_DUMMY:C_DUMMY + 1], ALU.mult, ALU.add)
                    v.tensor_scalar(dup[:, :], bank[5][:, 0:G], C[:, C_THR:C_THR + 1], None, ALU.is_gt).then_inc(chain, 1)
                    dve.wait_ge(chain, LINKS * g + 3)
                    v.tensor_tensor(far[:, :], far[:, :], dup[:, :], ALU.mult).then_inc(chain, 1)
                    dve.wait_ge(chain, LINKS * g + 4)
                    if late(g):
                        scattered(dve, g - 2)
                    v.tensor_tensor(sidx[k][:, :], far[:, :], ends[:, k, :, 1], ALU.add).then_inc(sidx_ready, 1)
                    dve.wait_ge(sidx_ready, g + 1)
                    for q in range(QUADS):
                        dve.wait_ge(spread_done, QUADS * g + q + 1)
                        v.tensor_tensor(quad_of(back, q), ea[:, k, QUAD * q:QUAD * (q + 1), :], as_quad(bank[q % 2]), ALU.mult).then_inc(back_ready, 1)
                    if late(g) or g:
                        sums(g - 1, range(QUAD, G))

                all_groups(dve, work)
                forward(ALLG - 1, (ALLG - 1) % 2)
                sums(ALLG - 1)

            @block.tensor
            def _(pe):
                def totals(g, k, q):
                    if q == QUADS - 1:
                        pe.wait_ge(added, G * g + QUAD)
                    elif late(g) or g:
                        pe.wait_ge(added, G * g)
                    for u in range(QUAD):
                        s = QUAD * q + u
                        last = nc.tensor.matmul(bank[2 + q % 3][:, u * P:(u + 1) * P], O[:, k, s, :], got_rows[:, k, s, :], start=True, stop=True)
                    last.then_inc(agg_psum, 1)

                def work(i, k):
                    g = 2 * i + k
                    before = late(g) or g
                    if before:
                        pe.wait_ge(fwd_ready, g)
                        for q in range(QUADS - 1):
                            totals(g - 1, 1 - k, q)
                    pe.wait_ge(same_ready, g + 1)
                    if before:
                        pe.wait_ge(sidx_ready, g)
                    for s in range(G):
                        last = nc.tensor.matmul(bank[5][:, s:s + 1], same[:, s, :], C[:, C_W3:C_W3 + 1], start=True, stop=True)
                    last.then_inc(rank_psum, 1)
                    pe.wait_ge(OT_ready, g + 1)
                    for q in range(QUADS):
                        if q == 2 and before:
                            totals(g - 1, 1 - k, QUADS - 1)
                        blocks = windows(nc, pe, m, g, q)
                        if before or q > 1:
                            pe.wait_ge(back_ready, QUADS * g + q - 1)
                        for u in range(QUAD):
                            last = nc.tensor.matmul(bank[q % 2][:, u * P:(u + 1) * P], OT[:, QUAD * q + u, :],
                                                    m.x1[:, bass.ds(blocks[u], 1), :].rearrange("p b f -> p (b f)"), start=True, stop=True)
                        last.then_inc(spread_done, 1)
                    for q in range(QUADS):
                        pe.wait_ge(back_ready, QUADS * g + q + 1)
                        if q > 1:
                            pe.wait_ge(merged_ready[q - 2], g + 1)
                        elif before:
                            pe.wait_ge(merged_ready[q + 2], g)
                        for u in range(QUAD):
                            s = QUAD * q + u
                            last = nc.tensor.matmul(bank[6 + q % 2][:, u * P:(u + 1) * P], same[:, s, :], back[:, s, :], start=True, stop=True)
                        last.then_inc(merged_psum, 1)
                all_groups(pe, work)
                pe.wait_ge(fwd_ready, ALLG)
                for q in range(QUADS):
                    totals(ALLG - 1, (ALLG - 1) % 2, q)


def gnn(nc, x, src, dst, ea, ea16, W_node, W_edge, attn, const, out):
    m = Memory()
    m.x = x
    m.given, m.ordered = Edges(), Edges()
    m.given.dst, m.given.src, m.given.ea, m.given.ea16 = dst, src, ea, ea16
    m.W_node, m.W_edge, m.attn, m.in_const, m.out = W_node, W_edge, attn, const, out
    dram = lambda name, shape: nc.dram_tensor(name, shape, F32, kind="Internal").ap()
    m.ordered.dst = nc.dram_tensor("dst_ordered", (EDGES,), I32, kind="Internal").ap()
    m.ordered.src = nc.dram_tensor("src_ordered", (EDGES,), I32, kind="Internal").ap()
    m.ordered.ea, m.ordered.ea16 = dram("ea_ordered", (EDGES, FEAT)), dram("ea16_ordered", (EDGES, EDIM))
    m.hist = dram("hist_d", (TROWS, 1))
    m.H, m.X1 = dram("h_rows", (NODES, HW)), dram("x1_rows", (NODES, FEAT))
    m.Hs, m.meta = dram("h_of_src", (EDGES, FEAT)), dram("edge_rows", (EDGES, MW))
    m.table = [dram(f"table{t}", (TROWS, FEAT)) for t in range(TABLES)]
    m.tips, m.carries = dram("tips_d", (P, 2)), dram("carries_d", (P, 2))
    with ExitStack() as ctx:
        sb = lambda name, shape, dt=F32: ctx.enter_context(nc.sbuf_tensor(name, shape, dt))
        m.bank = [ctx.enter_context(nc.psum_tensor(f"bank{n}", [P, 512], F32)) for n in range(8)]
        m.begun = ctx.enter_context(nc.semaphore("begun"))
        m.got = [ctx.enter_context(nc.semaphore(f"got{s}")) for s in range(G)]
        m.norm = {n: ctx.enter_context(nc.semaphore(n)) for n in NORM_SEMAPHORES}
        m.const = sb("const", [P, C_WIDTH])
        m.spare = sb("spare", [P, 4])
        m.unsorted = sb("unsorted", [1, 1], I32)
        m.c_in, m.taken, m.placed = (ctx.enter_context(nc.semaphore(n)) for n in ("c_in", "taken", "placed"))
        m.z_out = ctx.enter_context(nc.semaphore("z_out"))
        m.wtab, m.ttab = sb("wtab", [1, STEPS // QUAD], I32), sb("ttab", [1, RES // 2], I32)
        m.baseB = sb("baseB", [P, STEPS])
        m.nodeB = sb("nodeB", [P, STEPS])
        m.wblock = sb("wblock", [P, 2, CHUNKS, HEADS])
        m.dstT, m.srcT = sb("dstT", [P, TILES]), sb("srcT", [P, TILES])
        m.sdst = sb("sdst", [P, BLOCKS, 2 * HEADS])
        m.acc = sb("acc", [P, BLOCKS, HW])
        m.acc_flat = m.acc[:, :, :].rearrange("p b f -> p (b f)")
        phase_order(nc, m)
        with ExitStack() as early:
            m.scratch = early.enter_context(nc.sbuf_tensor("scratch", [P, TILES // 2], F32))
            phase_nodes(nc, m)
        odd = sb("acc_odd", [P, BLOCKS * HW])
        m.acc_odd = odd[:, :].rearrange("p (b f) -> p b f", b=BLOCKS)
        phase_attend(nc, m)
        m.x1 = odd[:, 0:BLOCKS * FEAT].rearrange("p (b f) -> p b f", b=BLOCKS)
        phase_norm(nc, m, last_layer=False)
        m.acc1 = m.acc_flat[:, 0:BLOCKS * FEAT].rearrange("p (b f) -> p b f", b=BLOCKS)
        phase_messages(nc, m)
        phase_norm(nc, m, last_layer=True)


def kernel(x, src, dst, edge_attr_128, edge_attr_16, L0_gnn_W_node, L0_gnn_W_edge, L0_gnn_attn_vec):
    import concourse.bacc as bacc
    from concourse.bass_utils import run_bass_kernel_spmd

    def rows(a, n):
        a = np.asarray(a)
        return np.concatenate([a, np.zeros((n - a.shape[0],) + a.shape[1:], a.dtype)])

    def indices(a):
        a = np.asarray(a)
        return np.concatenate([a, np.full(EDGES - E_REAL, NODES - 1, a.dtype)])

    attn = np.asarray(L0_gnn_attn_vec).reshape(HEADS, 3, HDIM).transpose(0, 2, 1).reshape(P, 3)
    arrays = {
        "x": rows(x, NODES), "src": indices(src), "dst": indices(dst),
        "ea": rows(edge_attr_128, EDGES), "ea16": rows(edge_attr_16, EDGES),
        "W_node": np.ascontiguousarray(L0_gnn_W_node), "W_edge": np.ascontiguousarray(L0_gnn_W_edge),
        "attn": np.ascontiguousarray(attn), "const": shape_constants(),
    }
    nc = bacc.Bacc("TRN2", target_bir_lowering=False, num_devices=1)
    args = {n: nc.dram_tensor("in_" + n, a.shape, mybir.dt.from_np(a.dtype), kind="ExternalInput").ap() for n, a in arrays.items()}
    out = nc.dram_tensor("out_rows", (N_REAL, FEAT), F32, kind="ExternalOutput").ap()
    gnn(nc, out=out, **args)
    r = run_bass_kernel_spmd(nc, [{"in_" + n: a for n, a in arrays.items()}], core_ids=[0])
    return r.results[0]["out_rows"]
```
